# Optimizing a Trainium2 kernel written in Bass

```python
import numpy as np
import jax
import jax.numpy as jnp

def _softmax(x, axis=-1):
    return jax.nn.softmax(x, axis=axis)

def _gelu(x):
    return jax.nn.gelu(x, approximate=True)

def _silu(x):
    return jax.nn.silu(x)

def _sigmoid(x):
    return jax.nn.sigmoid(x)

def _layernorm(x, axis=-1, eps=1e-05):
    m = jnp.mean(x, axis=axis, keepdims=True)
    v = jnp.var(x, axis=axis, keepdims=True)
    return (x - m) / jnp.sqrt(v + eps)

def _scatter_add(tgt, idx, src, axis=0):
    return tgt.at[idx].add(src)

def _segment_sum(src, seg, n):
    return jax.ops.segment_sum(src, seg, n)
kernel_name = 'mk_gnn_resnorm_d4_gnn_r8_a627c1'

def setup_inputs(seed: int=0):
    np.random.seed(seed)
    _w = jnp.asarray

    def _rec_inputs():
        import jax
        import jax.numpy as jnp
        _gk = jax.random.key(seed)
        x = -0.0007083 + 1.001 * jax.random.normal(jax.random.fold_in(_gk, 1), (6250, 48), jnp.float32)
        _s = jax.random.randint(jax.random.fold_in(_gk, 2), (100000,), 0, 6250, jnp.int32)
        _d = jax.random.randint(jax.random.fold_in(_gk, 3), (100000,), 0, 6250, jnp.int32)
        _loop = jnp.arange(6250, dtype=jnp.int32)
        src = jnp.concatenate([_s, _d, _loop])
        dst = jnp.concatenate([_d, _s, _loop])
        _o = jnp.argsort(dst, stable=True)
        src = src[_o]
        dst = dst[_o]
        edge_attr_40 = jax.random.uniform(jax.random.fold_in(_gk, 13), (206250, 40), jnp.float32, 0.0, 1)
        edge_type_8 = jax.random.randint(jax.random.fold_in(_gk, 15), (206250,), 0, 8, jnp.int32)
        edge_weight = jax.random.uniform(jax.random.fold_in(_gk, 16), (206250,), jnp.float32, 0.0, 6.99999)
        edge_weight1 = jax.random.uniform(jax.random.fold_in(_gk, 17), (206250, 1), jnp.float32, 0.0, 1)
        node_type_119 = jax.random.randint(jax.random.fold_in(_gk, 18), (6250,), 0, 119, jnp.int32)
        node_vec = jax.random.uniform(jax.random.fold_in(_gk, 19), (6250,), jnp.float32, 0.0, 1.49999)
        return (x, src, dst, edge_attr_40, edge_type_8, edge_weight, edge_weight1, node_type_119, node_vec)
    x, src, dst, edge_attr_40, edge_type_8, edge_weight, edge_weight1, node_type_119, node_vec = _rec_inputs()

    def _L0_gnn_setup():
        import jax, jax.numpy as jnp
        import numpy as np
        N_NODES = 6250
        N_EDGES = 200000
        IN_FEAT = 48
        OUT_FEAT = 48
        NUM_RELS = 8
        key = jax.random.key(seed)
        ks = jax.random.split(key, 9)
        s1 = float(np.sqrt(2.0) * np.sqrt(6.0 / (IN_FEAT + IN_FEAT)))
        s2 = float(np.sqrt(2.0) * np.sqrt(6.0 / (IN_FEAT + OUT_FEAT)))
        return {'inputs': jax.random.normal(ks[0], (N_NODES, IN_FEAT), dtype=jnp.float32), 'norm': jax.random.uniform(ks[1], (N_EDGES, 1), dtype=jnp.float32), 'weight1': jax.random.uniform(ks[2], (NUM_RELS, IN_FEAT, IN_FEAT), jnp.float32, -s1, s1), 'weight2': jax.random.uniform(ks[3], (NUM_RELS, IN_FEAT, OUT_FEAT), jnp.float32, -s2, s2), 'bias1': jax.random.normal(ks[4], (IN_FEAT,), dtype=jnp.float32) * 0.1, 'bias2': jax.random.normal(ks[5], (OUT_FEAT,), dtype=jnp.float32) * 0.1, 'src': jax.random.randint(ks[6], (N_EDGES,), 0, N_NODES, dtype=jnp.int64) if jax.config.jax_enable_x64 else jax.random.randint(ks[6], (N_EDGES,), 0, N_NODES).astype(jnp.int32), 'dst': jax.random.randint(ks[7], (N_EDGES,), 0, N_NODES).astype(jnp.int32), 'rel_type': jax.random.randint(ks[8], (N_EDGES,), 0, NUM_RELS).astype(jnp.int32)}
    _L0_gnn_all = _L0_gnn_setup()
    _L0_gnn_in = {k: v for k, v in _L0_gnn_all.items() if k in ('weight1', 'weight2', 'bias1', 'bias2')}
    del _L0_gnn_all

    def _L1_gnn_setup():
        import jax, jax.numpy as jnp
        import numpy as np
        N_NODES = 12500
        N_EDGES = 200000
        N_CLASSES = 48
        key = jax.random.key(seed)
        k1, k2, k3, k4 = jax.random.split(key, 4)
        soft_label = jax.random.normal(k1, (N_NODES, N_CLASSES), dtype=jnp.float32)
        e = jax.random.normal(k2, (N_EDGES, 1), dtype=jnp.float32)
        src = jax.random.randint(k3, (N_EDGES,), 0, N_NODES)
        dst = jax.random.randint(k4, (N_EDGES,), 0, N_NODES)
        return {'soft_label': soft_label, 'e': e, 'src': src, 'dst': dst}
    _L1_gnn_all = _L1_gnn_setup()
    _L1_gnn_in = {k: v for k, v in _L1_gnn_all.items() if k in ()}
    del _L1_gnn_all

    def _L2_gnn_setup():
        import jax, jax.numpy as jnp
        import numpy as np
        N_NODES = 12500
        N_EDGES = 200000
        D_FEAT = 48
        N_LAYERS = 2
        key = jax.random.key(seed)
        k1, k2, k3 = jax.random.split(key, 3)
        row = jax.random.randint(k1, (N_EDGES,), 0, N_NODES, dtype=jnp.int32)
        col = jax.random.randint(k2, (N_EDGES,), 0, N_NODES, dtype=jnp.int32)
        x = jax.random.normal(k3, (N_NODES, D_FEAT), dtype=jnp.float32)
        return {'row': row, 'col': col, 'x': x}
    _L2_gnn_all = _L2_gnn_setup()
    _L2_gnn_in = {k: v for k, v in _L2_gnn_all.items() if k in ()}
    del _L2_gnn_all

    def _L3_gnn_setup():
        import jax, jax.numpy as jnp
        import numpy as np
        CUTOFF = 6.0
        LN_EPS = 1e-05
        key = jax.random.key(seed)
        ks = jax.random.split(key, 16)
        N, E, H, R, NEL, G = (6250, 100000, 48, 40, 119, 32)
        inp = {'h': jax.random.normal(ks[0], (N, H), jnp.float32), 'edge_index': jax.random.randint(ks[1], (2, E), 0, N, jnp.int64), 'edge_attr': jax.random.uniform(ks[2], (E, R), jnp.float32), 'distances': jax.random.uniform(ks[3], (E,), jnp.float32) * 7.0, 'atom_z': jax.random.randint(ks[4], (N,), 0, NEL, jnp.int64), 'node_mult': jax.random.uniform(ks[5], (N,), jnp.float32) + 0.5, 'batch': jnp.zeros((N,), jnp.int64), 'W1': jax.random.normal(ks[6], (H, R), jnp.float32) / np.sqrt(R), 'b1': jax.random.normal(ks[7], (H,), jnp.float32) * 0.01, 'W2': jax.random.normal(ks[8], (H, H), jnp.float32) / np.sqrt(H), 'b2': jax.random.normal(ks[9], (H,), jnp.float32) * 0.01, 'emb': jax.random.normal(ks[10], (NEL, G), jnp.float32) * 0.01, 'adaptW': jax.random.normal(ks[11], (G, G), jnp.float32) * 0.01, 'gamma': jnp.ones((H,), jnp.float32), 'beta': jnp.zeros((H,), jnp.float32)}
        return inp
    _L3_gnn_all = _L3_gnn_setup()
    _L3_gnn_in = {k: v for k, v in _L3_gnn_all.items() if k in ('W1', 'b1', 'W2', 'b2', 'emb', 'adaptW', 'gamma', 'beta')}
    del _L3_gnn_all
    return {'x': x, 'src': src, 'dst': dst, 'edge_attr_40': edge_attr_40, 'edge_type_8': edge_type_8, 'edge_weight': edge_weight, 'edge_weight1': edge_weight1, 'node_type_119': node_type_119, 'node_vec': node_vec, 'L0_gnn_weight1': _L0_gnn_in['weight1'], 'L0_gnn_weight2': _L0_gnn_in['weight2'], 'L0_gnn_bias1': _L0_gnn_in['bias1'], 'L0_gnn_bias2': _L0_gnn_in['bias2'], 'L3_gnn_W1': _L3_gnn_in['W1'], 'L3_gnn_b1': _L3_gnn_in['b1'], 'L3_gnn_W2': _L3_gnn_in['W2'], 'L3_gnn_b2': _L3_gnn_in['b2'], 'L3_gnn_emb': _L3_gnn_in['emb'], 'L3_gnn_adaptW': _L3_gnn_in['adaptW'], 'L3_gnn_gamma': _L3_gnn_in['gamma'], 'L3_gnn_beta': _L3_gnn_in['beta']}

def reference(x, src, dst, edge_attr_40, edge_type_8, edge_weight, edge_weight1, node_type_119, node_vec, L0_gnn_weight1, L0_gnn_weight2, L0_gnn_bias1, L0_gnn_bias2, L3_gnn_W1, L3_gnn_b1, L3_gnn_W2, L3_gnn_b2, L3_gnn_emb, L3_gnn_adaptW, L3_gnn_gamma, L3_gnn_beta):
    import jax
    import jax.numpy as jnp

    def _L0_gnn_ref(inputs, norm, weight1, weight2, bias1, bias2, src, dst, rel_type):
        import jax, jax.numpy as jnp
        import numpy as np
        N_NODES = 6250
        N_EDGES = 200000
        IN_FEAT = 48
        OUT_FEAT = 48
        NUM_RELS = 8
        h1 = jax.nn.relu(jnp.einsum('ni,rij->nrj', inputs, weight1) + bias1)
        h2 = jnp.einsum('nrj,rjo->nro', h1, weight2)
        msg = h2[src, rel_type] * norm
        agg = jax.ops.segment_sum(msg, dst, num_segments=inputs.shape[0])
        return jax.nn.relu(agg + bias2)

    def _L1_gnn_ref(soft_label, e, src, dst):
        import jax, jax.numpy as jnp
        import numpy as np
        N_NODES = 12500
        N_EDGES = 200000
        N_CLASSES = 48
        N = soft_label.shape[0]
        logits = e[:, 0]
        seg_max = jax.ops.segment_max(logits, dst, num_segments=N)
        seg_max = jnp.where(jnp.isfinite(seg_max), seg_max, 0.0)
        ex = jnp.exp(logits - seg_max[dst])
        seg_sum = jax.ops.segment_sum(ex, dst, num_segments=N)
        a = ex / seg_sum[dst]
        msg = soft_label[src] * a[:, None]
        rst = jax.ops.segment_sum(msg, dst, num_segments=N)
        return jax.nn.elu(rst)

    def _L2_gnn_ref(row, col, x):
        import jax, jax.numpy as jnp
        import numpy as np
        N_NODES = 12500
        N_EDGES = 200000
        D_FEAT = 48
        N_LAYERS = 2
        n = x.shape[0]
        loop = jnp.arange(n, dtype=row.dtype)
        r = jnp.concatenate([row, loop])
        c = jnp.concatenate([col, loop])
        deg = jax.ops.segment_sum(jnp.ones(r.shape, dtype=x.dtype), r, num_segments=n)
        dinv = jnp.where(deg > 0, jax.lax.rsqrt(deg), 0.0)
        w = dinv[r] * dinv[c]
        for _ in range(N_LAYERS):
            x = jax.ops.segment_sum(w[:, None] * x[c], r, num_segments=n)
        return x

    def _L3_gnn_ref(h, edge_index, edge_attr, distances, atom_z, node_mult, batch, W1, b1, W2, b2, emb, adaptW, gamma, beta):
        import jax, jax.numpy as jnp
        import numpy as np
        CUTOFF = 6.0
        LN_EPS = 1e-05
        src, dst = (edge_index[0], edge_index[1])
        N = h.shape[0]
        gate = jax.nn.silu(edge_attr @ W1.T + b1) @ W2.T + b2
        ei = emb[atom_z[src]]
        ej = emb[atom_z[dst]]
        adapt_logit = jnp.sum(ei * (ej @ adaptW.T), axis=-1, keepdims=True)
        gate = gate + adapt_logit
        cw = jnp.where(distances < CUTOFF, 0.5 * (jnp.cos(jnp.pi * distances / CUTOFF) + 1.0), 0.0)
        mj = node_mult[dst]
        msg = gate * h[dst] * (cw * mj)[:, None]
        agg = jax.ops.segment_sum(msg, src, num_segments=N)
        tot = jax.ops.segment_sum(mj, src, num_segments=N)
        agg = agg / jnp.clip(tot, 1e-08, None)[:, None]
        x = h + agg
        mu = jnp.mean(x, axis=-1, keepdims=True)
        var = jnp.mean(jnp.square(x - mu), axis=-1, keepdims=True)
        return (x - mu) / jnp.sqrt(var + LN_EPS) * gamma + beta
    edge_index = jnp.stack([src, dst])
    batch0 = jnp.zeros((6250,), jnp.int32)
    x = _layernorm(x + _L0_gnn_ref(x, edge_weight1, L0_gnn_weight1, L0_gnn_weight2, L0_gnn_bias1, L0_gnn_bias2, src, dst, edge_type_8), axis=-1)
    x = _layernorm(x + _L1_gnn_ref(x, edge_weight1, src, dst), axis=-1)
    x = _layernorm(x + _L2_gnn_ref(src, dst, x), axis=-1)
    x = _layernorm(x + _L3_gnn_ref(x, edge_index, edge_attr_40, edge_weight, node_type_119, node_vec, batch0, L3_gnn_W1, L3_gnn_b1, L3_gnn_W2, L3_gnn_b2, L3_gnn_emb, L3_gnn_adaptW, L3_gnn_gamma, L3_gnn_beta), axis=-1)
    return x

_drawn_inputs = setup_inputs


def setup_inputs(seed=0):
    import zlib

    import numpy as np

    out = dict(_drawn_inputs(seed))
    spreads = {'L3_gnn_gamma': (1.0, 0.2), 'L3_gnn_beta': (0.0, 0.1)}
    factors = {'edge_attr_40': 6.367,
     'edge_weight': 4.932,
     'node_vec': 8.0,
     'L3_gnn_b1': 64.0,
     'L3_gnn_b2': 64.0,
     'L3_gnn_emb': 64.0,
     'L3_gnn_adaptW': 64.0}
    for name, (base, spread) in spreads.items():
        noise = np.random.default_rng([zlib.crc32(name.encode()), seed]).standard_normal(out[name].shape)
        drawn = base * np.exp(spread * noise) if base else spread * noise
        out[name] = jnp.asarray(drawn.astype(out[name].dtype))
    for name, factor in factors.items():
        out[name] = (out[name] * factor).astype(out[name].dtype)
    return out
```

```python
from contextlib import ExitStack

import numpy as np
import concourse.bass as bass
from concourse import mybir

F32 = mybir.dt.float32
BF16 = mybir.dt.bfloat16
I32 = mybir.dt.int32
U16 = mybir.dt.uint16
ALU = mybir.AluOpType
ACT = mybir.ActivationFunctionType
AX_X = mybir.AxisListType.X
PE_ONLY = (mybir.EngineType.PE,)
DVE_ONLY = (mybir.EngineType.DVE,)
ACT_ONLY = (mybir.EngineType.Activation,)

P = 128
N_NODES, FEAT, N_EDGES = 6250, 48, 206250
RELS, ATTR, EMB = 8, 40, 32
N_BUCKETS = -(-N_NODES // P)
SLOTS = N_BUCKETS + 1
NODES = SLOTS * P
PAD_NODE = N_BUCKETS * P - 1
assert PAD_NODE >= N_NODES
TILES_IN = -(-N_EDGES // P)
GROUP = 8
GROUPS = -(-(TILES_IN + N_BUCKETS) // GROUP)
TILES = GROUPS * GROUP
QUAD = 4
QUADS_IN = TILES_IN // QUAD
QUADS = TILES // QUAD
assert QUADS_IN * QUAD == TILES_IN
BANK = 512
ACC_W = 50
PER_BANK = BANK // ACC_W
ACC_BANKS = SLOTS // PER_BANK
assert ACC_BANKS * PER_BANK == SLOTS
REC = 52
R_LO, R_CW, R_DST = FEAT, FEAT + 1, FEAT + 2
META = 4
M_LO, M_IDX, M_SRC, M_NORM = range(META)
X3_MJ, X3_EMB = FEAT, FEAT + 1
X3_W = FEAT + 1 + EMB
RING = 4
RECS = 4
CHUNK = 2
CHUNKS = SLOTS // CHUNK
PAIRS = RELS // 2
CUTOFF, LN_EPS = 6.0, 1e-5
NEG = -float(2.0 ** 126)
TCH = TILES // 4


def build(nc, A):
    with ExitStack() as ctx:
        def sb(name, shape, dt=F32):
            return ctx.enter_context(nc.sbuf_tensor(name, shape, dt))

        def sem(name):
            return ctx.enter_context(nc.semaphore(name))

        def dram(name, shape, dt=F32):
            return nc.dram_tensor(name, shape, dt, kind="Internal").ap()

        h2_table = dram("h2_table", (NODES * RELS, FEAT))
        x1_table = dram("x1_table", (NODES, FEAT))
        y_table = [dram("y0_table", (NODES, FEAT)), dram("y1_table", (NODES, FEAT))]
        x3_table = dram("x3_table", (NODES, X3_W))
        emb_table = dram("emb_table", (P, 2 * EMB))
        by_dst = dram("by_dst", (TILES * P, META))
        by_src = dram("by_src", (TILES * P, REC))

        ident = sb("ident", [P, P])
        before = sb("before", [P, P])
        upto = sb("upto", [P, P])
        iota = sb("iota", [P, P])
        iota_b = sb("iota_b", [P, P], BF16)
        ones = sb("ones", [P, P])
        zeros_b = sb("zeros_b", [P, BANK], BF16)
        default = sb("default", [P, GROUP * REC])
        default_meta = sb("default_meta", [P, GROUP * META])
        w1T = sb("w1T", [ATTR, FEAT])
        w2T = sb("w2T", [FEAT, FEAT])
        b1c = sb("b1c", [FEAT, 1])
        b2r = sb("b2r", [P, FEAT])
        embT = sb("embT", [EMB, P])
        adaptT = sb("adaptT", [EMB, EMB])
        emb_rows = sb("emb_rows", [P, 2 * EMB])
        rw1 = sb("rw1", [FEAT, PAIRS, 2 * FEAT])
        rw2 = sb("rw2", [2 * FEAT, PAIRS, 2 * FEAT])
        rb1 = sb("rb1", [2 * FEAT, 1])
        rb2 = sb("rb2", [P, FEAT])
        gamma = sb("gamma", [P, FEAT])
        beta = sb("beta", [P, FEAT])
        zeros_c = sb("zeros_c", [P, 1])
        halfpi = sb("halfpi", [P, 1])

        big = sb("big", [P, 4 * TILES_IN])
        src_i = big[:, 0:TILES_IN].bitcast(I32)
        dst_i = sb("dst_i", [P, TILES_IN], I32)
        until_sorted = sb("until_sorted", [P, 2 * TILES_IN])
        cw = until_sorted[:, 0:TILES_IN]
        lo_src = until_sorted[:, TILES_IN:2 * TILES_IN]
        embs = until_sorted[:, 0:SLOTS * 2 * EMB].rearrange("p (b w) -> p b w", w=2 * EMB)
        row_dst = sb("row_dst", [P, TILES_IN], I32)
        row_src = sb("row_src", [P, TILES_IN], I32)
        bucket = sb("bucket", [P, TILES_IN], BF16)
        hit = big[:, TILES_IN:2 * TILES_IN].bitcast(U16).rearrange("p (s t) -> p s t", s=2)
        count = big[:, 2 * TILES_IN:3 * TILES_IN]
        scratch = big[:, 3 * TILES_IN:4 * TILES_IN]
        assert 4 * TILES_IN >= SLOTS * P
        scratch_i = scratch.bitcast(I32)
        count_i = count.bitcast(I32)
        meta_a = sb("meta_a", [P, TILES, META])
        meta_b = sb("meta_b", [P, TILES, META])
        small = sb("small", [P, 8, SLOTS])
        small_i = sb("small_i", [P, SLOTS], I32)
        acc_at = sb("acc_at", [1, 2, TILES], I32)
        max_at = sb("max_at", [1, 1, TILES], I32)

        X = sb("X", [P, SLOTS, FEAT])
        V = sb("V", [P, SLOTS, FEAT])
        Q = sb("Q", [P, SLOTS, FEAT])
        node_z = sb("node_z", [P, SLOTS], I32)
        node_mj = sb("node_mj", [P, SLOTS])
        tile_no = X[0:N_BUCKETS, :, :].rearrange("p b w -> p (b w)")[:, 0:TILES]
        dinv = sb("dinv", [P, SLOTS])
        seg_max = sb("seg_max", [P, SLOTS])

        ring = sb("ring", [P, RING, GROUP, X3_W])
        ring_f = ring[:, :, :, :].rearrange("p r j w -> p (r j w)")
        xT = ring_f[0:FEAT, 0:2 * CHUNK * P].rearrange("p (s n) -> p s n", s=2)
        h1 = ring_f[0:2 * FEAT, 512:512 + PAIRS * CHUNK * P].rearrange("p (q n) -> p q n", q=PAIRS)
        h2 = ring_f[:, 1536:1536 + 2 * RELS * FEAT].rearrange("p (s n) -> p s n", s=2)
        W = sb("W", [P, 2, GROUP, P])
        ex = sb("ex", [P, 2, GROUP, P])
        hot = row_dst[:, 0:GROUP * P].bitcast(BF16).rearrange("p (s j n) -> p s j n", s=2, j=GROUP)
        free = meta_a[:, :, :].rearrange("p t w -> p (t w)")
        attr = free[0:ATTR, 0:4 * QUAD * P].rearrange("p (s n) -> p s n", s=2)
        sT = free[0:FEAT, 2048:2048 + 2 * QUAD * P].rearrange("p (s n) -> p s n", s=2)
        rec = free[:, 3072:3072 + RECS * QUAD * REC].rearrange("p (s j w) -> p s j w", s=RECS, j=QUAD)
        vf = V[:, :, :].rearrange("p b w -> p (b w)")
        qf = Q[:, :, :].rearrange("p b w -> p (b w)")
        started = vf[0:N_BUCKETS, 0:TILES]
        bt = qf[0:1, 0:TILES]
        tens = W[:, :, :, :].rearrange("p s j n -> p (s j n)")[0:1, 0:TILES]
        bt_i = ex[:, :, :, :].rearrange("p s j n -> p (s j n)")[0:1, 0:TILES].bitcast(I32)
        red = sb("red", [P, 2, QUAD])
        hi_hot = sb("hi_hot", [P, 2, QUAD, SLOTS], BF16)

        ps = ctx.enter_context(nc.psum_tensor("ps", [P, 8 * BANK], F32))

        def bank(i, n=BANK, parts=P, at=0):
            return ps[0:parts, i * BANK + at:i * BANK + at + n]

        acc = ps[:, 0:ACC_BANKS * BANK].rearrange("p (k c) -> p k c", c=BANK)[:, :, 0:PER_BANK * ACC_W] \
            .rearrange("p k (s w) -> p k s w", w=ACC_W)

        s_const = sem("s_const")
        s_edges = sem("s_edges")
        s_node = sem("s_node")
        s_set = sem("s_set")
        s_xT = [sem(f"s_xT{i}") for i in range(2)]
        s_h1p = sem("s_h1p")
        s_h1 = sem("s_h1")
        s_h2p = sem("s_h2p")
        s_h2 = sem("s_h2")
        s_h2w = [sem(f"s_h2w{i}") for i in range(2)]
        s_embp = sem("s_embp")
        s_embs = sem("s_embs")
        s_embw = sem("s_embw")
        s_embg = sem("s_embg")
        s_init = sem("s_init")
        s_dve = sem("s_dve")
        s_cosarg = sem("s_cosarg")
        s_cos = sem("s_cos")
        s_tot = sem("s_tot")
        s_pre = sem("s_pre")
        s_nt = sem("s_nt")
        s_end = sem("s_end")
        s_cmp = sem("s_cmp")
        s_bt = sem("s_bt")
        s_plan = sem("s_plan")
        s_s1 = sem("s_s1")
        s_m1 = sem("s_m1")
        s_m2 = sem("s_m2")
        s_gat = [sem(f"s_gat{i}") for i in range(RING)]
        s_w = sem("s_w")
        s_used = sem("s_used")
        s_zero = sem("s_zero")
        s_epi = sem("s_epi")
        s_tab = sem("s_tab")
        s_tabw = sem("s_tabw")
        s_attr = [sem(f"s_attr{i}") for i in range(2)]
        s_sp = sem("s_sp")
        s_s = sem("s_s")
        s_gp = sem("s_gp")
        s_small = sem("s_small")
        s_rec = sem("s_rec")
        s_sc = [sem(f"s_sc{i}") for i in range(RECS)]
        s_degh = sem("s_degh")
        s_deg = sem("s_deg")
        s_mask = sem("s_mask")
        s_mval = sem("s_mval")
        s_mT = sem("s_mT")
        s_red = sem("s_red")
        s_maxd = sem("s_maxd")
        s_diag = sem("s_diag")
        s_bc = sem("s_bc")
        s_bcc = sem("s_bcc")
        s_ex = sem("s_ex")
        s_sq = sem("s_sq")
        s_sr = sem("s_sr")
        s_recl = [sem(f"s_recl{i}") for i in range(2)]
        s_oh = sem("s_oh")
        s_ohp = sem("s_ohp")
        s_ohT = sem("s_ohT")
        s_ei = sem("s_ei")
        s_eir = sem("s_eir")
        s_out = sem("s_out")

        block = ctx.enter_context(nc.Block())

        n_const = [0]
        asks = []

        by_dst_v = by_dst.rearrange("(g p j) w -> p g (j w)", p=P, j=GROUP)
        by_src_v = by_src.rearrange("(g p j) w -> p g j w", p=P, j=GROUP)

        def table_v(t):
            return t.rearrange("(b p) w -> p b w", p=P)

        oh_T = ex
        rec_in = big[:, 0:2 * GROUP * REC].rearrange("p (s j w) -> p s j w", s=2, j=GROUP)
        msg = big[:, 1024:1024 + 2 * GROUP * ACC_W].rearrange("p (s j w) -> p s j w", s=2, j=GROUP)
        prod = big[:, 2048:2048 + GROUP * EMB].rearrange("p (j w) -> p j w", j=GROUP)
        adapt = big[:, 2304:2304 + GROUP]
        wgt = big[:, 2320:2320 + GROUP]
        emb_of = big[:, 2560:2560 + ACC_BANKS * BANK]
        emb_of_v = emb_of.rearrange("p (k c) -> p k c", c=BANK)[:, :, 0:PER_BANK * ACC_W] \
            .rearrange("p k (s w) -> p k s w", w=ACC_W)
        seg_run = big[:, 0:SLOTS * P].rearrange("p (b n) -> p b n", n=P)[:, :, 0]

        REQ = [("sqrt", small[:, 3, :]), ("sqrt", small[:, 7, :]), ("exp", Q), ("sqrt", small[:, 3, :]),
               ("sqrt", small[:, 3, :]), ("sqrt", small[:, 3, :]), ("sqrt", small[:, 3, :])]

        @block.sync
        def _(sp):
            def const(dst, src):
                sp.dma_start(dst, src).then_inc(s_const, 16)
                n_const[0] += 16

            sp.dma_start(dst_i[:, :], A["dst"]).then_inc(s_edges, 16)
            sp.dma_start(count_i, A["etype"]).then_inc(s_edges, 16)
            sp.dma_start(src_i, A["src"]).then_inc(s_edges, 16)
            sp.dma_start(scratch, A["norm"]).then_inc(s_edges, 16)
            sp.dma_start(cw, A["dist"]).then_inc(s_edges, 16)
            const(ident[:, :], A["const"][0])
            const(before[:, :], A["const"][1])
            const(upto[:, :], A["const"][2])
            const(iota[:, :], A["const"][3])
            const(tile_no, A["tile_no"])
            const(default[:, :], A["default"])
            const(default_meta[:, :], A["default_meta"])
            const(w1T[:, :], A["W1T"])
            const(w2T[:, :], A["W2T"])
            const(b1c[:, :], A["b1"].rearrange("(a b) -> a b", b=1))
            const(b2r[:, :], A["b2"].rearrange("(a b) -> a b", a=1).to_broadcast([P, FEAT]))
            const(embT[:, :], A["embT"])
            const(adaptT[:, :], A["adaptT"])
            for q in range(PAIRS):
                for r in range(2):
                    const(rw1[:, q, r * FEAT:(r + 1) * FEAT], A["weight1"][2 * q + r])
            for r in range(2):
                const(rb1[r * FEAT:(r + 1) * FEAT, :], A["bias1"].rearrange("(a b) -> a b", b=1))
            const(rb2[:, :], A["bias2"].rearrange("(a b) -> a b", a=1).to_broadcast([P, FEAT]))
            const(gamma[:, :], A["gamma"].rearrange("(a b) -> a b", a=1).to_broadcast([P, FEAT]))
            const(beta[:, :], A["beta"].rearrange("(a b) -> a b", a=1).to_broadcast([P, FEAT]))
            sp.wait_ge(s_set, 1)
            for q in range(PAIRS):
                for r in range(2):
                    const(rw2[r * FEAT:(r + 1) * FEAT, q, r * FEAT:(r + 1) * FEAT], A["weight2"][2 * q + r])
            sp.dma_start(node_z[:, :], A["node_z"]).then_inc(s_node, 16)
            sp.dma_start(node_mj[:, :], A["node_mj"]).then_inc(s_node, 16)
            sp.wait_ge(s_const, n_const[0])
            sp.dma_start(by_dst_v, default_meta[:, None, :].to_broadcast([P, GROUPS, GROUP * META])) \
                .then_inc(s_init, 16)
            for c in range(CHUNKS):
                if c >= 2:
                    sp.wait_ge(s_h1p, c - 1)
                sp.dma_start(xT[:, c % 2, :], A["xT"][:, c * CHUNK * P:(c + 1) * CHUNK * P]) \
                    .then_inc(s_xT[c % 2], 16)
                if c >= 1:
                    for n in range((c - 1) * CHUNK, c * CHUNK):
                        sp.wait_ge(s_h2, n + 1)
                        sp.dma_start(h2_table[n * P * RELS:(n + 1) * P * RELS, :].rearrange("(p r) w -> p (r w)", r=RELS),
                                     h2[:, n % 2, :]).then_inc(s_h2w[n % 2], 16)
            for n in range((CHUNKS - 1) * CHUNK, SLOTS):
                sp.wait_ge(s_h2, n + 1)
                sp.dma_start(h2_table[n * P * RELS:(n + 1) * P * RELS, :].rearrange("(p r) w -> p (r w)", r=RELS),
                             h2[:, n % 2, :]).then_inc(s_h2w[n % 2], 16)
            sp.wait_ge(s_embs, 1)
            sp.dma_start(emb_table, emb_rows[:, :]).then_inc(s_embw, 16)
            dv = by_src.rearrange("(g p j) w -> p g (j w)", p=P, j=GROUP)
            sp.dma_start(dv, default[:, None, :].to_broadcast([P, GROUPS, GROUP * REC])).then_inc(s_init, 16)
            sp.wait_ge(s_plan, 2)
            sp.dma_start(X[:, :, :], A["x"]).then_inc(s_node, 16)
            sp.wait_ge(s_s1, 16 * TILES_IN)
            sp.dma_start(meta_b[:, :, :].rearrange("p (g j) w -> p g (j w)", j=GROUP), by_dst_v).then_inc(s_m1, 16)
            for c in range(-(-QUADS_IN // 2)):
                n = min(2, QUADS_IN - 2 * c)
                if c >= 2:
                    sp.wait_ge(s_sp, 2 * (c - 1))
                sp.dma_start(attr[:, c % 2, 0:n * QUAD * P], A["attrT"][:, 2 * c * QUAD * P:(2 * c + n) * QUAD * P]) \
                    .then_inc(s_attr[c % 2], 16)
            sp.wait_ge(s_tab, 1)
            sp.dma_start(table_v(x1_table), X[:, :, :]).then_inc(s_tabw, 16)
            for i in range(RECS):
                sp.wait_ge(s_sc[i], 16 * QUAD * len(range(i, QUADS_IN, RECS)))
            for j in range(GROUP):
                sp.dma_start(meta_a[:, :, :].rearrange("p (g j) w -> p g j w", j=GROUP)[:, :, j, :],
                             by_src_v[:, :, j, FEAT:REC]).then_inc(s_m2, 16)
            for i in range(2):
                sp.wait_ge(s_tab, 2 + i)
                sp.dma_start(table_v(y_table[i]), V[:, :, :]).then_inc(s_tabw, 16)
            sp.wait_ge(s_tab, 4)
            sp.dma_start(table_v(x3_table)[:, :, 0:FEAT], X[:, :, :]).then_inc(s_tabw, 16)
            sp.dma_start(table_v(x3_table)[:, :, FEAT:X3_W], embs[:, :, EMB - 1:2 * EMB]).then_inc(s_tabw, 16)
            for g in range(GROUPS):
                if g >= 2:
                    sp.wait_ge(s_eir, g - 1)
                sp.dma_start(rec_in[:, g % 2, :, :], by_src_v[:, g, :, :]).then_inc(s_recl[g % 2], 16)
            sp.wait_ge(s_tab, 5)
            full = N_NODES // P
            sp.dma_start(A["out"][0:full * P, :].rearrange("(b p) w -> p b w", p=P), X[:, 0:full, :]).then_inc(s_out, 16)
            sp.dma_start(A["out"][full * P:N_NODES, :], X[0:N_NODES - full * P, full, :]).then_inc(s_out, 16)
            sp.wait_ge(s_out, 32)

        @block.gpsimd
        def _(pool):
            pool.wait_ge(s_init, 16)
            pool.wait_ge(s_plan, 1)
            for t in range(TILES_IN):
                pool.indirect_dma_start(by_dst, bass.IndirectOffsetOnAxis(ap=row_dst[:, t:t + 1], axis=0),
                                        meta_a[:, t, :], None).then_inc(s_s1, 16)

            def gather(k, table, width, index):
                for g in range(GROUPS):
                    gg = k * GROUPS + g
                    if gg >= RING:
                        pool.wait_ge(s_used, gg - RING + 1)
                    for j in range(GROUP):
                        pool.indirect_dma_start(ring[:, gg % RING, j, 0:width], None, table,
                                                bass.IndirectOffsetOnAxis(ap=index(g * GROUP + j), axis=0)) \
                            .then_inc(s_gat[gg % RING], 16)

            meta_b_i = meta_b[:, :, :].bitcast(I32)
            meta_a_i = meta_a[:, :, :].bitcast(I32)
            pool.wait_ge(s_m1, 16)
            for i in range(2):
                pool.wait_ge(s_h2w[i], 16 * SLOTS // 2)
            gather(0, h2_table, FEAT, lambda t: meta_b_i[:, t, M_IDX:M_IDX + 1])
            pool.wait_ge(s_plan, 2)
            pool.wait_ge(s_init, 32)
            for q in range(QUADS_IN):
                pool.wait_ge(s_rec, q + 1)
                for j in range(QUAD):
                    t = q * QUAD + j
                    pool.indirect_dma_start(by_src, bass.IndirectOffsetOnAxis(ap=row_src[:, t:t + 1], axis=0),
                                            rec[:, q % RECS, j, :], None).then_inc(s_sc[q % RECS], 16)
            pool.wait_ge(s_embw, 16)
            pool.wait_ge(s_node, 48)
            pool.wait_ge(s_small, QUADS_IN)
            pool.wait_ge(s_degh, QUADS_IN)
            for b in range(SLOTS):
                pool.indirect_dma_start(embs[:, b, :], None, emb_table,
                                        bass.IndirectOffsetOnAxis(ap=node_z[:, b:b + 1], axis=0)).then_inc(s_embg, 16)
            pool.wait_ge(s_tabw, 16)
            gather(1, x1_table, FEAT, lambda t: meta_b_i[:, t, M_SRC:M_SRC + 1])
            pool.wait_ge(s_m2, 16 * GROUP)
            by_s = lambda t: meta_a_i[:, t, R_DST - FEAT:R_DST - FEAT + 1]
            pool.wait_ge(s_tabw, 32)
            gather(2, y_table[0], FEAT, by_s)
            pool.wait_ge(s_tabw, 48)
            gather(3, y_table[1], FEAT, by_s)
            pool.wait_ge(s_tabw, 80)
            gather(4, x3_table, X3_W, by_s)

        def offsets(engines, table, row, g):
            src = table[0:1, row, g * GROUP:(g + 1) * GROUP] if row is not None else table[0:1, g * GROUP:(g + 1) * GROUP]
            return nc.values_load_multi_w_load_instructions(
                src, engines=engines, min_val=0, max_val=(N_BUCKETS - 1) * P if table is max_at else (ACC_BANKS - 1) * BANK + (PER_BANK - 1) * ACC_W,
                skip_runtime_bounds_check_because="made from bucket numbers that are clamped")[1]

        @block.tensor
        def _(pe):
            pe.wait_ge(s_const, n_const[0])
            pe.wait_ge(s_set, 4)
            pe.matmul(bank(7, EMB), embT[:, :], adaptT[:, :], start=True, stop=True).then_inc(s_embp, 1)
            pe.transpose(bank(7, EMB, at=64), embT[:, :], ident[0:EMB, 0:EMB]).then_inc(s_embp, 1)
            for c in range(CHUNKS):
                pe.wait_ge(s_xT[c % 2], 16 * (c // 2 + 1))
                if c >= 1:
                    pe.wait_ge(s_h1, 2 * c)
                for q in range(PAIRS):
                    mm = pe.matmul(bank(5 + q // 2, CHUNK * P, 2 * FEAT, (q % 2) * CHUNK * P), rw1[:, q, :],
                                   xT[:, c % 2, :], start=True, stop=True)
                mm.then_inc(s_h1p, 1)
                pe.wait_ge(s_h1, 2 * (c + 1))
                for i in range(CHUNK):
                    n = c * CHUNK + i
                    if n == 0:
                        pe.wait_ge(s_embs, 1)
                    if n >= 2:
                        pe.wait_ge(s_h2, n - 1)
                    for q in range(PAIRS):
                        mm = pe.matmul(bank(7 if n % 2 else 4, 2 * FEAT, P, q * 2 * FEAT), h1[:, q, i * P:(i + 1) * P],
                                       rw2[:, q, :], start=True, stop=True)
                    mm.then_inc(s_h2p, 1)

            for o in range(2):
                pe.wait_ge(s_tot, o + 1)
                tot = small[:, 0, 0:N_BUCKETS]
                pe.matmul(bank(5, N_BUCKETS), before[:, :], tot, start=True, stop=True)
                pe.matmul(bank(5, N_BUCKETS, at=64), ones[:, :], tot, start=True, stop=True)
                pe.matmul(bank(5, 1, N_BUCKETS, at=128), tot, ones[:, 0:1], start=True, stop=True).then_inc(s_pre, 1)
                pe.wait_ge(s_nt, o + 1)
                pe.matmul(bank(5, 1, N_BUCKETS, at=130), upto[0:N_BUCKETS, 0:N_BUCKETS], small[0:N_BUCKETS, 4, 0:1],
                          start=True, stop=True).then_inc(s_end, 1)
                for i in range(4):
                    pe.wait_ge(s_cmp, 4 * o + i + 1)
                    pe.matmul(bank(i, TCH, 1), ones[0:N_BUCKETS, 0:1], started[:, i * TCH:(i + 1) * TCH],
                              start=True, stop=True).then_inc(s_bt, 1)

            def zero_acc(k):
                pe.wait_ge(s_epi, k)
                for i in range(ACC_BANKS):
                    pe.matmul(bank(i, BANK), zeros_b[:, 0:P], zeros_b[:, :], start=True, stop=False,
                              skip_group_check=True)

            def sum_group(k, g, order, width, rhs, regs):
                gg = k * GROUPS + g
                pe.wait_ge(s_gat[gg % RING], 16 * GROUP * (gg // RING + 1))
                pe.wait_ge(s_w, gg + 1)
                for j in range(GROUP):
                    mm = pe.matmul(ps[:, bass.ds(regs[j], width)], W[:, gg % 2, j, :], rhs(gg, j),
                                   start=False, stop=False, skip_group_check=True)
                mm.then_inc(s_used, 1)

            def from_ring(width):
                return lambda gg, j: ring[:, gg % RING, j, 0:width]

            zero_acc(1)
            for g in range(GROUPS):
                regs = offsets(PE_ONLY, acc_at, 0, g)
                sum_group(0, g, 0, FEAT, from_ring(FEAT), regs)

            pe.wait_ge(s_epi, 2)
            for q in range(QUADS + 1):
                if q < QUADS_IN:
                    c = q // 2
                    if q % 2 == 0:
                        pe.wait_ge(s_attr[c % 2], 16 * (c // 2 + 1))
                    if q >= 2:
                        pe.wait_ge(s_s, q - 1)
                    pe.matmul(bank(5 + q % 2, QUAD * P, FEAT), w1T[:, :],
                              attr[:, c % 2, (q % 2) * QUAD * P:(q % 2 + 1) * QUAD * P],
                              start=True, stop=True).then_inc(s_sp, 1)
                if q < QUADS:
                    pe.wait_ge(s_mval, q + 1)
                    if q >= 2:
                        pe.wait_ge(s_red, q - 1)
                    for j in range(QUAD):
                        mm = pe.transpose(bank(q % 2, P, at=j * P), ex[:, q % 2, j, :], ident[:, :])
                    mm.then_inc(s_mT, 1)
                if 1 <= q <= QUADS_IN:
                    r = q - 1
                    pe.wait_ge(s_s, r + 1)
                    if r >= 2:
                        pe.wait_ge(s_rec, r - 1)
                    for j in range(QUAD):
                        mm = pe.matmul(bank(7 if r % 2 else 4, FEAT, at=j * FEAT), sT[:, r % 2, j * P:(j + 1) * P],
                                       w2T[:, :], start=True, stop=True)
                    mm.then_inc(s_gp, 1)
                    pe.wait_ge(s_degh, r + 1)
                    for j in range(QUAD):
                        mm = pe.matmul(bank(3, SLOTS), hot[:, r % 2, j, :], hi_hot[:, r % 2, j, :],
                                       start=(r == 0 and j == 0), stop=(r == QUADS_IN - 1 and j == QUAD - 1))
                    mm.then_inc(s_deg, 1)
            for b in range(SLOTS):
                pe.wait_ge(s_diag, b + 1)
                if b >= 2:
                    pe.wait_ge(s_bcc, b - 1)
                pe.matmul(bank(b % 2, P), ones[:, :], W[:, b % 2, 0, :], start=True, stop=True).then_inc(s_bc, 1)

            pe.wait_ge(s_bcc, SLOTS)
            zero_acc(3)
            for g in range(GROUPS):
                regs = offsets(PE_ONLY, acc_at, 0, g)
                sum_group(1, g, 0, FEAT + 1, from_ring(FEAT + 1), regs)
            for k in (2, 3):
                zero_acc(k + 2)
                for g in range(GROUPS):
                    regs = offsets(PE_ONLY, acc_at, 1, g)
                    sum_group(k, g, 1, FEAT, from_ring(FEAT), regs)
            zero_acc(6)
            for g in range(GROUPS + 1):
                if g < GROUPS:
                    gg = 4 * GROUPS + g
                    pe.wait_ge(s_oh, g + 1)
                    if g >= 1:
                        pe.wait_ge(s_ohT, 2 * g)
                    for j in range(GROUP):
                        mm = pe.transpose(bank(5 + j // 4, P, at=(j % 4) * P), W[:, gg % 2, j, :], ident[:, :])
                        if j % 4 == 3:
                            mm.then_inc(s_ohp, 1)
                    eregs = offsets(PE_ONLY, acc_at, 1, g)
                    pe.wait_ge(s_ohT, 2 * g + 2)
                    if g >= 1:
                        pe.wait_ge(s_eir, g)
                    for j in range(GROUP):
                        mm = pe.matmul(bank(7, EMB, at=j * EMB), oh_T[:, g % 2, j, :], emb_of[:, bass.ds(eregs[j], EMB)],
                                       start=True, stop=True)
                    mm.then_inc(s_ei, 1)
                if g >= 1:
                    regs = offsets(PE_ONLY, acc_at, 1, g - 1)
                    sum_group(4, g - 1, 1, FEAT + 1, lambda gg, j: msg[:, gg % 2, j, 0:FEAT + 1], regs)

        @block.scalar
        def _(act):
            act.wait_ge(s_const, n_const[0])
            act.wait_ge(s_set, 4)
            for c in range(CHUNKS):
                act.wait_ge(s_h1p, c + 1)
                if c >= 1:
                    act.wait_ge(s_h2p, CHUNK * c)
                for i in range(2):
                    act.activation(h1[:, 2 * i:2 * i + 2, :],
                                   bank(5 + i, 2 * CHUNK * P, 2 * FEAT).rearrange("p (q n) -> p q n", q=2),
                                   ACT.Relu, bias=rb1[:, 0:1]).then_inc(s_h1, 1)
            act.wait_ge(s_cosarg, 1)
            act.activation(cw, cw, ACT.Sin, bias=halfpi[:, 0:1], scale=-float(np.pi) / CUTOFF).then_inc(s_cos, 1)

            served = [0]

            def serve():
                name, ap = REQ[served[0]]
                ap = ap[:, :, :] if name == "exp" else ap
                served[0] += 1
                act.wait_ge(s_sq, served[0])
                act.activation(ap, ap, ACT.Exp if name == "exp" else ACT.Sqrt, bias=zeros_c[:, 0:1]).then_inc(s_sr, 1)

            serve()
            for q in range(QUADS):
                if q < QUADS_IN:
                    act.wait_ge(s_sp, q + 1)
                    if q >= 2:
                        act.wait_ge(s_gp, q - 1)
                    act.activation(sT[:, q % 2, :], bank(5 + q % 2, QUAD * P, FEAT), ACT.Silu,
                                   bias=b1c[:, 0:1]).then_inc(s_s, 1)
                    if q >= RECS:
                        act.wait_ge(s_sc[q % RECS], 16 * QUAD * (q // RECS))
                    ts = slice(q * QUAD, (q + 1) * QUAD)
                    act.activation(rec[:, q % RECS, :, R_LO], lo_src[:, ts], ACT.Copy)
                    act.activation(rec[:, q % RECS, :, R_CW], cw[:, ts], ACT.Copy)
                    act.activation(rec[:, q % RECS, :, R_DST + 1], lo_src[:, ts], ACT.Copy)
                    act.activation(rec[:, :, :, :].bitcast(I32)[:, q % RECS, :, R_DST], dst_i[:, ts],
                                   ACT.Copy).then_inc(s_small, 1)
                act.wait_ge(s_mask, q + 1)
                if q >= 2:
                    act.wait_ge(s_mT, q - 1)
                for j in range(QUAD):
                    t = q * QUAD + j
                    a = act.activation(ex[:, q % 2, j, :], hot[:, q % 2, 4 + j, :], ACT.Identity,
                                       bias=meta_b[:, t, M_NORM:M_NORM + 1])
                a.then_inc(s_mval, 1)
            act.wait_ge(s_maxd, 1)
            for b in range(SLOTS):
                if b >= 2:
                    act.wait_ge(s_bc, b - 1)
                act.activation(W[:, b % 2, 0, :], ident[:, :], ACT.Copy, scale=seg_max[:, b:b + 1]).then_inc(s_diag, 1)
            serve()
            act.wait_ge(s_bcc, SLOTS)
            for g in range(GROUPS):
                if g >= 2:
                    act.wait_ge(s_w, GROUPS + g - 1)
                regs = offsets(ACT_ONLY, max_at, 0, g)
                for j in range(GROUP):
                    t = g * GROUP + j
                    a = act.activation(ex[:, g % 2, j, :], big[:, bass.ds(regs[j], P)], ACT.Exp, scale=-1.0,
                                       bias=meta_b[:, t, M_NORM:M_NORM + 1])
                a.then_inc(s_ex, 1)
            serve()
            serve()
            serve()
            for g in range(GROUPS):
                for i in range(2):
                    act.wait_ge(s_ohp, 2 * g + i + 1)
                    act.activation(oh_T[:, g % 2, 4 * i:4 * i + 4, :],
                                   bank(5 + i).rearrange("p (j n) -> p j n", j=4), ACT.Copy).then_inc(s_ohT, 1)
            serve()
            serve()

        @block.vector
        def _(dve):
            chain = [0]

            def link(ins):
                chain[0] += 1
                ins.then_inc(s_dve, 1)
                dve.wait_ge(s_dve, chain[0])

            dve.memset(rw2[:, :, :], 0.0).then_inc(s_set, 1)
            dve.memset(ones[:, :], 1.0).then_inc(s_set, 1)
            dve.memset(zeros_b[:, :], 0.0)
            dve.memset(halfpi[:, :], float(np.pi) / 2)
            dve.memset(zeros_c[:, :], 0.0).then_inc(s_set, 1)
            dve.wait_ge(s_const, n_const[0])
            dve.tensor_copy(iota_b[:, :], iota[:, :]).then_inc(s_set, 1)
            dve.wait_ge(s_set, 4)
            dve.wait_ge(s_embp, 2)
            dve.tensor_copy(emb_rows[:, 0:EMB], bank(7, EMB, at=64))
            dve.tensor_copy(emb_rows[:, EMB:2 * EMB], bank(7, EMB)).then_inc(s_embs, 1)
            dve.wait_ge(s_edges, 80)

            meta_a_i = meta_a[:, 0:TILES_IN, :].bitcast(I32)
            link(dve.scalar_tensor_tensor(meta_a_i[:, :, M_IDX], src_i, float(RELS), count_i, ALU.mult, ALU.add))
            dve.tensor_copy(meta_a_i[:, :, M_SRC], src_i)
            link(dve.tensor_copy(meta_a[:, 0:TILES_IN, M_NORM], scratch))

            for n in range(SLOTS):
                dve.wait_ge(s_h2p, n + 1)
                if n >= 2:
                    dve.wait_ge(s_h2w[n % 2], 16 * (n // 2))
                dve.tensor_copy(h2[:, n % 2, :], bank(7 if n % 2 else 4, RELS * FEAT)).then_inc(s_h2, 1)

            link(dve.tensor_scalar(hit[:, 0, :], cw, CUTOFF, None, ALU.is_lt))
            link(dve.tensor_scalar(lo_src, cw, CUTOFF, 1.0 / (2 * CUTOFF), ALU.min, ALU.mult))
            link(dve.tensor_copy(scratch_i, lo_src))
            link(dve.tensor_copy(count, scratch_i))
            link(dve.tensor_scalar(cw, cw, CUTOFF, None, ALU.min))
            link(dve.scalar_tensor_tensor(cw, count, -2 * CUTOFF, cw, ALU.mult, ALU.add))
            link(dve.tensor_scalar(count, cw, -1.0, None, ALU.mult))
            link(dve.tensor_tensor(cw, cw, count, ALU.max))
            link(dve.tensor_scalar(count, cw, -1.0, 2 * CUTOFF, ALU.mult, ALU.add))
            dve.tensor_tensor(cw, cw, count, ALU.min).then_inc(s_cosarg, 1)
            dve.wait_ge(s_cos, 1)
            link(dve.tensor_scalar(cw, cw, 0.5, 0.5, ALU.mult, ALU.add))
            link(dve.tensor_tensor(cw, cw, hit[:, 0, :], ALU.mult))

            def plan(o, key, lo_out, rows):
                link(dve.tensor_scalar(scratch_i, key, P.bit_length() - 1, None, ALU.logical_shift_right))
                link(dve.tensor_copy(bucket[:, :], scratch_i))
                link(dve.tensor_scalar(scratch_i, key, P - 1, None, ALU.bitwise_and))
                link(dve.tensor_copy(lo_out, scratch_i))
                tot = small[:, 0, 0:N_BUCKETS]
                for b in range(N_BUCKETS):
                    if b >= 2:
                        dve.wait_ge(s_dve, chain[0] - 1)
                    dve.tensor_scalar(hit[:, b % 2, :], bucket[:, :], float(b), 0.0, ALU.is_equal, ALU.add,
                                      accum_out=small[:, 0, b:b + 1]).then_inc(s_dve, 1)
                    chain[0] += 1
                dve.wait_ge(s_dve, chain[0])
                dve.tensor_copy(small[:, 1, 0:N_BUCKETS], tot).then_inc(s_tot, 1)
                dve.wait_ge(s_pre, o + 1)
                link(dve.tensor_scalar(small_i[:, 0:N_BUCKETS], bank(5, N_BUCKETS, at=64), float(P - 1), None, ALU.add))
                link(dve.tensor_scalar(small_i[:, 0:N_BUCKETS], small_i[:, 0:N_BUCKETS], P.bit_length() - 1, None,
                                       ALU.logical_shift_right))
                link(dve.tensor_copy(small[:, 1, 0:N_BUCKETS], small_i[:, 0:N_BUCKETS]))
                nt = small[:, 1, 0:N_BUCKETS]
                link(dve.tensor_tensor_scan(small[:, 2, 0:N_BUCKETS], nt, nt, 0.0, ALU.add, ALU.max))
                link(dve.tensor_tensor(small[:, 2, 0:N_BUCKETS], small[:, 2, 0:N_BUCKETS], nt, ALU.subtract))
                link(dve.scalar_tensor_tensor(small[:, 2, 0:N_BUCKETS], small[:, 2, 0:N_BUCKETS], float(P),
                                              bank(5, N_BUCKETS), ALU.mult, ALU.add))
                link(dve.tensor_scalar(small_i[0:N_BUCKETS, 0:1], bank(5, 1, N_BUCKETS, at=128), float(P - 1), None, ALU.add))
                link(dve.tensor_scalar(small_i[0:N_BUCKETS, 0:1], small_i[0:N_BUCKETS, 0:1], P.bit_length() - 1, None,
                                       ALU.logical_shift_right))
                dve.tensor_copy(small[0:N_BUCKETS, 4, 0:1], small_i[0:N_BUCKETS, 0:1]).then_inc(s_nt, 1)
                dve.wait_ge(s_end, o + 1)
                link(dve.tensor_copy(small[0:N_BUCKETS, 5, 0:1], bank(5, 1, N_BUCKETS, at=130)))
                for i in range(4):
                    dve.tensor_scalar(started[:, i * TCH:(i + 1) * TCH], tile_no[:, i * TCH:(i + 1) * TCH],
                                      small[0:N_BUCKETS, 5, 0:1], None, ALU.is_ge).then_inc(s_cmp, 1)
                dve.wait_ge(s_bt, 4 * (o + 1))
                for i in range(4):
                    last = dve.tensor_scalar(bt[:, i * TCH:(i + 1) * TCH], bank(i, TCH, 1), float(N_BUCKETS - 1), None,
                                             ALU.min)
                link(last)
                link(dve.tensor_scalar(bt_i, bt, 205.0, None, ALU.mult))
                link(dve.tensor_scalar(bt_i, bt_i, 11, None, ALU.logical_shift_right))
                link(dve.tensor_copy(tens, bt_i))
                link(dve.tensor_scalar(tens, tens, float(BANK - PER_BANK * ACC_W), None, ALU.mult))
                link(dve.scalar_tensor_tensor(acc_at[0:1, o, :], bt, float(ACC_W), tens, ALU.mult, ALU.add))
                if o == 0:
                    link(dve.tensor_scalar(max_at[0:1, 0, :], bt, float(P), None, ALU.mult))
                for b in range(N_BUCKETS):
                    link(dve.tensor_scalar(hit[:, b % 2, :], bucket[:, :], float(b), None, ALU.is_equal))
                    link(dve.tensor_tensor_scan(count, hit[:, b % 2, :], hit[:, b % 2, :], small[:, 2, b:b + 1],
                                                ALU.add, ALU.max))
                    link(dve.copy_predicated(scratch, hit[:, b % 2, :], count))
                link(dve.tensor_scalar(rows, scratch, -1.0, None, ALU.add))
                link(dve.tensor_scalar(count_i, rows, P - 1, 3, ALU.bitwise_and, ALU.logical_shift_left))
                link(dve.tensor_scalar(scratch_i, rows, 7, GROUP - 1, ALU.logical_shift_right, ALU.bitwise_and))
                link(dve.tensor_tensor(count_i, count_i, scratch_i, ALU.bitwise_or))
                link(dve.tensor_scalar(scratch_i, rows, 10, 10, ALU.logical_shift_right, ALU.logical_shift_left))
                dve.tensor_tensor(rows, scratch_i, count_i, ALU.bitwise_or).then_inc(s_plan, 1)
                dve.wait_ge(s_plan, o + 1)

            plan(0, dst_i[:, :], meta_a[:, 0:TILES_IN, M_LO], row_dst[:, :])
            plan(1, src_i, lo_src, row_src[:, :])

            ask = [0]

            def asked():
                ask[0] += 1
                dve.wait_ge(s_sr, ask[0])

            def bc(ap):
                return ap[:, :, None].to_broadcast([P, SLOTS, FEAT])

            def layernorm(out, last=None):
                v = V[:, :, :]
                mean = small[:, 3, :]
                link(dve.tensor_reduce(mean, v, AX_X, ALU.add))
                link(dve.tensor_scalar(mean, mean, 1.0 / FEAT, None, ALU.mult))
                link(dve.tensor_tensor(v, v, bc(mean), ALU.subtract))
                link(dve.tensor_tensor(Q[:, :, :], v, v, ALU.mult))
                link(dve.tensor_reduce(mean, Q[:, :, :], AX_X, ALU.add))
                dve.tensor_scalar(mean, mean, 1.0 / FEAT, LN_EPS, ALU.mult, ALU.add).then_inc(s_sq, 1)
                asked()
                link(dve.reciprocal(mean, mean))
                link(dve.tensor_tensor(out, v, bc(mean), ALU.mult))

            def acc_rows(width):
                return acc[:, :, :, 0:width]

            def banks(ap):
                return ap[:, :, :].rearrange("p (k s) w -> p k s w", k=ACC_BANKS)

            def weights(k, meta, second):
                for g in range(GROUPS):
                    gg = k * GROUPS + g
                    if gg >= 2:
                        dve.wait_ge(s_used, gg - 1)
                    for j in range(GROUP):
                        t = g * GROUP + j
                        last = dve.tensor_scalar(W[:, gg % 2, j, :], iota[:, :], meta[:, t, 0:1],
                                                 meta[:, t, second:second + 1] if second else None,
                                                 ALU.is_equal, *([ALU.mult] if second else []))
                    last.then_inc(s_w, 1)

            dve.wait_ge(s_m1, 16)
            dve.wait_ge(s_set, 4)
            dve.tensor_copy(red[:, 0, 0:1], zeros_c[:, 0:1]).then_inc(s_epi, 1)
            weights(0, meta_b, M_NORM)
            dve.wait_ge(s_used, GROUPS)
            dve.wait_ge(s_node, 48)
            for k in range(ACC_BANKS):
                last = dve.tensor_tensor(banks(V)[:, k], acc[:, k, :, 0:FEAT],
                                         rb2[:, None, :].to_broadcast([P, PER_BANK, FEAT]), ALU.add)
            last.then_inc(s_epi, 1)
            dve.wait_ge(s_epi, 2)
            link(dve.scalar_tensor_tensor(V[:, :, :], V[:, :, :], 0.0, X[:, :, :], ALU.max, ALU.add))
            layernorm(X[:, :, :])
            dve.tensor_copy(red[:, 0, 0:1], zeros_c[:, 0:1]).then_inc(s_tab, 1)

            dve.memset(ring[:, :, :, FEAT], 1.0)
            link(dve.memset(big[:, 0:SLOTS * P], NEG))
            for q in range(QUADS + 1):
                if q < QUADS:
                    if q >= 2:
                        dve.wait_ge(s_mval, q - 1)
                    for j in range(QUAD):
                        t = q * QUAD + j
                        last = dve.tensor_scalar(hot[:, q % 2, 4 + j, :], iota_b[:, :], meta_b[:, t, M_LO:M_LO + 1], NEG,
                                                 ALU.not_equal, ALU.mult)
                    last.then_inc(s_mask, 1)
                if q < QUADS_IN:
                    if q >= 2:
                        dve.wait_ge(s_deg, q - 1)
                    for j in range(QUAD):
                        t = q * QUAD + j
                        dve.tensor_scalar(hot[:, q % 2, j, :], iota_b[:, :], lo_src[:, t:t + 1], None, ALU.is_equal)
                    last = dve.tensor_tensor(hi_hot[:, q % 2, :, :],
                                             bucket[:, q * QUAD:(q + 1) * QUAD][:, :, None].to_broadcast([P, QUAD, SLOTS]),
                                             iota_b[:, None, 0:SLOTS].to_broadcast([P, QUAD, SLOTS]), ALU.is_equal)
                    last.then_inc(s_degh, 1)
                if 1 <= q <= QUADS_IN:
                    r = q - 1
                    dve.wait_ge(s_gp, r + 1)
                    dve.wait_ge(s_small, r + 1)
                    dve.tensor_tensor(rec[:, r % RECS, :, 0:FEAT],
                                      bank(7 if r % 2 else 4, QUAD * FEAT).rearrange("p (j w) -> p j w", j=QUAD),
                                      b2r[:, None, :].to_broadcast([P, QUAD, FEAT]), ALU.add).then_inc(s_rec, 1)
                if q >= 1:
                    r = q - 1
                    if r % 2 == 0:
                        regs = offsets(DVE_ONLY, max_at, 0, r // 2)
                    dve.wait_ge(s_mT, r + 1)
                    dve.tensor_reduce(red[:, r % 2, :], bank(r % 2).rearrange("p (j n) -> p j n", j=QUAD), AX_X,
                                      ALU.max).then_inc(s_red, 1)
                    dve.wait_ge(s_red, r + 1)
                    for j in range(QUAD):
                        at = regs[(r % 2) * QUAD + j]
                        link(dve.tensor_tensor(big[:, bass.ds(at, 1)], big[:, bass.ds(at, 1)], red[:, r % 2, j:j + 1],
                                               ALU.max))
            link(dve.tensor_scalar(small[:, 6, :], seg_run, NEG / 2, None, ALU.is_gt))
            dve.tensor_tensor(seg_max[:, :], seg_run, small[:, 6, :], ALU.mult).then_inc(s_maxd, 1)
            for b in range(SLOTS):
                dve.wait_ge(s_bc, b + 1)
                dve.tensor_copy(big[:, b * P:(b + 1) * P], bank(b % 2, P)).then_inc(s_bcc, 1)
            dve.wait_ge(s_deg, QUADS_IN)
            dve.tensor_scalar(small[:, 7, :], bank(3, SLOTS), 1.0, None, ALU.add).then_inc(s_sq, 1)
            asked()
            dve.reciprocal(dinv[:, :], small[:, 7, :]).then_inc(s_epi, 1)
            for g in range(GROUPS):
                gg = GROUPS + g
                if g >= 2:
                    dve.wait_ge(s_used, gg - 1)
                for j in range(GROUP):
                    last = dve.tensor_scalar(hot[:, g % 2, j, :], iota_b[:, :], meta_b[:, g * GROUP + j, M_LO:M_LO + 1],
                                             None, ALU.is_equal)
                link(last)
                dve.wait_ge(s_ex, g + 1)
                dve.scalar_tensor_tensor(W[:, gg % 2, :, :], ex[:, g % 2, :, :], 1.0, hot[:, g % 2, :, :],
                                         ALU.min, ALU.mult).then_inc(s_w, 1)
            dve.wait_ge(s_used, 2 * GROUPS)
            link(dve.tensor_scalar(small[:, 5, :].rearrange("p (k s) -> p k s", k=ACC_BANKS), acc[:, :, :, FEAT],
                                   1e-30, None, ALU.max))
            link(dve.reciprocal(small[:, 5, :], small[:, 5, :]))
            for k in range(ACC_BANKS):
                inv = small[:, 5, k * PER_BANK:(k + 1) * PER_BANK]
                last = dve.tensor_tensor(banks(V)[:, k], acc[:, k, :, 0:FEAT],
                                         inv[:, :, None].to_broadcast([P, PER_BANK, FEAT]), ALU.mult)
            last.then_inc(s_epi, 1)
            dve.wait_ge(s_epi, 4)
            dve.tensor_scalar(Q[:, :, :], V[:, :, :], 0.0, None, ALU.min).then_inc(s_sq, 1)
            asked()
            link(dve.tensor_scalar(V[:, :, :], V[:, :, :], 0.0, -1.0, ALU.max, ALU.add))
            link(dve.tensor_tensor(V[:, :, :], V[:, :, :], Q[:, :, :], ALU.add))
            link(dve.tensor_tensor(V[:, :, :], V[:, :, :], X[:, :, :], ALU.add))
            layernorm(X[:, :, :])
            dve.tensor_tensor(V[:, :, :], X[:, :, :], bc(dinv[:, :]), ALU.mult).then_inc(s_tab, 1)
            dve.wait_ge(s_m2, 16 * GROUP)
            for k in (2, 3):
                weights(k, meta_a, 0)
                dve.wait_ge(s_used, (k + 1) * GROUPS)
                dve.wait_ge(s_tabw, 16 * k)
                dve.wait_ge(s_tab, k)
                for i in range(ACC_BANKS):
                    last = dve.tensor_tensor(banks(V)[:, i], acc[:, i, :, 0:FEAT], banks(V)[:, i], ALU.add)
                last.then_inc(s_epi, 1)
                dve.wait_ge(s_epi, k + 3)
                link(dve.tensor_tensor(V[:, :, :], V[:, :, :], bc(dinv[:, :]), ALU.mult))
                if k == 2:
                    dve.tensor_tensor(V[:, :, :], V[:, :, :], bc(dinv[:, :]), ALU.mult).then_inc(s_tab, 1)
            link(dve.tensor_tensor(V[:, :, :], V[:, :, :], X[:, :, :], ALU.add))
            layernorm(X[:, :, :])
            dve.wait_ge(s_embg, 16 * SLOTS)
            for k in range(ACC_BANKS):
                last = dve.tensor_copy(emb_of_v[:, k, :, 0:EMB], embs[:, k * PER_BANK:(k + 1) * PER_BANK, 0:EMB])
            link(last)
            dve.tensor_copy(embs[:, :, EMB - 1], node_mj[:, :]).then_inc(s_tab, 1)
            for g in range(GROUPS):
                gg = 4 * GROUPS + g
                dve.wait_ge(s_recl[g % 2], 16 * (g // 2 + 1))
                if g >= 2:
                    dve.wait_ge(s_used, gg - 1)
                for j in range(GROUP):
                    last = dve.tensor_scalar(W[:, gg % 2, j, :], iota[:, :], rec_in[:, g % 2, j, R_LO:R_LO + 1], None,
                                             ALU.is_equal)
                last.then_inc(s_oh, 1)
                dve.wait_ge(s_gat[gg % RING], 16 * GROUP * (gg // RING + 1))
                rows = ring[:, gg % RING, :, :]
                dve.wait_ge(s_ei, g + 1)
                link(dve.tensor_tensor(prod, bank(7, GROUP * EMB).rearrange("p (j w) -> p j w", j=GROUP),
                                       rows[:, :, X3_EMB:X3_W], ALU.mult))
                dve.tensor_tensor(wgt, rec_in[:, g % 2, :, R_CW], rows[:, :, X3_MJ], ALU.mult)
                dve.tensor_copy(msg[:, gg % 2, :, FEAT], rows[:, :, X3_MJ])
                link(dve.tensor_reduce(adapt, prod, AX_X, ALU.add))
                m = msg[:, gg % 2, :, 0:FEAT]
                full = [P, GROUP, FEAT]
                dve.tensor_tensor(m, rec_in[:, g % 2, :, 0:FEAT], adapt[:, :, None].to_broadcast(full), ALU.add) \
                    .then_inc(s_eir, 1)
                dve.wait_ge(s_eir, g + 1)
                link(dve.tensor_tensor(m, m, rows[:, :, 0:FEAT], ALU.mult))
                dve.tensor_tensor(m, m, wgt[:, :, None].to_broadcast(full), ALU.mult).then_inc(s_w, 1)
            dve.wait_ge(s_used, 5 * GROUPS)
            link(dve.tensor_scalar(small[:, 5, :].rearrange("p (k s) -> p k s", k=ACC_BANKS), acc[:, :, :, FEAT],
                                   1e-8, None, ALU.max))
            link(dve.reciprocal(small[:, 5, :], small[:, 5, :]))
            for k in range(ACC_BANKS):
                inv = small[:, 5, k * PER_BANK:(k + 1) * PER_BANK]
                last = dve.tensor_tensor(banks(V)[:, k], acc[:, k, :, 0:FEAT],
                                         inv[:, :, None].to_broadcast([P, PER_BANK, FEAT]), ALU.mult)
            link(last)
            link(dve.tensor_tensor(V[:, :, :], V[:, :, :], X[:, :, :], ALU.add))
            layernorm(V[:, :, :])
            row = [P, SLOTS, FEAT]
            link(dve.tensor_tensor(V[:, :, :], V[:, :, :], gamma[:, None, :].to_broadcast(row), ALU.mult))
            link(dve.tensor_tensor(V[:, :, :], V[:, :, :], beta[:, None, :].to_broadcast(row), ALU.add))
            link(dve.tensor_tensor(V[:, :, :], V[:, :, :], X[:, :, :], ALU.add))
            layernorm(X[:, :, :])
            dve.tensor_copy(red[:, 0, 0:1], zeros_c[:, 0:1]).then_inc(s_tab, 1)


def kernel(**inputs):
    import concourse.bacc as bacc
    from concourse.bass_utils import run_bass_kernel_spmd

    a = {k: np.asarray(v) for k, v in inputs.items()}

    def edges(v, fill):
        v = np.concatenate([v.reshape(-1), np.full(TILES_IN * P - N_EDGES, fill, v.dtype)])
        return np.ascontiguousarray(v.reshape(TILES_IN, P).T)

    def nodes(v):
        v = v.reshape(N_NODES, -1)
        v = np.concatenate([v, np.zeros((NODES - N_NODES, v.shape[1]), v.dtype)])
        return v

    def by_place(v):
        v = nodes(v)
        return np.ascontiguousarray(v.reshape(SLOTS, P, v.shape[1]).transpose(1, 0, 2))

    f = np.float32
    default = np.zeros((P, GROUP * REC), f)
    default_rec = default.copy().reshape(P, GROUP, REC)
    default_rec[:, :, R_LO] = -1.0
    i = np.arange(P)
    attrT = np.zeros((ATTR, TILES_IN * P), f)
    attrT[:, :N_EDGES] = a["edge_attr_40"].T
    embT = np.zeros((EMB, P), f)
    embT[:, :a["L3_gnn_emb"].shape[0]] = a["L3_gnn_emb"].T
    arrays = {
        "src": edges(a["src"], PAD_NODE), "dst": edges(a["dst"], PAD_NODE),
        "etype": edges(a["edge_type_8"], 0), "norm": edges(a["edge_weight1"], 0), "dist": edges(a["edge_weight"], 0),
        "attrT": attrT,
        "x": by_place(a["x"]), "xT": np.ascontiguousarray(nodes(a["x"]).T),
        "node_z": by_place(a["node_type_119"])[:, :, 0], "node_mj": by_place(a["node_vec"])[:, :, 0],
        "weight1": a["L0_gnn_weight1"], "weight2": a["L0_gnn_weight2"],
        "bias1": a["L0_gnn_bias1"], "bias2": a["L0_gnn_bias2"],
        "W1T": np.ascontiguousarray(a["L3_gnn_W1"].T), "W2T": np.ascontiguousarray(a["L3_gnn_W2"].T),
        "b1": a["L3_gnn_b1"], "b2": a["L3_gnn_b2"], "embT": embT,
        "adaptT": np.ascontiguousarray(a["L3_gnn_adaptW"].T),
        "gamma": a["L3_gnn_gamma"], "beta": a["L3_gnn_beta"],
        "const": np.stack([np.eye(P, dtype=f), (i[:, None] < i[None, :]).astype(f),
                           (i[:, None] <= i[None, :]).astype(f), np.tile(i.astype(f), (P, 1))]),
        "tile_no": np.tile(np.arange(TILES, dtype=f), (N_BUCKETS, 1)),
        "default": default_rec.reshape(P, GROUP * REC),
        "default_meta": np.tile(np.array([-1, 0, 0, 0], f), (P, GROUP)),
    }
    arrays = {k: np.ascontiguousarray(v) for k, v in arrays.items()}
    nc = bacc.Bacc("TRN2", target_bir_lowering=False, num_devices=1)
    A = {k: nc.dram_tensor(f"in_{k}", v.shape, mybir.dt.from_np(v.dtype), kind="ExternalInput").ap()
         for k, v in arrays.items()}
    A["out"] = nc.dram_tensor("out_x", (N_NODES, FEAT), F32, kind="ExternalOutput").ap()
    build(nc, A)
    r = run_bass_kernel_spmd(nc, [{f"in_{k}": v for k, v in arrays.items()}], core_ids=[0])
    return r.results[0]["out_x"]
```

```python
from contextlib import ExitStack

import numpy as np
import concourse.bass as bass
from concourse import mybir

F32 = mybir.dt.float32
BF16 = mybir.dt.bfloat16
I32 = mybir.dt.int32
U16 = mybir.dt.uint16
ALU = mybir.AluOpType
ACT = mybir.ActivationFunctionType
AX_X = mybir.AxisListType.X
PE_ONLY = (mybir.EngineType.PE,)
DVE_ONLY = (mybir.EngineType.DVE,)
ACT_ONLY = (mybir.EngineType.Activation,)

P = 128
N_NODES, FEAT, N_EDGES = 6250, 48, 206250
RELS, ATTR, EMB = 8, 40, 32
N_BUCKETS = -(-N_NODES // P)
SLOTS = N_BUCKETS + 1
NODES = SLOTS * P
PAD_NODE = N_BUCKETS * P - 1
assert PAD_NODE >= N_NODES
TILES_IN = -(-N_EDGES // P)
GROUP = 8
GROUPS = -(-(TILES_IN + N_BUCKETS) // GROUP)
TILES = GROUPS * GROUP
QUAD = 4
QUADS_IN = TILES_IN // QUAD
QUADS = TILES // QUAD
assert QUADS_IN * QUAD == TILES_IN
BANK = 512
ACC_W = 50
PER_BANK = BANK // ACC_W
ACC_BANKS = SLOTS // PER_BANK
assert ACC_BANKS * PER_BANK == SLOTS
REC = 52
R_CW, R_LO, R_DST = FEAT, FEAT + 1, FEAT + 2
META = 4
M_LO, M_IDX, M_SRC, M_NORM = range(META)
X3_MJ, X3_EMB = FEAT, FEAT + 1
X3_W = FEAT + 1 + EMB
RING = 4
RECS = 8
SPAN = 2
CHUNK = 2
CHUNKS = SLOTS // CHUNK
PAIRS = RELS // 2
CUTOFF, LN_EPS = 6.0, 1e-5
NEG = -float(2.0 ** 126)
TCH = TILES // 4
ICH = TILES_IN // 4
AT_DST, AT_SRC, AT_NEXT, AT_BUCKET = 0, 32, 64, 96


def build(nc, A):
    with ExitStack() as ctx:
        def sb(name, shape, dt=F32):
            return ctx.enter_context(nc.sbuf_tensor(name, shape, dt))

        def sem(name):
            return ctx.enter_context(nc.semaphore(name))

        def dram(name, shape, dt=F32):
            return nc.dram_tensor(name, shape, dt, kind="Internal").ap()

        h2_table = dram("h2_table", (NODES * RELS, FEAT))
        x1_table = dram("x1_table", (NODES, FEAT))
        y_table = [dram("y0_table", (NODES, FEAT)), dram("y1_table", (NODES, FEAT))]
        x3_table = dram("x3_table", (NODES, X3_W))
        emb_table = dram("emb_table", (P, 2 * EMB))
        by_dst = dram("by_dst", (TILES * P, META))
        by_src = dram("by_src", (TILES * P, REC))

        ident = sb("ident", [P, P])
        before = sb("before", [P, P])
        upto = sb("upto", [P, P])
        iota = sb("iota", [P, SPAN * P])
        iota_b = sb("iota_b", [P, SPAN * P], BF16)
        ones = sb("ones", [P, P])
        zeros_b = sb("zeros_b", [P, BANK], BF16)
        default = sb("default", [P, GROUP * REC])
        default_meta = sb("default_meta", [P, GROUP * META])
        first = sb("first", [P, P])
        w1T = sb("w1T", [ATTR, FEAT])
        w2T = sb("w2T", [FEAT, FEAT])
        b1c = sb("b1c", [FEAT, 1])
        b2r = sb("b2r", [P, FEAT])
        embT = sb("embT", [EMB, P])
        adaptT = sb("adaptT", [EMB, EMB])
        emb_rows = sb("emb_rows", [P, 2 * EMB])
        rw1 = sb("rw1", [FEAT, PAIRS, 2 * FEAT])
        rw2 = sb("rw2", [2 * FEAT, PAIRS, 2 * FEAT])
        rb1 = sb("rb1", [2 * FEAT, 1])
        rb2 = sb("rb2", [P, FEAT])
        seg_run = sb("seg_run", [P, SLOTS])
        order_mark = sb("order_mark", [P, 1])
        gamma = sb("gamma", [P, FEAT])
        beta = sb("beta", [P, FEAT])
        zeros_c = sb("zeros_c", [P, 1])
        halfpi = sb("halfpi", [P, 1])

        big = sb("big", [P, 4 * TILES_IN])
        src_i = big[:, 0:TILES_IN].bitcast(I32)
        dst_i = sb("dst_i", [P, TILES_IN], I32)
        until_sorted = sb("until_sorted", [P, 2 * TILES_IN])
        cw = until_sorted[:, 0:TILES_IN]
        lo_src = until_sorted[:, TILES_IN:2 * TILES_IN]
        embs = until_sorted[:, 0:SLOTS * 2 * EMB].rearrange("p (b w) -> p b w", w=2 * EMB)
        row_dst = sb("row_dst", [P, TILES_IN], I32)
        row_src = sb("row_src", [P, TILES_IN], I32)
        bucket = sb("bucket", [P, TILES_IN], BF16)
        hit = big[:, TILES_IN:2 * TILES_IN].bitcast(U16).rearrange("p (s t) -> p s t", s=2)
        count = big[:, 2 * TILES_IN:3 * TILES_IN]
        scratch = big[:, 3 * TILES_IN:4 * TILES_IN]
        assert 4 * TILES_IN >= SLOTS * P
        scratch_i = scratch.bitcast(I32)
        count_i = count.bitcast(I32)
        meta_a = sb("meta_a", [P, TILES, META])
        meta_b = sb("meta_b", [P, TILES, META])
        small = sb("small", [P, 8, SLOTS])
        small_i = sb("small_i", [P, SLOTS], I32)
        at_table = sb("at_table", [P, TILES], I32)
        flag = sb("flag", [P, 1], I32)

        X = sb("X", [P, SLOTS, FEAT])
        V = sb("V", [P, SLOTS, FEAT])
        Q = sb("Q", [P, SLOTS, FEAT])
        node_z = sb("node_z", [P, SLOTS], I32)
        node_mj = sb("node_mj", [P, SLOTS])
        tile_no = X[0:N_BUCKETS, :, :].rearrange("p b w -> p (b w)")[:, 0:TILES]
        dinv = sb("dinv", [P, SLOTS])
        seg_max = sb("seg_max", [P, SLOTS])

        ring = sb("ring", [P, RING, GROUP, X3_W])
        ex = sb("ex", [P, 2, QUAD, SPAN * P])
        ring_f = ring[:, :, :, :].rearrange("p r j w -> p (r j w)")
        xT = ring_f[0:FEAT, 0:2 * CHUNK * P].rearrange("p (s n) -> p s n", s=2)
        h1 = ring_f[0:2 * FEAT, 512:512 + PAIRS * CHUNK * P].rearrange("p (q n) -> p q n", q=PAIRS)
        h2 = ring_f[:, 1536:1536 + 2 * RELS * FEAT].rearrange("p (s n) -> p s n", s=2)
        W = sb("W", [P, 2, QUAD, SPAN * P])
        W_g = W[:, :, :, :].rearrange("p s j (h n) -> p s (j h) n", n=P)
        hot = row_dst[:, 0:QUAD * SPAN * P].bitcast(BF16).rearrange("p (s j n) -> p s j n", s=2, j=QUAD)
        hot_lo = sb("hot_lo", [P, 2, QUAD, P], BF16)
        free = meta_a[:, :, :].rearrange("p t w -> p (t w)")
        attr = free[0:ATTR, 0:4 * QUAD * P].rearrange("p (s n) -> p s n", s=2)
        sT = free[0:FEAT, 2048:2048 + 2 * QUAD * P].rearrange("p (s n) -> p s n", s=2)
        rec = free[:, 3072:3072 + RECS * QUAD * REC].rearrange("p (s j w) -> p s j w", s=RECS, j=QUAD)
        rec_i = rec.bitcast(I32)
        started = free[0:N_BUCKETS, 0:TILES]
        bt = free[:, TILES:2 * TILES]
        tens = free[:, 2 * TILES:3 * TILES]
        bt_i = free[:, 3 * TILES:4 * TILES].bitcast(I32)
        red = sb("red", [P, 2, QUAD, SPAN])
        hi_hot = sb("hi_hot", [P, 2, QUAD, SLOTS], BF16)

        ps = ctx.enter_context(nc.psum_tensor("ps", [P, 8 * BANK], F32))

        def bank(i, n=BANK, parts=P, at=0):
            return ps[0:parts, i * BANK + at:i * BANK + at + n]

        acc = ps[:, 0:ACC_BANKS * BANK].rearrange("p (k c) -> p k c", c=BANK)[:, :, 0:PER_BANK * ACC_W] \
            .rearrange("p k (s w) -> p k s w", w=ACC_W)

        s_const = sem("s_const")
        s_edges = sem("s_edges")
        s_node = sem("s_node")
        s_set = sem("s_set")
        s_xT = [sem(f"s_xT{i}") for i in range(2)]
        s_h1p = sem("s_h1p")
        s_h1 = sem("s_h1")
        s_h2p = sem("s_h2p")
        s_h2 = sem("s_h2")
        s_h2w = [sem(f"s_h2w{i}") for i in range(2)]
        s_embp = sem("s_embp")
        s_embs = sem("s_embs")
        s_embw = sem("s_embw")
        s_embg = sem("s_embg")
        s_init = sem("s_init")
        s_dve = sem("s_dve")
        s_cosarg = sem("s_cosarg")
        s_cos = sem("s_cos")
        s_b0in, s_b0, s_flagin, s_flagp, s_flag = [sem(n) for n in ("s_b0in", "s_b0", "s_flagin", "s_flagp", "s_flag")]
        s_tot = [sem(f"s_tot{o}") for o in range(2)]
        s_pre = [sem(f"s_pre{o}") for o in range(2)]
        s_nt = [sem(f"s_nt{o}") for o in range(2)]
        s_end = [sem(f"s_end{o}") for o in range(2)]
        s_cmp = [sem(f"s_cmp{o}") for o in range(2)]
        s_bt = [sem(f"s_bt{o}") for o in range(2)]
        s_plan = [sem(f"s_plan{o}") for o in range(2)]
        s_branch = sem("s_branch")
        s_order = sem("s_order")
        s_init1 = sem("s_init1")
        s_s1 = sem("s_s1")
        s_m1 = sem("s_m1")
        s_m2 = sem("s_m2")
        s_gat = [sem(f"s_gat{i}") for i in range(RING)]
        s_w = sem("s_w")
        s_used = sem("s_used")
        s_zero = sem("s_zero")
        s_epi = sem("s_epi")
        s_tab = sem("s_tab")
        s_tabw = sem("s_tabw")
        s_attr = [sem(f"s_attr{i}") for i in range(2)]
        s_sp = sem("s_sp")
        s_s = sem("s_s")
        s_gp = sem("s_gp")
        s_small = sem("s_small")
        s_rec = sem("s_rec")
        s_sc = [sem(f"s_sc{i}") for i in range(RECS)]
        s_degh = sem("s_degh")
        s_deg = sem("s_deg")
        s_mask = sem("s_mask")
        s_mval = sem("s_mval")
        s_mT = sem("s_mT")
        s_red = sem("s_red")
        s_maxd = sem("s_maxd")
        s_diag = sem("s_diag")
        s_bc = sem("s_bc")
        s_bcc = sem("s_bcc")
        s_ex = sem("s_ex")
        s_sq = sem("s_sq")
        s_sr = sem("s_sr")
        s_recl = [sem(f"s_recl{i}") for i in range(3)]
        s_dinv = sem("s_dinv")
        s_prod = sem("s_prod")
        s_oh = sem("s_oh")
        s_ohp = sem("s_ohp")
        s_ohT = sem("s_ohT")
        s_ei = sem("s_ei")
        s_eir = sem("s_eir")
        s_out = sem("s_out")

        block = ctx.enter_context(nc.Block())

        n_const = [0]
        asks = []

        PLAN_AT = GROUPS // 3
        COS_AT = 12
        MAX_EARLY = GROUPS
        assert QUADS - MAX_EARLY == QUADS // 2

        by_dst_v = by_dst.rearrange("(g p j) w -> p g (j w)", p=P, j=GROUP)
        by_src_v = by_src.rearrange("(g p j) w -> p g j w", p=P, j=GROUP)

        def table_v(t):
            return t.rearrange("(b p) w -> p b w", p=P)

        oh_T = ex[:, :, :, :].rearrange("p s j (h n) -> p s (j h) n", n=P)
        meta_f = meta_b[:, :, :].rearrange("p t w -> p (t w)")
        W3 = meta_f[:, 0:4 * GROUP * P].rearrange("p (s j n) -> p s j n", s=4, j=GROUP)
        rec_in = meta_f[:, 4096:4096 + 3 * GROUP * REC].rearrange("p (s j w) -> p s j w", s=3, j=GROUP)
        msg = big[:, 1024:1024 + 2 * GROUP * ACC_W].rearrange("p (s j w) -> p s j w", s=2, j=GROUP)
        prod = big[:, 2048:2048 + GROUP * EMB].rearrange("p (j w) -> p j w", j=GROUP)
        adapt = big[:, 2304:2304 + GROUP]
        wgt_2 = big[:, 2320:2320 + 2 * GROUP].rearrange("p (s j) -> p s j", s=2)
        emb_of = big[:, 2560:2560 + ACC_BANKS * BANK]
        emb_of_v = emb_of.rearrange("p (k c) -> p k c", c=BANK)[:, :, 0:PER_BANK * ACC_W] \
            .rearrange("p k (s w) -> p k s w", w=ACC_W)

        REQ = [("sqrt", small[:, 3, :]), ("sqrt", small[:, 7, :]), ("exp", Q), ("sqrt", small[:, 3, :]),
               ("sqrt", small[:, 3, :]), ("sqrt", small[:, 3, :]), ("sqrt", small[:, 3, :])]

        @block.sync
        def _(sp):
            def const(dst, src):
                sp.dma_start(dst, src).then_inc(s_const, 16)
                n_const[0] += 16

            sp.dma_start(dst_i[:, :], A["dst"]).then_inc(s_edges, 16)
            sp.dma_start(count_i, A["etype"]).then_inc(s_edges, 16)
            sp.dma_start(src_i, A["src"]).then_inc(s_edges, 16)
            sp.dma_start(scratch, A["norm"]).then_inc(s_edges, 16)
            sp.dma_start(cw, A["dist"]).then_inc(s_edges, 16)
            const(ident[:, :], A["const"][0])
            const(before[:, :], A["const"][1])
            const(upto[:, :], A["const"][2])
            for h in range(SPAN):
                const(iota[:, h * P:(h + 1) * P], A["const"][3 + h])
            const(first[:, :], A["const"][3 + SPAN])
            const(tile_no, A["tile_no"])
            const(default[:, :], A["default"])
            const(default_meta[:, :], A["default_meta"])
            const(w1T[:, :], A["W1T"])
            const(w2T[:, :], A["W2T"])
            const(b1c[:, :], A["b1"].rearrange("(a b) -> a b", b=1))
            const(b2r[:, :], A["b2"].rearrange("(a b) -> a b", a=1).to_broadcast([P, FEAT]))
            const(embT[:, :], A["embT"])
            const(adaptT[:, :], A["adaptT"])
            for q in range(PAIRS):
                for r in range(2):
                    const(rw1[:, q, r * FEAT:(r + 1) * FEAT], A["weight1"][2 * q + r])
            for r in range(2):
                const(rb1[r * FEAT:(r + 1) * FEAT, :], A["bias1"].rearrange("(a b) -> a b", b=1))
            const(rb2[:, :], A["bias2"].rearrange("(a b) -> a b", a=1).to_broadcast([P, FEAT]))
            const(gamma[:, :], A["gamma"].rearrange("(a b) -> a b", a=1).to_broadcast([P, FEAT]))
            const(beta[:, :], A["beta"].rearrange("(a b) -> a b", a=1).to_broadcast([P, FEAT]))
            sp.wait_ge(s_set, 1)
            for q in range(PAIRS):
                for r in range(2):
                    const(rw2[r * FEAT:(r + 1) * FEAT, q, r * FEAT:(r + 1) * FEAT], A["weight2"][2 * q + r])
            sp.dma_start(node_z[:, :], A["node_z"]).then_inc(s_node, 16)
            sp.dma_start(node_mj[:, :], A["node_mj"]).then_inc(s_node, 16)
            for c in range(CHUNKS):
                if c >= 2:
                    sp.wait_ge(s_h1p, c - 1)
                sp.dma_start(xT[:, c % 2, :], A["xT"][:, c * CHUNK * P:(c + 1) * CHUNK * P]) \
                    .then_inc(s_xT[c % 2], 16)
                if c >= 1:
                    for n in range((c - 1) * CHUNK, c * CHUNK):
                        sp.wait_ge(s_h2, n + 1)
                        sp.dma_start(h2_table[n * P * RELS:(n + 1) * P * RELS, :].rearrange("(p r) w -> p (r w)", r=RELS),
                                     h2[:, n % 2, :]).then_inc(s_h2w[n % 2], 16)
            for n in range((CHUNKS - 1) * CHUNK, SLOTS):
                sp.wait_ge(s_h2, n + 1)
                sp.dma_start(h2_table[n * P * RELS:(n + 1) * P * RELS, :].rearrange("(p r) w -> p (r w)", r=RELS),
                             h2[:, n % 2, :]).then_inc(s_h2w[n % 2], 16)
            sp.wait_ge(s_embs, 1)
            sp.dma_start(emb_table, emb_rows[:, :]).then_inc(s_embw, 16)
            dv = by_src.rearrange("(g p j) w -> p g (j w)", p=P, j=GROUP)
            sp.dma_start(dv, default[:, None, :].to_broadcast([P, GROUPS, GROUP * REC])).then_inc(s_init, 16)
            sp.wait_ge(s_plan[1], 1)
            sp.dma_start(X[:, :, :], A["x"]).then_inc(s_node, 16)
            for c in range(-(-QUADS_IN // 2)):
                n = min(2, QUADS_IN - 2 * c)
                if c >= 2:
                    sp.wait_ge(s_sp, 2 * (c - 1))
                sp.dma_start(attr[:, c % 2, 0:n * QUAD * P], A["attrT"][:, 2 * c * QUAD * P:(2 * c + n) * QUAD * P]) \
                    .then_inc(s_attr[c % 2], 16)
            sp.wait_ge(s_tab, 1)
            sp.dma_start(table_v(x1_table), X[:, :, :]).then_inc(s_tabw, 16)
            for i in range(RECS):
                sp.wait_ge(s_sc[i], 16 * QUAD * len(range(i, QUADS_IN, RECS)))
            for j in range(GROUP):
                sp.dma_start(meta_a[:, :, :].rearrange("p (g j) w -> p g j w", j=GROUP)[:, :, j, :],
                             by_src_v[:, :, j, FEAT:REC]).then_inc(s_m2, 16)
            for i in range(2):
                sp.wait_ge(s_tab, 2 + i)
                sp.dma_start(table_v(y_table[i]), V[:, :, :]).then_inc(s_tabw, 16)
            sp.wait_ge(s_tab, 4)
            sp.dma_start(table_v(x3_table)[:, :, 0:FEAT], X[:, :, :]).then_inc(s_tabw, 16)
            sp.dma_start(table_v(x3_table)[:, :, FEAT:X3_W], embs[:, :, EMB - 1:2 * EMB]).then_inc(s_tabw, 16)
            for g in range(GROUPS):
                if g >= 3:
                    sp.wait_ge(s_eir, g - 2)
                sp.dma_start(rec_in[:, g % 3, :, :], by_src_v[:, g, :, :]).then_inc(s_recl[g % 3], 16)
            sp.wait_ge(s_tab, 5)
            full = N_NODES // P
            sp.dma_start(A["out"][0:full * P, :].rearrange("(b p) w -> p b w", p=P), X[:, 0:full, :]).then_inc(s_out, 16)
            sp.dma_start(A["out"][full * P:N_NODES, :], X[0:N_NODES - full * P, full, :]).then_inc(s_out, 16)
            sp.wait_ge(s_out, 32)

        @block.gpsimd
        def _(pool):
            meta_b_i = meta_b[:, :, :].bitcast(I32)
            meta_a_i = meta_a[:, :, :].bitcast(I32)
            pool.wait_ge(s_flag, 1)
            halves = (slice(0, GROUPS // 2), slice(GROUPS // 2, GROUPS))
            with pool.If(pool.value_load(flag[0:1, 0:1], min_val=0, max_val=1)):
                for h in halves:
                    pool.dma_start(by_dst_v[:, h, :], default_meta[:, None, :].to_broadcast([P, GROUPS // 2, GROUP * META])) \
                        .then_inc(s_init1, 16)
                pool.wait_ge(s_plan[0], 1)
                pool.wait_ge(s_init1, 32)
                for t in range(TILES_IN):
                    pool.indirect_dma_start(by_dst, bass.IndirectOffsetOnAxis(ap=row_dst[:, t:t + 1], axis=0),
                                            meta_b[:, t, :], None).then_inc(s_s1, 16)
                pool.wait_ge(s_s1, 16 * TILES_IN)
                for h in halves:
                    pool.dma_start(meta_b[:, :, :].rearrange("p (g j) w -> p g (j w)", j=GROUP)[:, h, :],
                                   by_dst_v[:, h, :]).then_inc(s_m1, 16)
                pool.wait_ge(s_m1, 32)
            pool.memset(order_mark[:, :], 0.0).then_inc(s_order, 1)

            def gather(k, table, width, index):
                for g in range(GROUPS):
                    gg = k * GROUPS + g
                    if gg >= RING:
                        pool.wait_ge(s_used, 2 * (gg - RING + 1))
                    for j in range(GROUP):
                        pool.indirect_dma_start(ring[:, gg % RING, j, 0:width], None, table,
                                                bass.IndirectOffsetOnAxis(ap=index(g * GROUP + j), axis=0)) \
                            .then_inc(s_gat[gg % RING], 16)

            for i in range(2):
                pool.wait_ge(s_h2w[i], 16 * SLOTS // 2)
            gather(0, h2_table, FEAT, lambda t: meta_b_i[:, t, M_IDX:M_IDX + 1])
            pool.wait_ge(s_plan[1], 1)
            pool.wait_ge(s_init, 16)
            for q in range(QUADS_IN):
                pool.wait_ge(s_rec, q + 1)
                for j in range(QUAD):
                    t = q * QUAD + j
                    pool.indirect_dma_start(by_src, bass.IndirectOffsetOnAxis(ap=row_src[:, t:t + 1], axis=0),
                                            rec[:, q % RECS, j, :], None).then_inc(s_sc[q % RECS], 16)
            pool.wait_ge(s_embw, 16)
            pool.wait_ge(s_node, 48)
            pool.wait_ge(s_small, QUADS_IN)
            pool.wait_ge(s_degh, QUADS_IN)
            for b in range(SLOTS):
                pool.indirect_dma_start(embs[:, b, :], None, emb_table,
                                        bass.IndirectOffsetOnAxis(ap=node_z[:, b:b + 1], axis=0)).then_inc(s_embg, 16)
            pool.wait_ge(s_tabw, 16)
            gather(1, x1_table, FEAT, lambda t: meta_b_i[:, t, M_SRC:M_SRC + 1])
            pool.wait_ge(s_m2, 16 * GROUP)
            by_s = lambda t: meta_a_i[:, t, R_DST - FEAT:R_DST - FEAT + 1]
            pool.wait_ge(s_tabw, 32)
            gather(2, y_table[0], FEAT, by_s)
            pool.wait_ge(s_tabw, 48)
            gather(3, y_table[1], FEAT, by_s)
            pool.wait_ge(s_tabw, 80)
            gather(4, x3_table, X3_W, by_s)

        def offsets(engines, row, t0, n):
            top = N_BUCKETS - 1 if row == AT_BUCKET else (ACC_BANKS - 1) * BANK + (PER_BANK - 1) * ACC_W
            return nc.values_load_multi_w_load_instructions(
                at_table[row:row + 1, t0:t0 + n], engines=engines, min_val=0, max_val=top,
                skip_runtime_bounds_check_because="made from bucket numbers that are clamped")[1]

        @block.tensor
        def _(pe):
            pe.wait_ge(s_const, n_const[0])
            pe.wait_ge(s_set, 4)
            pe.matmul(bank(7, EMB), embT[:, :], adaptT[:, :], start=True, stop=True).then_inc(s_embp, 1)
            pe.transpose(bank(7, EMB, at=64), embT[:, :], ident[0:EMB, 0:EMB]).then_inc(s_embp, 1)
            pe.wait_ge(s_b0in, 1)
            for i in range(4):
                mm = pe.matmul(bank(i, ICH), first[:, :], count[:, i * ICH:(i + 1) * ICH], start=True, stop=True)
            mm.then_inc(s_b0, 1)

            def relation_chunk(c):
                pe.wait_ge(s_xT[c % 2], 16 * (c // 2 + 1))
                if c >= 1:
                    pe.wait_ge(s_h1, 2 * c)
                for q in range(PAIRS):
                    mm = pe.matmul(bank(5 + q // 2, CHUNK * P, 2 * FEAT, (q % 2) * CHUNK * P), rw1[:, q, :],
                                   xT[:, c % 2, :], start=True, stop=True)
                mm.then_inc(s_h1p, 1)
                pe.wait_ge(s_h1, 2 * (c + 1))
                for i in range(CHUNK):
                    n = c * CHUNK + i
                    if n == 0:
                        pe.wait_ge(s_embs, 1)
                    if n >= 2:
                        pe.wait_ge(s_h2, n - 1)
                    for q in range(PAIRS):
                        mm = pe.matmul(bank(7 if n % 2 else 4, 2 * FEAT, P, q * 2 * FEAT), h1[:, q, i * P:(i + 1) * P],
                                       rw2[:, q, :], start=True, stop=True)
                    mm.then_inc(s_h2p, 1)

            for c in range(CHUNKS):
                relation_chunk(c)
            pe.wait_ge(s_flagin, 1)
            pe.matmul(bank(3, 1), ones[:, :], small[:, 6, 0:1], start=True, stop=True).then_inc(s_flagp, 1)

            def plan_sums(o):
                pe.wait_ge(s_tot[o], 1)
                tot = small[:, 0, 0:N_BUCKETS]
                pe.matmul(bank(5, N_BUCKETS), before[:, :], tot, start=True, stop=True)
                pe.matmul(bank(5, N_BUCKETS, at=64), ones[:, :], tot, start=True, stop=True)
                pe.matmul(bank(5, 1, N_BUCKETS, at=128), tot, ones[:, 0:1], start=True, stop=True).then_inc(s_pre[o], 1)
                pe.wait_ge(s_nt[o], 1)
                pe.matmul(bank(5, 1, N_BUCKETS, at=130), upto[0:N_BUCKETS, 0:N_BUCKETS], small[0:N_BUCKETS, 4, 0:1],
                          start=True, stop=True).then_inc(s_end[o], 1)
                for i in range(4):
                    pe.wait_ge(s_cmp[o], i + 1)
                    pe.matmul(bank(6, TCH), ones[0:N_BUCKETS, :], started[:, i * TCH:(i + 1) * TCH],
                              start=True, stop=True).then_inc(s_bt[o], 1)

            pe.wait_ge(s_flag, 1)
            with pe.If(pe.value_load(flag[0:1, 0:1], min_val=0, max_val=1)):
                plan_sums(0)
            pe.wait_ge(s_order, 1)

            def zero_acc():
                for i in range(ACC_BANKS):
                    pe.matmul(bank(i, BANK), zeros_b[:, 0:P], zeros_b[:, :], start=True, stop=False,
                              skip_group_check=True)

            def transpose_logits(h, bank_no, lag):
                q, u = h // 2, h % 2
                pe.wait_ge(s_mval, q + 1)
                if h >= lag:
                    pe.wait_ge(s_red, h - lag + 1)
                for j in range(2):
                    for n in range(SPAN):
                        mm = pe.transpose(bank(bank_no, P, at=(2 * j + n) * P),
                                          ex[:, q % 2, 2 * u + j, n * P:(n + 1) * P], ident[:, :])
                mm.then_inc(s_mT, 1)

            def sum_quads(k, g, width):
                gg = k * GROUPS + g
                here = offsets(PE_ONLY, AT_DST, g * GROUP, GROUP)
                after = offsets(PE_ONLY, AT_NEXT, g * GROUP, GROUP)
                pe.wait_ge(s_gat[gg % RING], 16 * GROUP * (gg // RING + 1))
                for i in range(2):
                    if k == 0:
                        transpose_logits(2 * g + i, 7, 1)
                    pe.wait_ge(s_w, 2 * gg + i + 1)
                    for j in range(QUAD):
                        t = i * QUAD + j
                        for h, regs in enumerate((here, after)):
                            mm = pe.matmul(ps[:, bass.ds(regs[t], width)], W[:, i, j, h * P:(h + 1) * P],
                                           ring[:, gg % RING, t, 0:width], start=False, stop=False,
                                           skip_group_check=True)
                    mm.then_inc(s_used, 1)

            def sum_group(k, g, width, rhs, weights, slots):
                gg = k * GROUPS + g
                regs = offsets(PE_ONLY, AT_SRC, g * GROUP, GROUP)
                pe.wait_ge(s_gat[gg % RING], 16 * GROUP * (gg // RING + 1))
                pe.wait_ge(s_w, 2 * gg + 2)
                for j in range(GROUP):
                    mm = pe.matmul(ps[:, bass.ds(regs[j], width)], weights[:, gg % slots, j, :], rhs(gg, j),
                                   start=False, stop=False, skip_group_check=True)
                mm.then_inc(s_used, 2)

            def degree(q):
                pe.wait_ge(s_degh, q + 1)
                for j in range(QUAD):
                    mm = pe.matmul(bank(2, SLOTS), hot_lo[:, q % 2, j, :], hi_hot[:, q % 2, j, :],
                                   start=(q == 0 and j == 0), stop=(q == QUADS_IN - 1 and j == QUAD - 1))
                mm.then_inc(s_deg, 1)

            pe.wait_ge(s_epi, 1)
            zero_acc()
            for g in range(GROUPS):
                sum_quads(0, g, FEAT)
                if g == PLAN_AT:
                    plan_sums(1)

            pe.wait_ge(s_epi, 2)
            for q in range(QUADS + 1):
                if q < QUADS_IN:
                    c = q // 2
                    if q % 2 == 0:
                        pe.wait_ge(s_attr[c % 2], 16 * (c // 2 + 1))
                    if q >= 2:
                        pe.wait_ge(s_s, q - 1)
                    pe.matmul(bank(5 + q % 2, QUAD * P, FEAT), w1T[:, :],
                              attr[:, c % 2, (q % 2) * QUAD * P:(q % 2 + 1) * QUAD * P],
                              start=True, stop=True).then_inc(s_sp, 1)
                r = q - 1
                if 0 <= r < QUADS_IN:
                    pe.wait_ge(s_s, r + 1)
                    if r >= 2:
                        pe.wait_ge(s_rec, r - 1)
                    for j in range(QUAD):
                        mm = pe.matmul(bank(7 if r % 2 else 4, FEAT, at=j * FEAT), sT[:, r % 2, j * P:(j + 1) * P],
                                       w2T[:, :], start=True, stop=True)
                    mm.then_inc(s_gp, 1)
                    degree(r)
                if q < QUADS:
                    transpose_logits(2 * MAX_EARLY + q, q % 2, 1 if q == 0 else 2)
            for b in range(SLOTS):
                pe.wait_ge(s_diag, b + 1)
                if b >= 2:
                    pe.wait_ge(s_bcc, b - 1)
                pe.matmul(bank(5 + b % 2, P), ones[:, :], W[:, b % 2, 0, 0:P], start=True, stop=True).then_inc(s_bc, 1)

            pe.wait_ge(s_dinv, 1)
            pe.wait_ge(s_rec, QUADS_IN)
            zero_acc()
            for g in range(GROUPS):
                sum_quads(1, g, FEAT + 1)
            for k in (2, 3):
                pe.wait_ge(s_epi, k + 1)
                zero_acc()
                for g in range(GROUPS):
                    sum_group(k, g, FEAT, lambda gg, j: ring[:, gg % RING, j, 0:FEAT], W_g, 2)
            pe.wait_ge(s_epi, 5)
            zero_acc()
            for g in range(-1, GROUPS + 1):
                n = g + 1
                if n < GROUPS:
                    pe.wait_ge(s_oh, n + 1)
                    if n >= 1:
                        pe.wait_ge(s_ohT, 2 * n)
                    for j in range(GROUP):
                        mm = pe.transpose(bank(5 + j // 4, P, at=(j % 4) * P), W3[:, n % 4, j, :], ident[:, :])
                        if j % 4 == 3:
                            mm.then_inc(s_ohp, 1)
                if 0 <= g < GROUPS:
                    eregs = offsets(PE_ONLY, AT_SRC, g * GROUP, GROUP)
                    pe.wait_ge(s_ohT, 2 * g + 2)
                    if g >= 1:
                        pe.wait_ge(s_prod, g)
                    for j in range(GROUP):
                        mm = pe.matmul(bank(7, EMB, at=j * EMB), oh_T[:, g % 2, j, :],
                                       emb_of[:, bass.ds(eregs[j], EMB)], start=True, stop=True)
                    mm.then_inc(s_ei, 1)
                if g >= 1:
                    sum_group(4, g - 1, FEAT + 1, lambda gg, j: msg[:, gg % 2, j, 0:FEAT + 1], W3, 4)

        @block.scalar
        def _(act):
            act.wait_ge(s_const, n_const[0])
            act.wait_ge(s_set, 4)
            for c in range(CHUNKS):
                act.wait_ge(s_h1p, c + 1)
                if c >= 1:
                    act.wait_ge(s_h2p, CHUNK * c)
                for i in range(2):
                    act.activation(h1[:, 2 * i:2 * i + 2, :],
                                   bank(5 + i, 2 * CHUNK * P, 2 * FEAT).rearrange("p (q n) -> p q n", q=2),
                                   ACT.Relu, bias=rb1[:, 0:1]).then_inc(s_h1, 1)
            served = [0]

            def serve():
                name, ap = REQ[served[0]]
                ap = ap[:, :, :] if name == "exp" else ap
                served[0] += 1
                act.wait_ge(s_sq, served[0])
                act.activation(ap, ap, ACT.Exp if name == "exp" else ACT.Sqrt, bias=zeros_c[:, 0:1]).then_inc(s_sr, 1)

            def masked_logits(q):
                act.wait_ge(s_mask, q + 1)
                if q >= 2:
                    act.wait_ge(s_mT, 2 * (q - 1))
                for j in range(QUAD):
                    t = q * QUAD + j
                    a = act.activation(ex[:, q % 2, j, :], hot[:, q % 2, j, :], ACT.Identity,
                                       bias=meta_b[:, t, M_NORM:M_NORM + 1])
                a.then_inc(s_mval, 1)

            for q in range(COS_AT):
                masked_logits(q)
            act.wait_ge(s_cosarg, 1)
            act.activation(cw, cw, ACT.Sin, bias=halfpi[:, 0:1], scale=-float(np.pi) / CUTOFF).then_inc(s_cos, 1)
            for q in range(COS_AT, MAX_EARLY):
                masked_logits(q)
            serve()
            for q in range(QUADS):
                if q < QUADS_IN:
                    act.wait_ge(s_sp, q + 1)
                    if q >= 2:
                        act.wait_ge(s_gp, q - 1)
                    act.activation(sT[:, q % 2, :], bank(5 + q % 2, QUAD * P, FEAT), ACT.Silu,
                                   bias=b1c[:, 0:1]).then_inc(s_s, 1)
                    if q >= RECS:
                        act.wait_ge(s_sc[q % RECS], 16 * QUAD * (q // RECS))
                    ts = slice(q * QUAD, (q + 1) * QUAD)
                    act.activation(rec[:, q % RECS, :, R_CW:R_LO + 1].rearrange("p j w -> p w j"),
                                   until_sorted[:, :].rearrange("p (w t) -> p w t", w=2)[:, :, ts], ACT.Copy)
                    act.activation(rec_i[:, q % RECS, :, R_DST], dst_i[:, ts], ACT.Copy).then_inc(s_small, 1)
                if q % 2 == 0:
                    masked_logits(MAX_EARLY + q // 2)
            act.wait_ge(s_maxd, 1)
            for b in range(SLOTS):
                if b >= 2:
                    act.wait_ge(s_bc, b - 1)
                act.activation(W[:, b % 2, 0, 0:P], ident[:, :], ACT.Copy, scale=seg_max[:, b:b + 1]).then_inc(s_diag, 1)
            serve()
            act.wait_ge(s_bcc, SLOTS)
            for g in range(GROUPS):
                regs = offsets(ACT_ONLY, AT_BUCKET, g * GROUP, GROUP)
                for i in range(2):
                    q = 2 * g + i
                    if q >= 2:
                        act.wait_ge(s_w, 2 * GROUPS + q - 1)
                    for j in range(QUAD):
                        t = q * QUAD + j
                        a = act.activation(ex[:, i, j, :], big[:, bass.ds(regs[i * QUAD + j] * P, SPAN * P)], ACT.Exp,
                                           scale=-1.0, bias=meta_b[:, t, M_NORM:M_NORM + 1])
                    a.then_inc(s_ex, 1)
            serve()
            serve()
            serve()
            for g in range(GROUPS):
                for i in range(2):
                    act.wait_ge(s_ohp, 2 * g + i + 1)
                    act.activation(oh_T[:, g % 2, 4 * i:4 * i + 4, :],
                                   bank(5 + i).rearrange("p (j n) -> p j n", j=4), ACT.Copy).then_inc(s_ohT, 1)
            serve()
            serve()

        @block.vector
        def _(dve):
            chain = [0]

            def link(ins):
                chain[0] += 1
                ins.then_inc(s_dve, 1)
                dve.wait_ge(s_dve, chain[0])

            dve.memset(rw2[:, :, :], 0.0).then_inc(s_set, 1)
            dve.memset(ones[:, :], 1.0).then_inc(s_set, 1)
            dve.memset(zeros_b[:, :], 0.0)
            dve.memset(halfpi[:, :], float(np.pi) / 2)
            dve.memset(zeros_c[:, :], 0.0).then_inc(s_set, 1)
            dve.wait_ge(s_const, n_const[0])
            dve.tensor_copy(iota_b[:, :], iota[:, :]).then_inc(s_set, 1)
            dve.wait_ge(s_set, 4)
            dve.wait_ge(s_embp, 2)
            dve.tensor_copy(emb_rows[:, 0:EMB], bank(7, EMB, at=64))
            dve.tensor_copy(emb_rows[:, EMB:2 * EMB], bank(7, EMB)).then_inc(s_embs, 1)
            dve.wait_ge(s_edges, 80)

            meta_b_i = meta_b[:, :, :].bitcast(I32)
            real = slice(0, TILES_IN)
            link(dve.memset(meta_b[:, TILES_IN:TILES, :], 0.0))
            link(dve.memset(meta_b[:, TILES_IN:TILES, M_LO], -1.0))
            link(dve.scalar_tensor_tensor(meta_b_i[:, real, M_IDX], src_i, float(RELS), count_i, ALU.mult, ALU.add))
            link(dve.tensor_copy(meta_b[:, real, M_NORM], scratch))
            link(dve.tensor_scalar(scratch_i, dst_i[:, :], P.bit_length() - 1, None, ALU.logical_shift_right))
            dve.tensor_copy(count, scratch_i).then_inc(s_b0in, 1)
            link(dve.tensor_copy(meta_b_i[:, real, M_SRC], src_i))
            dve.wait_ge(s_b0, 1)
            for i in range(4):
                ts = slice(i * ICH, (i + 1) * ICH)
                dve.tensor_copy(bt[:, ts], bank(i, ICH))
                last = dve.scalar_tensor_tensor(meta_b[:, ts, M_LO], bank(i, ICH), -float(P), dst_i[:, ts],
                                                ALU.mult, ALU.add)
            link(last)
            link(dve.memset(bt[:, TILES_IN:TILES], float(N_BUCKETS - 1)))

            def columns(row, after, link):
                link(dve.tensor_scalar(bt_i, bt, float(after), 205.0, ALU.add, ALU.mult))
                link(dve.tensor_scalar(bt_i, bt_i, 11, None, ALU.logical_shift_right))
                link(dve.tensor_copy(tens, bt_i))
                link(dve.tensor_scalar(tens, tens, float(BANK - PER_BANK * ACC_W), float(after * ACC_W),
                                       ALU.mult, ALU.add))
                r = slice(row, row + 1)
                link(dve.scalar_tensor_tensor(at_table[r, :], bt[r, :], float(ACC_W), tens[r, :], ALU.mult, ALU.add))

            def dst_columns(link):
                columns(AT_DST, 0, link)
                columns(AT_NEXT, 1, link)
                r = slice(AT_BUCKET, AT_BUCKET + 1)
                link(dve.tensor_copy(at_table[r, :], bt[r, :]))

            link(dve.tensor_reduce(small[:, 6, 0:1], meta_b[:, real, M_LO], AX_X, ALU.max))
            link(dve.tensor_reduce(small[:, 6, 1:2], meta_b[:, real, M_LO], AX_X, ALU.min))
            link(dve.tensor_scalar(small[:, 6, 0:1], small[:, 6, 0:1], float(SPAN * P), None, ALU.is_ge))
            link(dve.tensor_scalar(small[:, 6, 1:2], small[:, 6, 1:2], 0.0, None, ALU.is_lt))
            dve.tensor_tensor(small[:, 6, 0:1], small[:, 6, 0:1], small[:, 6, 1:2], ALU.add).then_inc(s_flagin, 1)

            for n in range(SLOTS):
                if n == 1:
                    dst_columns(link)
                dve.wait_ge(s_h2p, n + 1)
                if n >= 2:
                    dve.wait_ge(s_h2w[n % 2], 16 * (n // 2))
                dve.tensor_copy(h2[:, n % 2, :], bank(7 if n % 2 else 4, RELS * FEAT)).then_inc(s_h2, 1)
            dve.wait_ge(s_flagp, 1)
            dve.tensor_scalar(flag[:, :], bank(3, 1), 0.5, None, ALU.is_gt).then_inc(s_flag, 1)

            def split(key, lo_out, link):
                link(dve.tensor_scalar(scratch_i, key, P.bit_length() - 1, None, ALU.logical_shift_right))
                yield
                link(dve.tensor_copy(bucket[:, :], scratch_i))
                yield
                link(dve.tensor_scalar(scratch_i, key, P - 1, None, ALU.bitwise_and))
                yield
                link(dve.tensor_copy(lo_out, scratch_i))
                yield

            def totals(o, link):
                for b in range(N_BUCKETS):
                    link(dve.tensor_scalar(hit[:, b % 2, :], bucket[:, :], float(b), 0.0, ALU.is_equal, ALU.add,
                                           accum_out=small[:, 0, b:b + 1]))
                    yield
                dve.tensor_copy(small[:, 1, 0:N_BUCKETS], small[:, 0, 0:N_BUCKETS]).then_inc(s_tot[o], 1)

            def tables(o, link):
                nt = small[:, 1, 0:N_BUCKETS]
                start = small[:, 2, 0:N_BUCKETS]
                nt_i = small_i[:, 0:N_BUCKETS]
                dve.wait_ge(s_tot[o], 1)
                dve.wait_ge(s_pre[o], 1)
                link(dve.tensor_scalar(nt_i, bank(5, N_BUCKETS, at=64), float(P - 1), None, ALU.add))
                link(dve.tensor_scalar(nt_i, nt_i, P.bit_length() - 1, None, ALU.logical_shift_right))
                link(dve.tensor_copy(nt, nt_i))
                link(dve.tensor_tensor_scan(start, nt, nt, 0.0, ALU.add, ALU.max))
                link(dve.tensor_tensor(start, start, nt, ALU.subtract))
                link(dve.scalar_tensor_tensor(start, start, float(P), bank(5, N_BUCKETS), ALU.mult, ALU.add))
                one = small_i[0:N_BUCKETS, 0:1]
                link(dve.tensor_scalar(one, bank(5, 1, N_BUCKETS, at=128), float(P - 1), None, ALU.add))
                link(dve.tensor_scalar(one, one, P.bit_length() - 1, None, ALU.logical_shift_right))
                dve.tensor_copy(small[0:N_BUCKETS, 4, 0:1], one).then_inc(s_nt[o], 1)
                dve.wait_ge(s_end[o], 1)
                link(dve.tensor_copy(small[0:N_BUCKETS, 5, 0:1], bank(5, 1, N_BUCKETS, at=130)))
                for i in range(4):
                    ts = slice(i * TCH, (i + 1) * TCH)
                    dve.tensor_scalar(started[:, ts], tile_no[:, ts], small[0:N_BUCKETS, 5, 0:1], None,
                                      ALU.is_ge).then_inc(s_cmp[o], 1)
                    dve.wait_ge(s_bt[o], i + 1)
                    link(dve.tensor_scalar(bt[:, ts], bank(6, TCH), float(N_BUCKETS - 1), None, ALU.min))
                if o == 0:
                    dst_columns(link)
                else:
                    columns(AT_SRC, 0, link)

            def ranks(o, rows, link):
                for b in range(N_BUCKETS):
                    link(dve.tensor_scalar(hit[:, b % 2, :], bucket[:, :], float(b), None, ALU.is_equal))
                    yield
                    link(dve.tensor_tensor_scan(count, hit[:, b % 2, :], hit[:, b % 2, :], small[:, 2, b:b + 1],
                                                ALU.add, ALU.max))
                    yield
                    link(dve.copy_predicated(scratch, hit[:, b % 2, :], count))
                    yield
                link(dve.tensor_scalar(rows, scratch, -1.0, None, ALU.add))
                yield
                link(dve.tensor_scalar(count_i, rows, P - 1, 3, ALU.bitwise_and, ALU.logical_shift_left))
                yield
                link(dve.tensor_scalar(scratch_i, rows, 7, GROUP - 1, ALU.logical_shift_right, ALU.bitwise_and))
                yield
                link(dve.tensor_tensor(count_i, count_i, scratch_i, ALU.bitwise_or))
                yield
                link(dve.tensor_scalar(scratch_i, rows, 10, 10, ALU.logical_shift_right, ALU.logical_shift_left))
                yield
                dve.tensor_tensor(rows, scratch_i, count_i, ALU.bitwise_or).then_inc(s_plan[o], 1)
                dve.wait_ge(s_plan[o], 1)

            def cutoff(link):
                link(dve.tensor_scalar(hit[:, 0, :], cw, CUTOFF, None, ALU.is_lt))
                yield
                link(dve.tensor_scalar(cw, cw, CUTOFF, None, ALU.min))
                yield
                link(dve.tensor_scalar(count, cw, 1.0 / (2 * CUTOFF), None, ALU.mult))
                yield
                link(dve.tensor_copy(scratch_i, count))
                yield
                link(dve.tensor_copy(count, scratch_i))
                yield
                link(dve.scalar_tensor_tensor(cw, count, -2 * CUTOFF, cw, ALU.mult, ALU.add))
                yield
                link(dve.tensor_scalar(count, cw, -1.0, None, ALU.mult))
                yield
                link(dve.tensor_tensor(cw, cw, count, ALU.max))
                yield
                link(dve.tensor_scalar(count, cw, -1.0, 2 * CUTOFF, ALU.mult, ALU.add))
                yield
                dve.tensor_tensor(cw, cw, count, ALU.min).then_inc(s_cosarg, 1)
                yield
                dve.wait_ge(s_cos, 1)
                link(dve.tensor_scalar(cw, cw, 0.5, 0.5, ALU.mult, ALU.add))
                yield
                link(dve.tensor_tensor(cw, cw, hit[:, 0, :], ALU.mult))
                yield

            dve.wait_ge(s_flag, 1)
            with dve.If(dve.value_load(flag[0:1, 0:1], min_val=0, max_val=1)):
                inner = [0]

                def inner_link(ins):
                    inner[0] += 1
                    ins.then_inc(s_branch, 1)
                    dve.wait_ge(s_branch, inner[0])

                for _ in split(dst_i[:, :], meta_b[:, real, M_LO], inner_link):
                    pass
                for _ in totals(0, inner_link):
                    pass
                tables(0, inner_link)
                for _ in ranks(0, row_dst[:, :], inner_link):
                    pass

            ask = [0]

            def asked():
                ask[0] += 1
                dve.wait_ge(s_sr, ask[0])

            def bc(ap):
                return ap[:, :, None].to_broadcast([P, SLOTS, FEAT])

            def layernorm(out, last=None):
                v = V[:, :, :]
                mean = small[:, 3, :]
                link(dve.tensor_reduce(mean, v, AX_X, ALU.add))
                link(dve.tensor_scalar(mean, mean, 1.0 / FEAT, None, ALU.mult))
                link(dve.tensor_tensor(v, v, bc(mean), ALU.subtract))
                link(dve.tensor_tensor(Q[:, :, :], v, v, ALU.mult))
                link(dve.tensor_reduce(mean, Q[:, :, :], AX_X, ALU.add))
                dve.tensor_scalar(mean, mean, 1.0 / FEAT, LN_EPS, ALU.mult, ALU.add).then_inc(s_sq, 1)
                asked()
                link(dve.reciprocal(mean, mean))
                link(dve.tensor_tensor(out, v, bc(mean), ALU.mult))

            def acc_rows(width):
                return acc[:, :, :, 0:width]

            def banks(ap):
                return ap[:, :, :].rearrange("p (k s) w -> p k s w", k=ACC_BANKS)

            def weights(k):
                for g in range(GROUPS):
                    gg = k * GROUPS + g
                    dve.wait_ge(s_used, 2 * (gg - 1))
                    for j in range(GROUP):
                        last = dve.tensor_scalar(W_g[:, gg % 2, j, :], iota[:, 0:P],
                                                 meta_a[:, g * GROUP + j, R_LO - FEAT:R_LO - FEAT + 1], None,
                                                 ALU.is_equal)
                    last.then_inc(s_w, 2)

            dve.wait_ge(s_order, 1)
            dve.tensor_copy(red[:, 0, 0:1, 0], zeros_c[:, 0:1]).then_inc(s_epi, 1)
            early = [split(src_i, lo_src, link), cutoff(link), totals(1, link)]
            late = [ranks(1, row_src[:, :], link)]

            def steps(queue, n):
                while queue and n > 0:
                    try:
                        next(queue[0])
                        n -= 1
                    except StopIteration:
                        queue.pop(0)

            def mask(q):
                if q >= 2:
                    dve.wait_ge(s_mval, q - 1)
                for j in range(QUAD):
                    last = dve.tensor_scalar(hot[:, q % 2, j, :], iota_b[:, :],
                                             meta_b[:, q * QUAD + j, M_LO:M_LO + 1], NEG, ALU.not_equal, ALU.mult)
                last.then_inc(s_mask, 1)

            regs_of = {}

            def take_maxima(h, bank_no):
                q, u = h // 2, h % 2
                if u == 0:
                    regs_of[0] = offsets(DVE_ONLY, AT_BUCKET, q * QUAD, QUAD)
                dve.wait_ge(s_mT, h + 1)
                dve.tensor_reduce(red[:, h % 2, 0:2, :], bank(bank_no).rearrange("p (j h n) -> p j h n", j=2, h=SPAN),
                                  AX_X, ALU.max).then_inc(s_red, 1)
                dve.wait_ge(s_red, h + 1)
                for j in range(2):
                    at = seg_run[:, bass.ds(regs_of[0][2 * u + j], SPAN)]
                    link(dve.tensor_tensor(at, at, red[:, h % 2, j, :], ALU.max))

            link(dve.memset(seg_run[:, :], NEG))
            mask(0)
            for g in range(GROUPS):
                for i in range(2):
                    q = 2 * g + i
                    if q >= 2:
                        dve.wait_ge(s_used, q - 1)
                    for j in range(QUAD):
                        t = q * QUAD + j
                        last = dve.tensor_scalar(W[:, i, j, :], iota[:, :], meta_b[:, t, M_LO:M_LO + 1],
                                                 meta_b[:, t, M_NORM:M_NORM + 1], ALU.is_equal, ALU.mult)
                    last.then_inc(s_w, 1)
                    if i == 0:
                        mask(g + 1)
                    if q >= 1:
                        take_maxima(q - 1, 7)
                if g < PLAN_AT:
                    steps(early, 4 if g == 0 else 1)
                elif g == PLAN_AT:
                    steps(early, 1000)
                    tables(1, link)
                else:
                    steps(late, 2 if g % 4 == 0 else 1)
            steps(late, 1000)
            take_maxima(2 * GROUPS - 1, 7)
            dve.wait_ge(s_used, 2 * GROUPS)
            dve.wait_ge(s_node, 48)
            for k in range(ACC_BANKS):
                last = dve.tensor_tensor(banks(V)[:, k], acc[:, k, :, 0:FEAT],
                                         rb2[:, None, :].to_broadcast([P, PER_BANK, FEAT]), ALU.add)
            last.then_inc(s_epi, 1)
            dve.wait_ge(s_epi, 2)
            link(dve.scalar_tensor_tensor(V[:, :, :], V[:, :, :], 0.0, X[:, :, :], ALU.max, ALU.add))
            layernorm(X[:, :, :])
            dve.tensor_copy(red[:, 0, 0:1, 0], zeros_c[:, 0:1]).then_inc(s_tab, 1)

            dve.memset(ring[:, :, :, FEAT], 1.0)
            link(dve.memset(rec[:, :, :, REC - 1], 0.0))
            for q in range(QUADS + 2):
                if q % 2 == 0 and MAX_EARLY + q // 2 + 1 < QUADS:
                    mask(MAX_EARLY + q // 2 + 1)
                if q < QUADS_IN:
                    if q >= 2:
                        dve.wait_ge(s_deg, q - 1)
                    for j in range(QUAD):
                        t = q * QUAD + j
                        dve.tensor_scalar(hot_lo[:, q % 2, j, :], iota_b[:, 0:P], lo_src[:, t:t + 1], None, ALU.is_equal)
                    dve.tensor_tensor(hi_hot[:, q % 2, :, :],
                                      bucket[:, q * QUAD:(q + 1) * QUAD][:, :, None].to_broadcast([P, QUAD, SLOTS]),
                                      iota_b[:, None, 0:SLOTS].to_broadcast([P, QUAD, SLOTS]),
                                      ALU.is_equal).then_inc(s_degh, 1)
                r = q - 2
                if 0 <= r < QUADS_IN:
                    dve.wait_ge(s_gp, r + 1)
                    dve.wait_ge(s_small, r + 1)
                    dve.tensor_tensor(rec[:, r % RECS, :, 0:FEAT],
                                      bank(7 if r % 2 else 4, QUAD * FEAT).rearrange("p (j w) -> p j w", j=QUAD),
                                      b2r[:, None, :].to_broadcast([P, QUAD, FEAT]), ALU.add).then_inc(s_rec, 1)
                if 0 <= q - 1 < QUADS:
                    take_maxima(2 * MAX_EARLY + q - 1, (q - 1) % 2)
            link(dve.tensor_scalar(small[:, 6, :], seg_run[:, :], NEG / 2, None, ALU.is_gt))
            dve.tensor_tensor(seg_max[:, :], seg_run[:, :], small[:, 6, :], ALU.mult).then_inc(s_maxd, 1)
            for b in range(SLOTS):
                dve.wait_ge(s_bc, b + 1)
                dve.tensor_copy(big[:, b * P:(b + 1) * P], bank(5 + b % 2, P)).then_inc(s_bcc, 1)
            dve.wait_ge(s_deg, QUADS_IN)
            dve.tensor_scalar(small[:, 7, :], bank(2, SLOTS), 1.0, None, ALU.add).then_inc(s_sq, 1)
            asked()
            dve.reciprocal(dinv[:, :], small[:, 7, :]).then_inc(s_dinv, 1)
            for q in range(QUADS):
                qq = QUADS + q
                dve.wait_ge(s_used, qq - 1)
                for j in range(QUAD):
                    last = dve.tensor_scalar(hot[:, q % 2, j, :], iota_b[:, :],
                                             meta_b[:, q * QUAD + j, M_LO:M_LO + 1], None, ALU.is_equal)
                link(last)
                dve.wait_ge(s_ex, q + 1)
                dve.scalar_tensor_tensor(W[:, q % 2, :, :], ex[:, q % 2, :, :], 1.0, hot[:, q % 2, :, :],
                                         ALU.min, ALU.mult).then_inc(s_w, 1)
            dve.wait_ge(s_used, 4 * GROUPS)
            link(dve.tensor_scalar(small[:, 5, :].rearrange("p (k s) -> p k s", k=ACC_BANKS), acc[:, :, :, FEAT],
                                   1e-30, None, ALU.max))
            link(dve.reciprocal(small[:, 5, :], small[:, 5, :]))
            for k in range(ACC_BANKS):
                inv = small[:, 5, k * PER_BANK:(k + 1) * PER_BANK]
                last = dve.tensor_tensor(banks(V)[:, k], acc[:, k, :, 0:FEAT],
                                         inv[:, :, None].to_broadcast([P, PER_BANK, FEAT]), ALU.mult)
            last.then_inc(s_epi, 1)
            dve.wait_ge(s_epi, 3)
            dve.tensor_scalar(Q[:, :, :], V[:, :, :], 0.0, None, ALU.min).then_inc(s_sq, 1)
            asked()
            link(dve.tensor_scalar(V[:, :, :], V[:, :, :], 0.0, -1.0, ALU.max, ALU.add))
            link(dve.tensor_tensor(V[:, :, :], V[:, :, :], Q[:, :, :], ALU.add))
            link(dve.tensor_tensor(V[:, :, :], V[:, :, :], X[:, :, :], ALU.add))
            layernorm(X[:, :, :])
            dve.tensor_tensor(V[:, :, :], X[:, :, :], bc(dinv[:, :]), ALU.mult).then_inc(s_tab, 1)
            dve.wait_ge(s_m2, 16 * GROUP)
            for k in (2, 3):
                weights(k)
                dve.wait_ge(s_used, 2 * (k + 1) * GROUPS)
                dve.wait_ge(s_tabw, 16 * k)
                dve.wait_ge(s_tab, k)
                for i in range(ACC_BANKS):
                    last = dve.tensor_tensor(banks(V)[:, i], acc[:, i, :, 0:FEAT], banks(V)[:, i], ALU.add)
                last.then_inc(s_epi, 1)
                dve.wait_ge(s_epi, k + 2)
                link(dve.tensor_tensor(V[:, :, :], V[:, :, :], bc(dinv[:, :]), ALU.mult))
                if k == 2:
                    dve.tensor_tensor(V[:, :, :], V[:, :, :], bc(dinv[:, :]), ALU.mult).then_inc(s_tab, 1)
            link(dve.tensor_tensor(V[:, :, :], V[:, :, :], X[:, :, :], ALU.add))
            layernorm(X[:, :, :])
            dve.wait_ge(s_embg, 16 * SLOTS)
            for k in range(ACC_BANKS):
                last = dve.tensor_copy(emb_of_v[:, k, :, 0:EMB], embs[:, k * PER_BANK:(k + 1) * PER_BANK, 0:EMB])
            link(last)
            dve.tensor_copy(embs[:, :, EMB - 1], node_mj[:, :]).then_inc(s_tab, 1)
            def one_hots(g):
                gg = 4 * GROUPS + g
                dve.wait_ge(s_recl[g % 3], 16 * (g // 3 + 1))
                dve.wait_ge(s_used, 2 * (gg - 3))
                for j in range(GROUP):
                    last = dve.tensor_scalar(W3[:, gg % 4, j, :], iota[:, 0:P], rec_in[:, g % 3, j, R_LO:R_LO + 1], None,
                                             ALU.is_equal)
                last.then_inc(s_oh, 1)

            one_hots(0)
            one_hots(1)
            for g in range(GROUPS):
                gg = 4 * GROUPS + g
                if g + 2 < GROUPS:
                    one_hots(g + 2)
                else:
                    dve.wait_ge(s_used, 2 * (gg - 1))
                dve.wait_ge(s_gat[gg % RING], 16 * GROUP * (gg // RING + 1))
                rows = ring[:, gg % RING, :, :]
                rin = rec_in[:, g % 3, :, :]
                wgt = wgt_2[:, g % 2, :]
                dve.wait_ge(s_ei, g + 1)
                dve.tensor_tensor(wgt, rin[:, :, R_CW], rows[:, :, X3_MJ], ALU.mult)
                dve.tensor_copy(msg[:, gg % 2, :, FEAT], rows[:, :, X3_MJ])
                dve.tensor_tensor(prod, bank(7, GROUP * EMB).rearrange("p (j w) -> p j w", j=GROUP),
                                  rows[:, :, X3_EMB:X3_W], ALU.mult).then_inc(s_prod, 1)
                dve.wait_ge(s_prod, g + 1)
                link(dve.tensor_reduce(adapt, prod, AX_X, ALU.add))
                m = msg[:, gg % 2, :, 0:FEAT]
                full = [P, GROUP, FEAT]
                dve.tensor_tensor(m, rin[:, :, 0:FEAT], adapt[:, :, None].to_broadcast(full), ALU.add) \
                    .then_inc(s_eir, 1)
                dve.wait_ge(s_eir, g + 1)
                link(dve.tensor_tensor(m, m, rows[:, :, 0:FEAT], ALU.mult))
                dve.tensor_tensor(m, m, wgt[:, :, None].to_broadcast(full), ALU.mult).then_inc(s_w, 2)
            dve.wait_ge(s_used, 10 * GROUPS)
            link(dve.tensor_scalar(small[:, 5, :].rearrange("p (k s) -> p k s", k=ACC_BANKS), acc[:, :, :, FEAT],
                                   1e-8, None, ALU.max))
            link(dve.reciprocal(small[:, 5, :], small[:, 5, :]))
            for k in range(ACC_BANKS):
                inv = small[:, 5, k * PER_BANK:(k + 1) * PER_BANK]
                last = dve.tensor_tensor(banks(V)[:, k], acc[:, k, :, 0:FEAT],
                                         inv[:, :, None].to_broadcast([P, PER_BANK, FEAT]), ALU.mult)
            link(last)
            link(dve.tensor_tensor(V[:, :, :], V[:, :, :], X[:, :, :], ALU.add))
            layernorm(V[:, :, :])
            row = [P, SLOTS, FEAT]
            link(dve.tensor_tensor(V[:, :, :], V[:, :, :], gamma[:, None, :].to_broadcast(row), ALU.mult))
            link(dve.tensor_tensor(V[:, :, :], V[:, :, :], beta[:, None, :].to_broadcast(row), ALU.add))
            link(dve.tensor_tensor(V[:, :, :], V[:, :, :], X[:, :, :], ALU.add))
            layernorm(X[:, :, :])
            dve.tensor_copy(red[:, 0, 0:1, 0], zeros_c[:, 0:1]).then_inc(s_tab, 1)


def kernel(**inputs):
    import concourse.bacc as bacc
    from concourse.bass_utils import run_bass_kernel_spmd

    a = {k: np.asarray(v) for k, v in inputs.items()}

    def edges(v, fill):
        v = np.concatenate([v.reshape(-1), np.full(TILES_IN * P - N_EDGES, fill, v.dtype)])
        return np.ascontiguousarray(v.reshape(TILES_IN, P).T)

    def nodes(v):
        v = v.reshape(N_NODES, -1)
        v = np.concatenate([v, np.zeros((NODES - N_NODES, v.shape[1]), v.dtype)])
        return v

    def by_place(v):
        v = nodes(v)
        return np.ascontiguousarray(v.reshape(SLOTS, P, v.shape[1]).transpose(1, 0, 2))

    f = np.float32
    default = np.zeros((P, GROUP * REC), f)
    default_rec = default.copy().reshape(P, GROUP, REC)
    default_rec[:, :, R_LO] = -1.0
    i = np.arange(P)
    attrT = np.zeros((ATTR, TILES_IN * P), f)
    attrT[:, :N_EDGES] = a["edge_attr_40"].T
    embT = np.zeros((EMB, P), f)
    embT[:, :a["L3_gnn_emb"].shape[0]] = a["L3_gnn_emb"].T
    arrays = {
        "src": edges(a["src"], PAD_NODE), "dst": edges(a["dst"], PAD_NODE),
        "etype": edges(a["edge_type_8"], 0), "norm": edges(a["edge_weight1"], 0), "dist": edges(a["edge_weight"], 0),
        "attrT": attrT,
        "x": by_place(a["x"]), "xT": np.ascontiguousarray(nodes(a["x"]).T),
        "node_z": by_place(a["node_type_119"])[:, :, 0], "node_mj": by_place(a["node_vec"])[:, :, 0],
        "weight1": a["L0_gnn_weight1"], "weight2": a["L0_gnn_weight2"],
        "bias1": a["L0_gnn_bias1"], "bias2": a["L0_gnn_bias2"],
        "W1T": np.ascontiguousarray(a["L3_gnn_W1"].T), "W2T": np.ascontiguousarray(a["L3_gnn_W2"].T),
        "b1": a["L3_gnn_b1"], "b2": a["L3_gnn_b2"], "embT": embT,
        "adaptT": np.ascontiguousarray(a["L3_gnn_adaptW"].T),
        "gamma": a["L3_gnn_gamma"], "beta": a["L3_gnn_beta"],
        "const": np.stack([np.eye(P, dtype=f), (i[:, None] < i[None, :]).astype(f),
                           (i[:, None] <= i[None, :]).astype(f)]
                          + [np.tile((h * P + i).astype(f), (P, 1)) for h in range(SPAN)]
                          + [np.tile((i == 0).astype(f)[:, None], (1, P))]),
        "tile_no": np.tile(np.arange(TILES, dtype=f), (N_BUCKETS, 1)),
        "default": default_rec.reshape(P, GROUP * REC),
        "default_meta": np.tile(np.array([-1, 0, 0, 0], f), (P, GROUP)),
    }
    arrays = {k: np.ascontiguousarray(v) for k, v in arrays.items()}
    nc = bacc.Bacc("TRN2", target_bir_lowering=False, num_devices=1)
    A = {k: nc.dram_tensor(f"in_{k}", v.shape, mybir.dt.from_np(v.dtype), kind="ExternalInput").ap()
         for k, v in arrays.items()}
    A["out"] = nc.dram_tensor("out_x", (N_NODES, FEAT), F32, kind="ExternalOutput").ap()
    build(nc, A)
    r = run_bass_kernel_spmd(nc, [{f"in_{k}": v for k, v in arrays.items()}], core_ids=[0])
    return r.results[0]["out_x"]
```

```python
from contextlib import ExitStack

import numpy as np
import concourse.bass as bass
from concourse import mybir

F32 = mybir.dt.float32
BF16 = mybir.dt.bfloat16
I32 = mybir.dt.int32
I16 = mybir.dt.int16
U16 = mybir.dt.uint16
ALU = mybir.AluOpType
ACT = mybir.ActivationFunctionType
AX_X = mybir.AxisListType.X
PE_ONLY = (mybir.EngineType.PE,)
DVE_ONLY = (mybir.EngineType.DVE,)
ACT_ONLY = (mybir.EngineType.Activation,)

P = 128
N_NODES, FEAT, N_EDGES = 6250, 48, 206250
RELS, ATTR, EMB = 8, 40, 32
N_BUCKETS = -(-N_NODES // P)
SLOTS = N_BUCKETS + 1
NODES = SLOTS * P
PAD_NODE = N_BUCKETS * P - 1
assert PAD_NODE >= N_NODES
TILES_IN = -(-N_EDGES // P)
GROUP = 8
GROUPS = -(-(TILES_IN + N_BUCKETS) // GROUP)
TILES = GROUPS * GROUP
QUAD = 4
QUADS_IN = TILES_IN // QUAD
QUADS = TILES // QUAD
assert QUADS_IN * QUAD == TILES_IN
BANK = 512
ACC_W = 50
PER_BANK = BANK // ACC_W
ACC_BANKS = SLOTS // PER_BANK
assert ACC_BANKS * PER_BANK == SLOTS
REC = 52
R_CW, R_LO, R_DST = FEAT, FEAT + 1, FEAT + 2
META = 4
M_LO, M_IDX, M_SRC, M_NORM = range(META)
X3_MJ, X3_EMB = FEAT, FEAT + 1
X3_W = FEAT + 1 + EMB
RING = 4
RECS = 8
NEAR = 3
SPAN = 2
CHUNK = 2
CHUNKS = SLOTS // CHUNK
PAIRS = RELS // 2
CUTOFF, LN_EPS = 6.0, 1e-5
NEG = -float(2.0 ** 126)
TCH = TILES // 4
ICH = TILES_IN // 4
AT_DST, AT_SRC, AT_NEXT, AT_BUCKET = 0, 32, 64, 96
AT_NEAR = AT_BUCKET


def build(nc, A):
    with ExitStack() as ctx:
        def sb(name, shape, dt=F32):
            return ctx.enter_context(nc.sbuf_tensor(name, shape, dt))

        def sem(name):
            return ctx.enter_context(nc.semaphore(name))

        def dram(name, shape, dt=F32):
            return nc.dram_tensor(name, shape, dt, kind="Internal").ap()

        h2_table = dram("h2_table", (NODES * RELS, FEAT))
        x1_table = dram("x1_table", (NODES, FEAT))
        y_table = [dram("y0_table", (NODES, FEAT)), dram("y1_table", (NODES, FEAT))]
        x3_table = dram("x3_table", (NODES, X3_W))
        emb_table = dram("emb_table", (P, 2 * EMB))
        by_dst = dram("by_dst", (TILES * P, META))
        by_src = dram("by_src", (TILES * P, REC))

        ident = sb("ident", [P, P])
        before = sb("before", [P, P])
        upto = sb("upto", [P, P])
        iota = sb("iota", [P, SPAN * P])
        iota_b = sb("iota_b", [P, SPAN * P], BF16)
        iota_s = sb("iota_s", [P, NEAR * P], I16)
        before_b = sb("before_b", [P, P], BF16)
        from_b = sb("from_b", [P, P], BF16)
        ones = sb("ones", [P, P])
        zeros_b = sb("zeros_b", [P, BANK], BF16)
        default = sb("default", [P, GROUP * REC])
        default_meta = sb("default_meta", [P, GROUP * META])
        first = sb("first", [P, P])
        w1T = sb("w1T", [ATTR, FEAT])
        w2T = sb("w2T", [FEAT, FEAT])
        b1c = sb("b1c", [FEAT, 1])
        b2r = sb("b2r", [P, FEAT])
        embT = sb("embT", [EMB, P])
        adaptT = sb("adaptT", [EMB, EMB])
        emb_rows = sb("emb_rows", [P, 2 * EMB])
        rw1 = sb("rw1", [FEAT, PAIRS, 2 * FEAT])
        rw2 = sb("rw2", [2 * FEAT, PAIRS, 2 * FEAT])
        rb1 = sb("rb1", [2 * FEAT, 1])
        rb2 = sb("rb2", [P, FEAT])
        seg_run = sb("seg_run", [P, SLOTS])
        order_mark = sb("order_mark", [P, 1])
        gamma = sb("gamma", [P, FEAT])
        beta = sb("beta", [P, FEAT])
        zeros_c = sb("zeros_c", [P, 1])
        halfpi = sb("halfpi", [P, 1])

        big = sb("big", [P, 4 * TILES_IN])
        src_i = big[:, 0:TILES_IN].bitcast(I32)
        dst_i = sb("dst_i", [P, TILES_IN], I32)
        until_sorted = sb("until_sorted", [P, 2 * TILES_IN])
        cw = until_sorted[:, 0:TILES_IN]
        lo_src = until_sorted[:, TILES_IN:2 * TILES_IN]
        embs = until_sorted[:, 0:SLOTS * 2 * EMB].rearrange("p (b w) -> p b w", w=2 * EMB)
        row_dst = sb("row_dst", [P, TILES_IN], I32)
        row_src = sb("row_src", [P, TILES_IN], I32)
        bucket = sb("bucket", [P, TILES_IN], BF16)
        hit = big[:, TILES_IN:2 * TILES_IN].bitcast(BF16).rearrange("p (s t) -> p s t", s=2)
        count = big[:, 2 * TILES_IN:3 * TILES_IN]
        scratch = big[:, 3 * TILES_IN:4 * TILES_IN]
        assert 4 * TILES_IN >= SLOTS * P
        scratch_i = scratch.bitcast(I32)
        count_i = count.bitcast(I32)
        meta_a = sb("meta_a", [P, TILES, META])
        meta_b = sb("meta_b", [P, TILES, META])
        small = sb("small", [P, 8, SLOTS])
        small_i = sb("small_i", [P, SLOTS], I32)
        at_table = sb("at_table", [P, TILES], I32)
        far = sb("far", [P, 2], I32)
        flag = sb("flag", [P, 1], I32)

        X = sb("X", [P, SLOTS, FEAT])
        V = sb("V", [P, SLOTS, FEAT])
        Q = sb("Q", [P, SLOTS, FEAT])
        node_z = sb("node_z", [P, SLOTS], I32)
        node_mj = sb("node_mj", [P, SLOTS])
        tile_no = X[0:N_BUCKETS, :, :].rearrange("p b w -> p (b w)")[:, 0:TILES]
        dinv = sb("dinv", [P, SLOTS])
        seg_max = sb("seg_max", [P, SLOTS])

        ring = sb("ring", [P, RING, GROUP, X3_W])
        ex = sb("ex", [P, 2, QUAD, SPAN * P])
        ring_f = ring[:, :, :, :].rearrange("p r j w -> p (r j w)")
        xT = ring_f[0:FEAT, 0:2 * CHUNK * P].rearrange("p (s n) -> p s n", s=2)
        h2 = ring_f[:, 512:512 + 4 * RELS * FEAT].rearrange("p (s n) -> p s n", s=4)
        W = sb("W", [P, 2, QUAD, SPAN * P])
        h1 = W[0:2 * FEAT, :, :, :].rearrange("p s j n -> p (s j n)") \
            .rearrange("p (s q n) -> p s q n", s=2, q=PAIRS)
        W_g = W[:, :, :, :].rearrange("p s j (h n) -> p s (j h) n", n=P)
        hot = row_dst[:, 0:QUAD * SPAN * P].bitcast(BF16).rearrange("p (s j n) -> p s j n", s=2, j=QUAD)
        hot_lo = sb("hot_lo", [P, 2, QUAD, P], BF16)
        free = meta_a[:, :, :].rearrange("p t w -> p (t w)")
        attr = free[0:ATTR, 0:4 * QUAD * P].rearrange("p (s n) -> p s n", s=2)
        sT = free[0:FEAT, 2048:2048 + 2 * QUAD * P].rearrange("p (s n) -> p s n", s=2)
        rec = free[:, 3072:3072 + RECS * QUAD * REC].rearrange("p (s j w) -> p s j w", s=RECS, j=QUAD)
        rec_i = rec.bitcast(I32)
        vf = V[:, :, :].rearrange("p b w -> p (b w)")
        qf = Q[:, :, :].rearrange("p b w -> p (b w)")
        started = free[0:N_BUCKETS, 0:TILES]
        bt = free[:, TILES:2 * TILES]
        tens = free[:, 2 * TILES:3 * TILES]
        bt_i = free[:, 3 * TILES:4 * TILES].bitcast(I32)
        red = sb("red", [P, 2, QUAD, SPAN])
        hi_hot = sb("hi_hot", [P, 2, QUAD, SLOTS], BF16)

        ps = ctx.enter_context(nc.psum_tensor("ps", [P, 8 * BANK], F32))

        def bank(i, n=BANK, parts=P, at=0):
            return ps[0:parts, i * BANK + at:i * BANK + at + n]

        acc = ps[:, 0:ACC_BANKS * BANK].rearrange("p (k c) -> p k c", c=BANK)[:, :, 0:PER_BANK * ACC_W] \
            .rearrange("p k (s w) -> p k s w", w=ACC_W)

        s_const = sem("s_const")
        s_edges = sem("s_edges")
        s_node = sem("s_node")
        s_set = sem("s_set")
        s_xT = [sem(f"s_xT{i}") for i in range(2)]
        s_h1p = sem("s_h1p")
        s_h1 = sem("s_h1")
        s_h2p = sem("s_h2p")
        s_h2 = sem("s_h2")
        s_h2w = [sem(f"s_h2w{i}") for i in range(4)]
        s_embp = sem("s_embp")
        s_embs = sem("s_embs")
        s_embw = sem("s_embw")
        s_embg = sem("s_embg")
        s_init = sem("s_init")
        s_dve = sem("s_dve")
        s_cosarg = sem("s_cosarg")
        s_cos = sem("s_cos")
        s_b0in, s_b0, s_flagin, s_flagp, s_flag = [sem(n) for n in ("s_b0in", "s_b0", "s_flagin", "s_flagp", "s_flag")]
        s_tot = [sem(f"s_tot{o}") for o in range(2)]
        s_pre = [sem(f"s_pre{o}") for o in range(2)]
        s_nt = [sem(f"s_nt{o}") for o in range(2)]
        s_end = [sem(f"s_end{o}") for o in range(2)]
        s_cmp = [sem(f"s_cmp{o}") for o in range(2)]
        s_bt = [sem(f"s_bt{o}") for o in range(2)]
        s_plan = [sem(f"s_plan{o}") for o in range(2)]
        s_hit = [sem(f"s_hit{o}") for o in range(2)]
        s_step = [sem(f"s_step{o}") for o in range(2)]
        s_scan = [sem(f"s_scan{o}") for o in range(2)]
        s_near1, s_near2, s_nearf, s_nearp, s_flag2 = [sem(n) for n in ("s_near1", "s_near2", "s_nearf", "s_nearp", "s_flag2")]
        s_gat_b = [sem(f"s_gat_b{i}") for i in range(RING)]
        s_used_b, s_w_b = sem("s_used_b"), sem("s_w_b")
        s_foh = sem("s_foh")
        s_fm = sem("s_fm")
        s_fa, s_fd = sem("s_fa"), sem("s_fd")
        s_fu = sem("s_fu")
        s_branch = sem("s_branch")
        s_order = sem("s_order")
        s_init1 = sem("s_init1")
        s_s1 = sem("s_s1")
        s_m1 = sem("s_m1")
        s_m2 = sem("s_m2")
        s_gat = [sem(f"s_gat{i}") for i in range(RING)]
        s_w = sem("s_w")
        s_used = sem("s_used")
        s_zero = sem("s_zero")
        s_epi = sem("s_epi")
        s_tab = sem("s_tab")
        s_tabw = sem("s_tabw")
        s_attr = [sem(f"s_attr{i}") for i in range(2)]
        s_sp = sem("s_sp")
        s_s = sem("s_s")
        s_gp = sem("s_gp")
        s_small = sem("s_small")
        s_rec = sem("s_rec")
        s_sc = [sem(f"s_sc{i}") for i in range(RECS)]
        s_degh = sem("s_degh")
        s_deg = sem("s_deg")
        s_mask = sem("s_mask")
        s_mval = sem("s_mval")
        s_mT = sem("s_mT")
        s_red = sem("s_red")
        s_maxd = sem("s_maxd")
        s_diag = sem("s_diag")
        s_bc = sem("s_bc")
        s_bcc = sem("s_bcc")
        s_ex = sem("s_ex")
        s_sq = sem("s_sq")
        s_sr = sem("s_sr")
        s_recl = [sem(f"s_recl{i}") for i in range(3)]
        s_dinv = sem("s_dinv")
        s_prod = sem("s_prod")
        s_oh = sem("s_oh")
        s_ohp = sem("s_ohp")
        s_ohT = sem("s_ohT")
        s_ei = sem("s_ei")
        s_eir = sem("s_eir")
        s_out = sem("s_out")

        block = ctx.enter_context(nc.Block())

        n_const = [0]
        asks = []

        PLAN_AT = GROUPS // 3
        PIECES = 4 * N_BUCKETS
        COUNT_AT = [PLAN_AT + 1 + c * (GROUPS - PLAN_AT - 3) // PIECES for c in range(PIECES)]
        NEAR_AT = 60

        def by_dve(t):
            return t % 4 == 3

        def taken(tt):
            return (s_fd, tt // 4 + 1) if by_dve(tt) else (s_fa, tt - tt // 4 + 1)

        def flow(k):
            if k in (2, 3):
                return s_gat_b, s_used_b, s_w_b, (k - 2) * GROUPS
            return s_gat, s_used, s_w, (2 if k == 4 else k) * GROUPS

        def counted_at(g):
            return [c for c in range(PIECES) if COUNT_AT[c] == g]

        assert max(COUNT_AT) < GROUPS
        COS_AT = 12
        MAX_EARLY = GROUPS
        assert QUADS - MAX_EARLY == QUADS // 2

        H1_BANKS = ((5, 6), (2, 3))
        by_dst_v = by_dst.rearrange("(g p j) w -> p g (j w)", p=P, j=GROUP)
        by_src_v = by_src.rearrange("(g p j) w -> p g j w", p=P, j=GROUP)

        def table_v(t):
            return t.rearrange("(b p) w -> p b w", p=P)

        oh_T = ex[:, :, :, :].rearrange("p s j (h n) -> p s (j h) n", n=P)
        meta_f = meta_b[:, :, :].rearrange("p t w -> p (t w)")
        W3 = meta_f[:, 0:4 * GROUP * P].rearrange("p (s j n) -> p s j n", s=4, j=GROUP)
        near_d = meta_f[:, 0:4 * NEAR * P].bitcast(BF16).rearrange("p (s n) -> p s n", s=8)
        near_s = meta_f[:, 1536:1536 + 4 * P].bitcast(BF16).rearrange("p (s n) -> p s n", s=8)
        near_m = meta_f[:, 2048:2048 + 4 * NEAR * P].rearrange("p (s n) -> p s n", s=4)
        rec_in = meta_f[:, 4096:4096 + 3 * GROUP * REC].rearrange("p (s j w) -> p s j w", s=3, j=GROUP)
        msg = big[:, 1024:1024 + 2 * GROUP * ACC_W].rearrange("p (s j w) -> p s j w", s=2, j=GROUP)
        prod = big[:, 2048:2048 + GROUP * EMB].rearrange("p (j w) -> p j w", j=GROUP)
        adapt = big[:, 2304:2304 + GROUP]
        wgt_2 = big[:, 2320:2320 + 2 * GROUP].rearrange("p (s j) -> p s j", s=2)
        emb_of = big[:, 2560:2560 + ACC_BANKS * BANK]
        emb_of_v = emb_of.rearrange("p (k c) -> p k c", c=BANK)[:, :, 0:PER_BANK * ACC_W] \
            .rearrange("p k (s w) -> p k s w", w=ACC_W)

        REQ = [("sqrt", small[:, 3, :]), ("sqrt", small[:, 7, :]), ("exp", Q), ("sqrt", small[:, 3, :]),
               ("sqrt", small[:, 3, :]), ("sqrt", small[:, 3, :]), ("sqrt", small[:, 3, :])]

        @block.sync
        def _(sp):
            def const(dst, src):
                sp.dma_start(dst, src).then_inc(s_const, 16)
                n_const[0] += 16

            sp.dma_start(dst_i[:, :], A["dst"]).then_inc(s_edges, 16)
            sp.dma_start(count_i, A["etype"]).then_inc(s_edges, 16)
            sp.dma_start(src_i, A["src"]).then_inc(s_edges, 16)
            sp.dma_start(scratch, A["norm"]).then_inc(s_edges, 16)
            sp.dma_start(cw, A["dist"]).then_inc(s_edges, 16)
            const(ident[:, :], A["const"][0])
            const(before[:, :], A["const"][1])
            const(upto[:, :], A["const"][2])
            for h in range(SPAN):
                const(iota[:, h * P:(h + 1) * P], A["const"][3 + h])
            const(first[:, :], A["const"][3 + SPAN])
            const(tile_no, A["tile_no"])
            const(default[:, :], A["default"])
            const(default_meta[:, :], A["default_meta"])
            const(w1T[:, :], A["W1T"])
            const(w2T[:, :], A["W2T"])
            const(b1c[:, :], A["b1"].rearrange("(a b) -> a b", b=1))
            const(b2r[:, :], A["b2"].rearrange("(a b) -> a b", a=1).to_broadcast([P, FEAT]))
            const(embT[:, :], A["embT"])
            const(adaptT[:, :], A["adaptT"])
            for q in range(PAIRS):
                for r in range(2):
                    const(rw1[:, q, r * FEAT:(r + 1) * FEAT], A["weight1"][2 * q + r])
            for r in range(2):
                const(rb1[r * FEAT:(r + 1) * FEAT, :], A["bias1"].rearrange("(a b) -> a b", b=1))
            const(rb2[:, :], A["bias2"].rearrange("(a b) -> a b", a=1).to_broadcast([P, FEAT]))
            const(gamma[:, :], A["gamma"].rearrange("(a b) -> a b", a=1).to_broadcast([P, FEAT]))
            const(beta[:, :], A["beta"].rearrange("(a b) -> a b", a=1).to_broadcast([P, FEAT]))
            sp.wait_ge(s_set, 1)
            for q in range(PAIRS):
                for r in range(2):
                    const(rw2[r * FEAT:(r + 1) * FEAT, q, r * FEAT:(r + 1) * FEAT], A["weight2"][2 * q + r])
            sp.dma_start(node_z[:, :], A["node_z"]).then_inc(s_node, 16)
            sp.dma_start(node_mj[:, :], A["node_mj"]).then_inc(s_node, 16)
            for c in range(CHUNKS):
                if c >= 2:
                    sp.wait_ge(s_h1p, c - 1)
                sp.dma_start(xT[:, c % 2, :], A["xT"][:, c * CHUNK * P:(c + 1) * CHUNK * P]) \
                    .then_inc(s_xT[c % 2], 16)
                if c >= 1:
                    for n in range((c - 1) * CHUNK, c * CHUNK):
                        sp.wait_ge(s_h2, n + 1)
                        sp.dma_start(h2_table[n * P * RELS:(n + 1) * P * RELS, :].rearrange("(p r) w -> p (r w)", r=RELS),
                                     h2[:, n % 4, :]).then_inc(s_h2w[n % 4], 16)
            for n in range((CHUNKS - 1) * CHUNK, SLOTS):
                sp.wait_ge(s_h2, n + 1)
                sp.dma_start(h2_table[n * P * RELS:(n + 1) * P * RELS, :].rearrange("(p r) w -> p (r w)", r=RELS),
                             h2[:, n % 4, :]).then_inc(s_h2w[n % 4], 16)
            sp.wait_ge(s_embs, 1)
            sp.dma_start(emb_table, emb_rows[:, :]).then_inc(s_embw, 16)
            dv = by_src.rearrange("(g p j) w -> p g (j w)", p=P, j=GROUP)
            sp.dma_start(dv, default[:, None, :].to_broadcast([P, GROUPS, GROUP * REC])).then_inc(s_init, 16)
            sp.wait_ge(s_plan[1], 1)
            sp.dma_start(X[:, :, :], A["x"]).then_inc(s_node, 16)
            for c in range(-(-QUADS_IN // 2)):
                n = min(2, QUADS_IN - 2 * c)
                if c >= 2:
                    sp.wait_ge(s_sp, 2 * (c - 1))
                sp.dma_start(attr[:, c % 2, 0:n * QUAD * P], A["attrT"][:, 2 * c * QUAD * P:(2 * c + n) * QUAD * P]) \
                    .then_inc(s_attr[c % 2], 16)
            sp.wait_ge(s_tab, 1)
            sp.dma_start(table_v(x1_table), X[:, :, :]).then_inc(s_tabw, 16)
            for i in range(RECS):
                sp.wait_ge(s_sc[i], 16 * QUAD * len(range(i, QUADS_IN, RECS)))
            for j in range(GROUP):
                sp.dma_start(meta_a[:, :, :].rearrange("p (g j) w -> p g j w", j=GROUP)[:, :, j, :],
                             by_src_v[:, :, j, FEAT:REC]).then_inc(s_m2, 16)
            for i in range(2):
                sp.wait_ge(s_tab, 2 + i)
                sp.dma_start(table_v(y_table[i]), V[:, :, :]).then_inc(s_tabw, 16)
            sp.wait_ge(s_tab, 4)
            sp.dma_start(table_v(x3_table)[:, :, 0:FEAT], X[:, :, :]).then_inc(s_tabw, 16)
            sp.dma_start(table_v(x3_table)[:, :, FEAT:X3_W], embs[:, :, EMB - 1:2 * EMB]).then_inc(s_tabw, 16)
            for g in range(GROUPS):
                if g >= 3:
                    sp.wait_ge(s_eir, g - 2)
                sp.dma_start(rec_in[:, g % 3, :, :], by_src_v[:, g, :, :]).then_inc(s_recl[g % 3], 16)
            sp.wait_ge(s_tab, 5)
            full = N_NODES // P
            sp.dma_start(A["out"][0:full * P, :].rearrange("(b p) w -> p b w", p=P), X[:, 0:full, :]).then_inc(s_out, 16)
            sp.dma_start(A["out"][full * P:N_NODES, :], X[0:N_NODES - full * P, full, :]).then_inc(s_out, 16)
            sp.wait_ge(s_out, 32)

        @block.gpsimd
        def _(pool):
            meta_b_i = meta_b[:, :, :].bitcast(I32)
            meta_a_i = meta_a[:, :, :].bitcast(I32)
            pool.wait_ge(s_flag, 1)
            halves = (slice(0, GROUPS // 2), slice(GROUPS // 2, GROUPS))
            with pool.If(pool.value_load(flag[0:1, 0:1], min_val=0, max_val=1)):
                for h in halves:
                    pool.dma_start(by_dst_v[:, h, :], default_meta[:, None, :].to_broadcast([P, GROUPS // 2, GROUP * META])) \
                        .then_inc(s_init1, 16)
                pool.wait_ge(s_plan[0], 1)
                pool.wait_ge(s_init1, 32)
                for t in range(TILES_IN):
                    pool.indirect_dma_start(by_dst, bass.IndirectOffsetOnAxis(ap=row_dst[:, t:t + 1], axis=0),
                                            meta_b[:, t, :], None).then_inc(s_s1, 16)
                pool.wait_ge(s_s1, 16 * TILES_IN)
                for h in halves:
                    pool.dma_start(meta_b[:, :, :].rearrange("p (g j) w -> p g (j w)", j=GROUP)[:, h, :],
                                   by_dst_v[:, h, :]).then_inc(s_m1, 16)
                pool.wait_ge(s_m1, 32)
            pool.memset(order_mark[:, :], 0.0).then_inc(s_order, 1)

            def gather(k, table, width, index):
                s_gat, s_used, _, first = flow(k)
                for g in range(GROUPS):
                    gg = first + g
                    if gg >= RING:
                        pool.wait_ge(s_used, 2 * (gg - RING + 1))
                    for j in range(GROUP):
                        pool.indirect_dma_start(ring[:, gg % RING, j, 0:width], None, table,
                                                bass.IndirectOffsetOnAxis(ap=index(g * GROUP + j), axis=0)) \
                            .then_inc(s_gat[gg % RING], 16)

            for i in range(4):
                pool.wait_ge(s_h2w[i], 16 * len(range(i, SLOTS, 4)))
            gather(0, h2_table, FEAT, lambda t: meta_b_i[:, t, M_IDX:M_IDX + 1])
            pool.wait_ge(s_plan[1], 1)
            pool.wait_ge(s_init, 16)
            for q in range(QUADS_IN):
                pool.wait_ge(s_rec, q + 1)
                for j in range(QUAD):
                    t = q * QUAD + j
                    pool.indirect_dma_start(by_src, bass.IndirectOffsetOnAxis(ap=row_src[:, t:t + 1], axis=0),
                                            rec[:, q % RECS, j, :], None).then_inc(s_sc[q % RECS], 16)
            pool.wait_ge(s_embw, 16)
            pool.wait_ge(s_node, 48)
            pool.wait_ge(s_small, QUADS_IN)
            pool.wait_ge(s_degh, QUADS_IN)
            for b in range(SLOTS):
                pool.indirect_dma_start(embs[:, b, :], None, emb_table,
                                        bass.IndirectOffsetOnAxis(ap=node_z[:, b:b + 1], axis=0)).then_inc(s_embg, 16)
            pool.wait_ge(s_tabw, 16)
            gather(1, x1_table, FEAT, lambda t: meta_b_i[:, t, M_SRC:M_SRC + 1])
            pool.wait_ge(s_m2, 16 * GROUP)
            by_s = lambda t: meta_a_i[:, t, R_DST - FEAT:R_DST - FEAT + 1]
            pool.wait_ge(s_flag2, 1)
            with pool.If(pool.value_load(far[0:1, 0:1], min_val=0, max_val=1)):
                pool.wait_ge(s_tabw, 32)
                gather(2, y_table[0], FEAT, by_s)
                pool.wait_ge(s_tabw, 48)
                gather(3, y_table[1], FEAT, by_s)
            pool.wait_ge(s_tabw, 80)
            gather(4, x3_table, X3_W, by_s)

        def offsets(engines, row, t0, n):
            top = (SLOTS - NEAR) * FEAT if row == AT_NEAR and engines == PE_ONLY else N_BUCKETS - 1 if row == AT_BUCKET else (ACC_BANKS - 1) * BANK + (PER_BANK - 1) * ACC_W
            return nc.values_load_multi_w_load_instructions(
                at_table[row:row + 1, t0:t0 + n], engines=engines, min_val=0, max_val=top,
                skip_runtime_bounds_check_because="made from bucket numbers that are clamped")[1]

        @block.tensor
        def _(pe):
            pe.wait_ge(s_const, n_const[0])
            pe.wait_ge(s_set, 4)
            pe.matmul(bank(7, EMB), embT[:, :], adaptT[:, :], start=True, stop=True).then_inc(s_embp, 1)
            pe.transpose(bank(7, EMB, at=64), embT[:, :], ident[0:EMB, 0:EMB]).then_inc(s_embp, 1)
            pe.wait_ge(s_b0in, 1)
            for i in range(4):
                mm = pe.matmul(bank(i, ICH), first[:, :], count[:, i * ICH:(i + 1) * ICH], start=True, stop=True)
            mm.then_inc(s_b0, 1)

            def relation_in(c):
                pe.wait_ge(s_xT[c % 2], 16 * (c // 2 + 1))
                if c == 1:
                    pe.wait_ge(s_flagin, 1)
                    pe.matmul(bank(4, 1), ones[:, :], small[:, 6, 0:1], start=True, stop=True).then_inc(s_flagp, 1)
                if c >= 2:
                    pe.wait_ge(s_h1, 2 * (c - 1))
                for q in range(PAIRS):
                    mm = pe.matmul(bank(H1_BANKS[c % 2][q // 2], CHUNK * P, 2 * FEAT, (q % 2) * CHUNK * P), rw1[:, q, :],
                                   xT[:, c % 2, :], start=True, stop=True)
                mm.then_inc(s_h1p, 1)

            def relation_out(c):
                pe.wait_ge(s_h1, 2 * (c + 1))
                for i in range(CHUNK):
                    n = c * CHUNK + i
                    if n == 0:
                        pe.wait_ge(s_embs, 1)
                        pe.wait_ge(s_flag, 1)
                    if n >= 2:
                        pe.wait_ge(s_h2, n - 1)
                    for q in range(PAIRS):
                        mm = pe.matmul(bank(7 if n % 2 else 4, 2 * FEAT, P, q * 2 * FEAT),
                                       h1[:, c % 2, q, i * P:(i + 1) * P], rw2[:, q, :], start=True, stop=True)
                    mm.then_inc(s_h2p, 1)

            relation_in(0)
            for c in range(CHUNKS):
                if c + 1 < CHUNKS:
                    relation_in(c + 1)
                relation_out(c)
            def plan_sums(o):
                pe.wait_ge(s_tot[o], 1)
                tot = small[:, 0, 0:N_BUCKETS]
                pe.matmul(bank(5, N_BUCKETS, at=64), ones[:, :], tot, start=True, stop=True)
                pe.matmul(bank(5, 1, N_BUCKETS, at=128), tot, ones[:, 0:1], start=True, stop=True).then_inc(s_pre[o], 1)
                pe.wait_ge(s_nt[o], 1)
                pe.matmul(bank(5, 1, N_BUCKETS, at=130), upto[0:N_BUCKETS, 0:N_BUCKETS], small[0:N_BUCKETS, 4, 0:1],
                          start=True, stop=True).then_inc(s_end[o], 1)
                for i in range(4):
                    pe.wait_ge(s_cmp[o], i + 1)
                    pe.matmul(bank(6, TCH), ones[0:N_BUCKETS, :], started[:, i * TCH:(i + 1) * TCH],
                              start=True, stop=True).then_inc(s_bt[o], 1)

            def count_steps(o, c):
                b, i = divmod(c, 4)
                pe.wait_ge(s_hit[o], b + 1)
                if c >= 2:
                    pe.wait_ge(s_scan[o], c - 1)
                t0, skip = i * ICH, 1 if i == 0 else 0
                pe.matmul(bank(5 + i % 2, ICH), before_b[:, :], hit[:, b % 2, t0:t0 + ICH], start=True, stop=False)
                pe.matmul(bank(5 + i % 2, ICH - skip, at=skip), from_b[:, :],
                          hit[:, b % 2, t0 - 1 + skip:t0 - 1 + ICH], start=False, stop=True).then_inc(s_step[o], 1)

            pe.wait_ge(s_flag, 1)
            with pe.If(pe.value_load(flag[0:1, 0:1], min_val=0, max_val=1)):
                plan_sums(0)
                for c in range(PIECES):
                    count_steps(0, c)
            pe.wait_ge(s_order, 1)

            def zero_acc():
                for i in range(ACC_BANKS):
                    pe.matmul(bank(i, BANK), zeros_b[:, 0:P], zeros_b[:, :], start=True, stop=False,
                              skip_group_check=True)

            def transpose_logits(h, bank_no, lag):
                q, u = h // 2, h % 2
                pe.wait_ge(s_mval, q + 1)
                if h >= lag:
                    pe.wait_ge(s_red, h - lag + 1)
                for j in range(2):
                    for n in range(SPAN):
                        mm = pe.transpose(bank(bank_no, P, at=(2 * j + n) * P),
                                          ex[:, q % 2, 2 * u + j, n * P:(n + 1) * P], ident[:, :])
                mm.then_inc(s_mT, 1)

            def sum_quads(k, g, width):
                gg = k * GROUPS + g
                here = offsets(PE_ONLY, AT_DST, g * GROUP, GROUP)
                after = offsets(PE_ONLY, AT_NEXT, g * GROUP, GROUP)
                pe.wait_ge(s_gat[gg % RING], 16 * GROUP * (gg // RING + 1))
                for i in range(2):
                    if k == 0:
                        transpose_logits(2 * g + i, 7, 1)
                    pe.wait_ge(s_w, 2 * gg + i + 1)
                    for j in range(QUAD):
                        t = i * QUAD + j
                        for h, regs in enumerate((here, after)):
                            mm = pe.matmul(ps[:, bass.ds(regs[t], width)], W[:, i, j, h * P:(h + 1) * P],
                                           ring[:, gg % RING, t, 0:width], start=False, stop=False,
                                           skip_group_check=True)
                    mm.then_inc(s_used, 1)

            def sum_group(k, g, width, rhs, weights, slots):
                s_gat, s_used, s_w, first = flow(k)
                gg = first + g
                regs = offsets(PE_ONLY, AT_SRC, g * GROUP, GROUP)
                pe.wait_ge(s_gat[gg % RING], 16 * GROUP * (gg // RING + 1))
                pe.wait_ge(s_w, 2 * gg + 2)
                for j in range(GROUP):
                    mm = pe.matmul(ps[:, bass.ds(regs[j], width)], weights[:, gg % slots, j, :], rhs(gg, j),
                                   start=False, stop=False, skip_group_check=True)
                mm.then_inc(s_used, 2)

            def degree(q):
                pe.wait_ge(s_degh, q + 1)
                for j in range(QUAD):
                    mm = pe.matmul(bank(2, SLOTS), hot_lo[:, q % 2, j, :], hi_hot[:, q % 2, j, :],
                                   start=(q == 0 and j == 0), stop=(q == QUADS_IN - 1 and j == QUAD - 1))
                mm.then_inc(s_deg, 1)

            pe.wait_ge(s_epi, 1)
            zero_acc()
            for g in range(GROUPS):
                for c in counted_at(g):
                    count_steps(1, c)
                sum_quads(0, g, FEAT)
                if g == PLAN_AT:
                    plan_sums(1)

            pe.wait_ge(s_epi, 2)
            def hidden(q):
                c = q // 2
                if q % 2 == 0:
                    pe.wait_ge(s_attr[c % 2], 16 * (c // 2 + 1))
                if q >= 2:
                    pe.wait_ge(s_s, q - 1)
                pe.matmul(bank(5 + q % 2, QUAD * P, FEAT), w1T[:, :],
                          attr[:, c % 2, (q % 2) * QUAD * P:(q % 2 + 1) * QUAD * P],
                          start=True, stop=True).then_inc(s_sp, 1)

            hidden(0)
            for q in range(QUADS + 1):
                r = q - 1
                if 0 <= r < QUADS_IN:
                    pe.wait_ge(s_s, r + 1)
                    if r >= 2:
                        pe.wait_ge(s_rec, r - 1)
                    for j in range(QUAD):
                        mm = pe.matmul(bank(7 if r % 2 else 4, FEAT, at=j * FEAT), sT[:, r % 2, j * P:(j + 1) * P],
                                       w2T[:, :], start=True, stop=True)
                    mm.then_inc(s_gp, 1)
                    degree(r)
                if q + 1 < QUADS_IN:
                    hidden(q + 1)
                if q < QUADS:
                    transpose_logits(2 * MAX_EARLY + q, q % 2, 1 if q == 0 else 2)
            for b in range(SLOTS):
                pe.wait_ge(s_diag, b + 1)
                if b >= 2:
                    pe.wait_ge(s_bcc, b - 1)
                pe.matmul(bank(5 + b % 2, P), ones[:, :], W[:, b % 2, 0, 0:P], start=True, stop=True).then_inc(s_bc, 1)

            pe.wait_ge(s_dinv, 1)
            pe.wait_ge(s_rec, QUADS_IN)
            zero_acc()
            for g in range(GROUPS):
                sum_quads(1, g, FEAT + 1)
                if g == NEAR_AT:
                    for i in range(4):
                        pe.wait_ge(s_near1, i + 1)
                        pe.matmul(bank(5, TCH), first[:, :], qf[:, i * TCH:(i + 1) * TCH],
                                  start=True, stop=True).then_inc(s_near2, 1)
                    pe.wait_ge(s_nearf, 1)
                    pe.matmul(bank(5, 1), ones[:, :], small[:, 6, 0:1], start=True, stop=True).then_inc(s_nearp, 1)
            def near_pass(k):
                first = (k - 2) * TILES

                def matrix(t):
                    tt = first + t
                    pe.wait_ge(s_foh, tt + 1)
                    if tt >= 3:
                        pe.wait_ge(*taken(tt - 3))
                    for j in range(NEAR):
                        mm = pe.matmul(bank(5 + tt % 3, P, at=j * P), near_d[:, tt % 8, j * P:(j + 1) * P],
                                       near_s[:, tt % 8, :], start=True, stop=True)
                    mm.then_inc(s_fm, 1)

                for _ in range(24):
                    pe.matmul(bank(5, BANK), zeros_b[:, 0:P], zeros_b[:, :], start=True, stop=True)
                matrix(0)
                matrix(1)
                for t in range(TILES):
                    if t + 2 < TILES:
                        matrix(t + 2)
                    if t % GROUP == 0:
                        to = offsets(PE_ONLY, AT_SRC, t, GROUP)
                        rows = offsets(PE_ONLY, AT_NEAR, t, GROUP)
                    tt = first + t
                    pe.wait_ge(*taken(tt))
                    at = vf[:, bass.ds(rows[t % GROUP], NEAR * FEAT)]
                    for j in range(NEAR):
                        mm = pe.matmul(ps[:, bass.ds(to[t % GROUP], FEAT)], near_m[:, tt % 4, j * P:(j + 1) * P],
                                       at[:, j * FEAT:(j + 1) * FEAT], start=False, stop=False, skip_group_check=True)
                    mm.then_inc(s_fu, 1)

            for k in (2, 3):
                pe.wait_ge(s_epi, k + 1)
                pe.wait_ge(s_tab, k)
                zero_acc()
                with pe.If(pe.value_load(far[0:1, 0:1], min_val=0, max_val=1)):
                    for g in range(GROUPS):
                        sum_group(k, g, FEAT, lambda gg, j: ring[:, gg % RING, j, 0:FEAT], W_g, 2)
                with pe.If(pe.value_load(far[0:1, 1:2], min_val=0, max_val=1)):
                    near_pass(k)
            pe.wait_ge(s_epi, 5)
            zero_acc()
            for g in range(-1, GROUPS + 1):
                n = g + 1
                if n < GROUPS:
                    pe.wait_ge(s_oh, n + 1)
                    if n >= 1:
                        pe.wait_ge(s_ohT, 2 * n)
                    for j in range(GROUP):
                        mm = pe.transpose(bank(5 + j // 4, P, at=(j % 4) * P), W3[:, n % 4, j, :], ident[:, :])
                        if j % 4 == 3:
                            mm.then_inc(s_ohp, 1)
                if 0 <= g < GROUPS:
                    eregs = offsets(PE_ONLY, AT_SRC, g * GROUP, GROUP)
                    pe.wait_ge(s_ohT, 2 * g + 2)
                    if g >= 1:
                        pe.wait_ge(s_prod, g)
                    for j in range(GROUP):
                        mm = pe.matmul(bank(7, EMB, at=j * EMB), oh_T[:, g % 2, j, :],
                                       emb_of[:, bass.ds(eregs[j], EMB)], start=True, stop=True)
                    mm.then_inc(s_ei, 1)
                if g >= 1:
                    sum_group(4, g - 1, FEAT + 1, lambda gg, j: msg[:, gg % 2, j, 0:FEAT + 1], W3, 4)

        @block.scalar
        def _(act):
            act.wait_ge(s_const, n_const[0])
            act.wait_ge(s_set, 4)
            for c in range(CHUNKS):
                act.wait_ge(s_h1p, c + 1)
                if c >= 2:
                    act.wait_ge(s_h2p, CHUNK * (c - 1))
                for i in range(2):
                    act.activation(h1[:, c % 2, 2 * i:2 * i + 2, :],
                                   bank(H1_BANKS[c % 2][i], 2 * CHUNK * P, 2 * FEAT).rearrange("p (q n) -> p q n", q=2),
                                   ACT.Relu, bias=rb1[:, 0:1]).then_inc(s_h1, 1)
            served = [0]

            def serve():
                name, ap = REQ[served[0]]
                ap = ap[:, :, :] if name == "exp" else ap
                served[0] += 1
                act.wait_ge(s_sq, served[0])
                act.activation(ap, ap, ACT.Exp if name == "exp" else ACT.Sqrt, bias=zeros_c[:, 0:1]).then_inc(s_sr, 1)

            def masked_logits(q):
                act.wait_ge(s_mask, q + 1)
                if q >= 2:
                    act.wait_ge(s_mT, 2 * (q - 1))
                for j in range(QUAD):
                    t = q * QUAD + j
                    a = act.activation(ex[:, q % 2, j, :], hot[:, q % 2, j, :], ACT.Identity,
                                       bias=meta_b[:, t, M_NORM:M_NORM + 1])
                a.then_inc(s_mval, 1)

            for q in range(COS_AT):
                masked_logits(q)
            act.wait_ge(s_cosarg, 1)
            act.activation(cw, cw, ACT.Sin, bias=halfpi[:, 0:1], scale=-float(np.pi) / CUTOFF).then_inc(s_cos, 1)
            for q in range(COS_AT, MAX_EARLY):
                masked_logits(q)
            serve()
            for q in range(QUADS):
                if q < QUADS_IN:
                    act.wait_ge(s_sp, q + 1)
                    if q >= 2:
                        act.wait_ge(s_gp, q - 1)
                    act.activation(sT[:, q % 2, :], bank(5 + q % 2, QUAD * P, FEAT), ACT.Silu,
                                   bias=b1c[:, 0:1]).then_inc(s_s, 1)
                    if q >= RECS:
                        act.wait_ge(s_sc[q % RECS], 16 * QUAD * (q // RECS))
                    ts = slice(q * QUAD, (q + 1) * QUAD)
                    act.activation(rec[:, q % RECS, :, R_CW:R_LO + 1].rearrange("p j w -> p w j"),
                                   until_sorted[:, :].rearrange("p (w t) -> p w t", w=2)[:, :, ts], ACT.Copy)
                    act.activation(rec_i[:, q % RECS, :, R_DST], dst_i[:, ts], ACT.Copy).then_inc(s_small, 1)
                if q % 2 == 0:
                    masked_logits(MAX_EARLY + q // 2)
            act.wait_ge(s_maxd, 1)
            for b in range(SLOTS):
                if b >= 2:
                    act.wait_ge(s_bc, b - 1)
                act.activation(W[:, b % 2, 0, 0:P], ident[:, :], ACT.Copy, scale=seg_max[:, b:b + 1]).then_inc(s_diag, 1)
            serve()
            act.wait_ge(s_bcc, SLOTS)
            for g in range(GROUPS):
                regs = offsets(ACT_ONLY, AT_BUCKET, g * GROUP, GROUP)
                for i in range(2):
                    q = 2 * g + i
                    if q >= 2:
                        act.wait_ge(s_w, 2 * GROUPS + q - 1)
                    for j in range(QUAD):
                        t = q * QUAD + j
                        a = act.activation(ex[:, i, j, :], big[:, bass.ds(regs[i * QUAD + j] * P, SPAN * P)], ACT.Exp,
                                           scale=-1.0, bias=meta_b[:, t, M_NORM:M_NORM + 1])
                    a.then_inc(s_ex, 1)
            serve()
            serve()
            for k in (2, 3):
                act.wait_ge(s_flag2, 1)
                with act.If(act.value_load(far[0:1, 1:2], min_val=0, max_val=1)):
                    for t in range(TILES):
                        tt = (k - 2) * TILES + t
                        if by_dve(tt):
                            continue
                        act.wait_ge(s_fm, tt + 1)
                        if tt >= 4:
                            act.wait_ge(s_fu, tt - 3)
                        act.activation(near_m[:, tt % 4, :], bank(5 + tt % 3, NEAR * P), ACT.Copy).then_inc(s_fa, 1)
            serve()
            for g in range(GROUPS):
                for i in range(2):
                    act.wait_ge(s_ohp, 2 * g + i + 1)
                    act.activation(oh_T[:, g % 2, 4 * i:4 * i + 4, :],
                                   bank(5 + i).rearrange("p (j n) -> p j n", j=4), ACT.Copy).then_inc(s_ohT, 1)
            serve()
            serve()

        @block.vector
        def _(dve):
            chain = [0]

            def link(ins):
                chain[0] += 1
                ins.then_inc(s_dve, 1)
                dve.wait_ge(s_dve, chain[0])

            dve.memset(rw2[:, :, :], 0.0).then_inc(s_set, 1)
            dve.memset(ones[:, :], 1.0).then_inc(s_set, 1)
            dve.memset(zeros_b[:, :], 0.0)
            dve.memset(halfpi[:, :], float(np.pi) / 2)
            dve.memset(zeros_c[:, :], 0.0).then_inc(s_set, 1)
            dve.wait_ge(s_const, n_const[0])
            dve.tensor_copy(iota_s[:, 0:SPAN * P], iota[:, :])
            dve.tensor_scalar(iota_s[:, SPAN * P:NEAR * P], iota[:, 0:P], float(SPAN * P), None, ALU.add)
            dve.tensor_copy(before_b[:, :], before[:, :])
            dve.tensor_scalar(from_b[:, :], before[:, :], -1.0, 1.0, ALU.mult, ALU.add)
            dve.tensor_copy(iota_b[:, :], iota[:, :]).then_inc(s_set, 1)
            dve.wait_ge(s_set, 4)
            dve.wait_ge(s_embp, 2)
            dve.tensor_copy(emb_rows[:, 0:EMB], bank(7, EMB, at=64))
            dve.tensor_copy(emb_rows[:, EMB:2 * EMB], bank(7, EMB)).then_inc(s_embs, 1)
            dve.wait_ge(s_edges, 80)

            meta_b_i = meta_b[:, :, :].bitcast(I32)
            real = slice(0, TILES_IN)
            link(dve.memset(meta_b[:, TILES_IN:TILES, :], 0.0))
            link(dve.memset(meta_b[:, TILES_IN:TILES, M_LO], -1.0))
            link(dve.scalar_tensor_tensor(meta_b_i[:, real, M_IDX], src_i, float(RELS), count_i, ALU.mult, ALU.add))
            link(dve.tensor_copy(meta_b[:, real, M_NORM], scratch))
            link(dve.tensor_scalar(scratch_i, dst_i[:, :], P.bit_length() - 1, None, ALU.logical_shift_right))
            dve.tensor_copy(count, scratch_i).then_inc(s_b0in, 1)
            link(dve.tensor_copy(meta_b_i[:, real, M_SRC], src_i))
            dve.wait_ge(s_b0, 1)
            for i in range(4):
                ts = slice(i * ICH, (i + 1) * ICH)
                dve.tensor_copy(bt[:, ts], bank(i, ICH))
                last = dve.scalar_tensor_tensor(meta_b[:, ts, M_LO], bank(i, ICH), -float(P), dst_i[:, ts],
                                                ALU.mult, ALU.add)
            link(last)
            link(dve.memset(bt[:, TILES_IN:TILES], float(N_BUCKETS - 1)))

            def columns(row, after, link):
                link(dve.tensor_scalar(bt_i, bt, float(after), 205.0, ALU.add, ALU.mult))
                link(dve.tensor_scalar(bt_i, bt_i, 11, None, ALU.logical_shift_right))
                link(dve.tensor_copy(tens, bt_i))
                link(dve.tensor_scalar(tens, tens, float(BANK - PER_BANK * ACC_W), float(after * ACC_W),
                                       ALU.mult, ALU.add))
                r = slice(row, row + 1)
                link(dve.scalar_tensor_tensor(at_table[r, :], bt[r, :], float(ACC_W), tens[r, :], ALU.mult, ALU.add))

            def dst_columns(link):
                columns(AT_DST, 0, link)
                columns(AT_NEXT, 1, link)
                r = slice(AT_BUCKET, AT_BUCKET + 1)
                link(dve.tensor_copy(at_table[r, :], bt[r, :]))

            link(dve.tensor_reduce(small[:, 6, 0:1], meta_b[:, real, M_LO], AX_X, ALU.max))
            link(dve.tensor_reduce(small[:, 6, 1:2], meta_b[:, real, M_LO], AX_X, ALU.min))
            link(dve.tensor_scalar(small[:, 6, 0:1], small[:, 6, 0:1], float(SPAN * P), None, ALU.is_ge))
            link(dve.tensor_scalar(small[:, 6, 1:2], small[:, 6, 1:2], 0.0, None, ALU.is_lt))
            dve.tensor_tensor(small[:, 6, 0:1], small[:, 6, 0:1], small[:, 6, 1:2], ALU.add).then_inc(s_flagin, 1)

            for n in range(SLOTS):
                if n == 0:
                    dve.wait_ge(s_flagp, 1)
                    dve.tensor_scalar(flag[:, :], bank(4, 1), 0.5, None, ALU.is_gt).then_inc(s_flag, 1)
                if n == 1:
                    dst_columns(link)
                dve.wait_ge(s_h2p, n + 1)
                if n >= 4:
                    dve.wait_ge(s_h2w[n % 4], 16 * (n // 4))
                dve.tensor_copy(h2[:, n % 4, :], bank(7 if n % 2 else 4, RELS * FEAT)).then_inc(s_h2, 1)

            def split(key, lo_out, link):
                link(dve.tensor_scalar(scratch_i, key, P.bit_length() - 1, None, ALU.logical_shift_right))
                yield
                link(dve.tensor_copy(bucket[:, :], scratch_i))
                yield
                link(dve.tensor_scalar(scratch_i, key, P - 1, None, ALU.bitwise_and))
                yield
                link(dve.tensor_copy(lo_out, scratch_i))
                yield

            def totals(o, link):
                for b in range(N_BUCKETS):
                    link(dve.tensor_scalar(hit[:, b % 2, :], bucket[:, :], float(b), 0.0, ALU.is_equal, ALU.add,
                                           accum_out=small[:, 0, b:b + 1]))
                    yield
                dve.tensor_copy(small[:, 1, 0:N_BUCKETS], small[:, 0, 0:N_BUCKETS]).then_inc(s_tot[o], 1)

            def tables(o, link):
                nt = small[:, 1, 0:N_BUCKETS]
                start = small[:, 2, 0:N_BUCKETS]
                nt_i = small_i[:, 0:N_BUCKETS]
                dve.wait_ge(s_tot[o], 1)
                dve.wait_ge(s_pre[o], 1)
                link(dve.tensor_scalar(nt_i, bank(5, N_BUCKETS, at=64), float(P - 1), None, ALU.add))
                link(dve.tensor_scalar(nt_i, nt_i, P.bit_length() - 1, None, ALU.logical_shift_right))
                link(dve.tensor_copy(nt, nt_i))
                link(dve.tensor_tensor_scan(start, nt, nt, 0.0, ALU.add, ALU.max))
                link(dve.tensor_tensor(start, start, nt, ALU.subtract))
                link(dve.tensor_scalar(start, start, float(P), None, ALU.mult))
                one = small_i[0:N_BUCKETS, 0:1]
                link(dve.tensor_scalar(one, bank(5, 1, N_BUCKETS, at=128), float(P - 1), None, ALU.add))
                link(dve.tensor_scalar(one, one, P.bit_length() - 1, None, ALU.logical_shift_right))
                dve.tensor_copy(small[0:N_BUCKETS, 4, 0:1], one).then_inc(s_nt[o], 1)
                dve.wait_ge(s_end[o], 1)
                link(dve.tensor_copy(small[0:N_BUCKETS, 5, 0:1], bank(5, 1, N_BUCKETS, at=130)))
                for i in range(4):
                    ts = slice(i * TCH, (i + 1) * TCH)
                    dve.tensor_scalar(started[:, ts], tile_no[:, ts], small[0:N_BUCKETS, 5, 0:1], None,
                                      ALU.is_ge).then_inc(s_cmp[o], 1)
                    dve.wait_ge(s_bt[o], i + 1)
                    link(dve.tensor_scalar(bt[:, ts], bank(6, TCH), float(N_BUCKETS - 1), None, ALU.min))
                if o == 0:
                    dst_columns(link)
                else:
                    columns(AT_SRC, 0, link)

            def mark_bucket(o, b):
                dve.tensor_scalar(hit[:, b % 2, :], bucket[:, :], float(b), None, ALU.is_equal).then_inc(s_hit[o], 1)

            def count_piece(o, c, link):
                b, i = divmod(c, 4)
                dve.wait_ge(s_step[o], c + 1)
                if i >= 1:
                    dve.wait_ge(s_scan[o], c)
                t0 = i * ICH
                dve.tensor_tensor_scan(count[:, t0:t0 + ICH], bank(5 + i % 2, ICH), zeros_b[:, 0:ICH],
                                       count[:, t0 - 1:t0] if i else small[:, 2, b:b + 1],
                                       ALU.add, ALU.add).then_inc(s_scan[o], 1)
                if i == 3:
                    dve.wait_ge(s_scan[o], c + 1)
                    link(dve.copy_predicated(scratch, hit[:, b % 2, :].bitcast(U16), count))
                    if b + 2 < N_BUCKETS:
                        mark_bucket(o, b + 2)

            def place(o, rows, link):
                link(dve.tensor_copy(rows, scratch))
                yield
                link(dve.tensor_scalar(count_i, rows, P - 1, 3, ALU.bitwise_and, ALU.logical_shift_left))
                yield
                link(dve.tensor_scalar(scratch_i, rows, 7, GROUP - 1, ALU.logical_shift_right, ALU.bitwise_and))
                yield
                link(dve.tensor_tensor(count_i, count_i, scratch_i, ALU.bitwise_or))
                yield
                link(dve.tensor_scalar(scratch_i, rows, 10, 10, ALU.logical_shift_right, ALU.logical_shift_left))
                yield
                dve.tensor_tensor(rows, scratch_i, count_i, ALU.bitwise_or).then_inc(s_plan[o], 1)
                dve.wait_ge(s_plan[o], 1)

            def cutoff(link):
                link(dve.tensor_scalar(hit[:, 0, :], cw, CUTOFF, None, ALU.is_lt))
                yield
                link(dve.tensor_scalar(cw, cw, CUTOFF, None, ALU.min))
                yield
                link(dve.tensor_scalar(count, cw, 1.0 / (2 * CUTOFF), None, ALU.mult))
                yield
                link(dve.tensor_copy(scratch_i, count))
                yield
                link(dve.tensor_copy(count, scratch_i))
                yield
                link(dve.scalar_tensor_tensor(cw, count, -2 * CUTOFF, cw, ALU.mult, ALU.add))
                yield
                link(dve.tensor_scalar(count, cw, -1.0, None, ALU.mult))
                yield
                link(dve.tensor_tensor(cw, cw, count, ALU.max))
                yield
                link(dve.tensor_scalar(count, cw, -1.0, 2 * CUTOFF, ALU.mult, ALU.add))
                yield
                dve.tensor_tensor(cw, cw, count, ALU.min).then_inc(s_cosarg, 1)
                yield
                dve.wait_ge(s_cos, 1)
                link(dve.tensor_scalar(cw, cw, 0.5, 0.5, ALU.mult, ALU.add))
                yield
                link(dve.tensor_tensor(cw, cw, hit[:, 0, :], ALU.mult))
                yield

            dve.wait_ge(s_flag, 1)
            with dve.If(dve.value_load(flag[0:1, 0:1], min_val=0, max_val=1)):
                inner = [0]

                def inner_link(ins):
                    inner[0] += 1
                    ins.then_inc(s_branch, 1)
                    dve.wait_ge(s_branch, inner[0])

                for _ in split(dst_i[:, :], meta_b[:, real, M_LO], inner_link):
                    pass
                for _ in totals(0, inner_link):
                    pass
                tables(0, inner_link)
                mark_bucket(0, 0)
                mark_bucket(0, 1)
                for c in range(PIECES):
                    count_piece(0, c, inner_link)
                for _ in place(0, row_dst[:, :], inner_link):
                    pass

            ask = [0]

            def asked():
                ask[0] += 1
                dve.wait_ge(s_sr, ask[0])

            def bc(ap):
                return ap[:, :, None].to_broadcast([P, SLOTS, FEAT])

            def layernorm(out, last=None):
                v = V[:, :, :]
                mean = small[:, 3, :]
                link(dve.tensor_reduce(mean, v, AX_X, ALU.add))
                link(dve.tensor_scalar(mean, mean, 1.0 / FEAT, None, ALU.mult))
                link(dve.tensor_tensor(v, v, bc(mean), ALU.subtract))
                link(dve.tensor_tensor(Q[:, :, :], v, v, ALU.mult))
                link(dve.tensor_reduce(mean, Q[:, :, :], AX_X, ALU.add))
                dve.tensor_scalar(mean, mean, 1.0 / FEAT, LN_EPS, ALU.mult, ALU.add).then_inc(s_sq, 1)
                asked()
                link(dve.reciprocal(mean, mean))
                link(dve.tensor_tensor(out, v, bc(mean), ALU.mult))

            def acc_rows(width):
                return acc[:, :, :, 0:width]

            def banks(ap):
                return ap[:, :, :].rearrange("p (k s) w -> p k s w", k=ACC_BANKS)

            def weights(k):
                _, s_used, s_w, first = flow(k)
                for g in range(GROUPS):
                    gg = first + g
                    if gg >= 2:
                        dve.wait_ge(s_used, 2 * (gg - 1))
                    for j in range(GROUP):
                        last = dve.tensor_scalar(W_g[:, gg % 2, j, :], iota[:, 0:P],
                                                 meta_a[:, g * GROUP + j, R_LO - FEAT:R_LO - FEAT + 1], None,
                                                 ALU.is_equal)
                    last.then_inc(s_w, 2)

            dve.wait_ge(s_order, 1)
            dve.tensor_copy(red[:, 0, 0:1, 0], zeros_c[:, 0:1]).then_inc(s_epi, 1)
            early = [split(src_i, lo_src, link), cutoff(link), totals(1, link)]

            def steps(queue, n):
                while queue and n > 0:
                    try:
                        next(queue[0])
                        n -= 1
                    except StopIteration:
                        queue.pop(0)

            def mask(q):
                if q >= 2:
                    dve.wait_ge(s_mval, q - 1)
                for j in range(QUAD):
                    last = dve.tensor_scalar(hot[:, q % 2, j, :], iota_b[:, :],
                                             meta_b[:, q * QUAD + j, M_LO:M_LO + 1], NEG, ALU.not_equal, ALU.mult)
                last.then_inc(s_mask, 1)

            regs_of = {}

            def take_maxima(h, bank_no):
                q, u = h // 2, h % 2
                if u == 0:
                    regs_of[0] = offsets(DVE_ONLY, AT_BUCKET, q * QUAD, QUAD)
                dve.wait_ge(s_mT, h + 1)
                dve.tensor_reduce(red[:, h % 2, 0:2, :], bank(bank_no).rearrange("p (j h n) -> p j h n", j=2, h=SPAN),
                                  AX_X, ALU.max).then_inc(s_red, 1)
                dve.wait_ge(s_red, h + 1)
                for j in range(2):
                    at = seg_run[:, bass.ds(regs_of[0][2 * u + j], SPAN)]
                    link(dve.tensor_tensor(at, at, red[:, h % 2, j, :], ALU.max))

            link(dve.memset(seg_run[:, :], NEG))
            mask(0)
            for g in range(GROUPS):
                for i in range(2):
                    q = 2 * g + i
                    if q >= 2:
                        dve.wait_ge(s_used, q - 1)
                    for j in range(QUAD):
                        t = q * QUAD + j
                        last = dve.tensor_scalar(W[:, i, j, :], iota[:, :], meta_b[:, t, M_LO:M_LO + 1],
                                                 meta_b[:, t, M_NORM:M_NORM + 1], ALU.is_equal, ALU.mult)
                    last.then_inc(s_w, 1)
                    if i == 0:
                        mask(g + 1)
                    if q >= 1:
                        take_maxima(q - 1, 7)
                if g < PLAN_AT:
                    steps(early, 4 if g == 0 else 1)
                elif g == PLAN_AT:
                    steps(early, 1000)
                    tables(1, link)
                    mark_bucket(1, 0)
                    mark_bucket(1, 1)
                for c in counted_at(g):
                    count_piece(1, c, link)
            steps([place(1, row_src[:, :], link)], 1000)
            take_maxima(2 * GROUPS - 1, 7)
            dve.wait_ge(s_used, 2 * GROUPS)
            dve.wait_ge(s_node, 48)
            for k in range(ACC_BANKS):
                last = dve.tensor_tensor(banks(V)[:, k], acc[:, k, :, 0:FEAT],
                                         rb2[:, None, :].to_broadcast([P, PER_BANK, FEAT]), ALU.add)
            last.then_inc(s_epi, 1)
            dve.wait_ge(s_epi, 2)
            link(dve.scalar_tensor_tensor(V[:, :, :], V[:, :, :], 0.0, X[:, :, :], ALU.max, ALU.add))
            layernorm(X[:, :, :])
            dve.tensor_copy(red[:, 0, 0:1, 0], zeros_c[:, 0:1]).then_inc(s_tab, 1)

            dve.memset(ring[:, :, :, FEAT], 1.0)
            link(dve.memset(rec[:, :, :, REC - 1], 0.0))
            for q in range(QUADS + 2):
                if q % 2 == 0 and MAX_EARLY + q // 2 + 1 < QUADS:
                    mask(MAX_EARLY + q // 2 + 1)
                if q < QUADS_IN:
                    if q >= 2:
                        dve.wait_ge(s_deg, q - 1)
                    for j in range(QUAD):
                        t = q * QUAD + j
                        dve.tensor_scalar(hot_lo[:, q % 2, j, :], iota_b[:, 0:P], lo_src[:, t:t + 1], None, ALU.is_equal)
                    dve.tensor_tensor(hi_hot[:, q % 2, :, :],
                                      bucket[:, q * QUAD:(q + 1) * QUAD][:, :, None].to_broadcast([P, QUAD, SLOTS]),
                                      iota_b[:, None, 0:SLOTS].to_broadcast([P, QUAD, SLOTS]),
                                      ALU.is_equal).then_inc(s_degh, 1)
                r = q - 2
                if 0 <= r < QUADS_IN:
                    dve.wait_ge(s_gp, r + 1)
                    dve.wait_ge(s_small, r + 1)
                    dve.tensor_tensor(rec[:, r % RECS, :, 0:FEAT],
                                      bank(7 if r % 2 else 4, QUAD * FEAT).rearrange("p (j w) -> p j w", j=QUAD),
                                      b2r[:, None, :].to_broadcast([P, QUAD, FEAT]), ALU.add).then_inc(s_rec, 1)
                if 0 <= q - 1 < QUADS:
                    take_maxima(2 * MAX_EARLY + q - 1, (q - 1) % 2)
            link(dve.tensor_scalar(small[:, 6, :], seg_run[:, :], NEG / 2, None, ALU.is_gt))
            dve.tensor_tensor(seg_max[:, :], seg_run[:, :], small[:, 6, :], ALU.mult).then_inc(s_maxd, 1)
            for b in range(SLOTS):
                dve.wait_ge(s_bc, b + 1)
                dve.tensor_copy(big[:, b * P:(b + 1) * P], bank(5 + b % 2, P)).then_inc(s_bcc, 1)
            dve.wait_ge(s_deg, QUADS_IN)
            dve.tensor_scalar(small[:, 7, :], bank(2, SLOTS), 1.0, None, ALU.add).then_inc(s_sq, 1)
            asked()
            dve.reciprocal(dinv[:, :], small[:, 7, :]).then_inc(s_dinv, 1)
            for q in range(QUADS):
                qq = QUADS + q
                dve.wait_ge(s_used, qq - 1)
                for j in range(QUAD):
                    last = dve.tensor_scalar(hot[:, q % 2, j, :], iota_b[:, :],
                                             meta_b[:, q * QUAD + j, M_LO:M_LO + 1], None, ALU.is_equal)
                link(last)
                dve.wait_ge(s_ex, q + 1)
                dve.scalar_tensor_tensor(W[:, q % 2, :, :], ex[:, q % 2, :, :], 1.0, hot[:, q % 2, :, :],
                                         ALU.min, ALU.mult).then_inc(s_w, 1)
                if q == 2 * NEAR_AT + 1:
                    dve.wait_ge(s_m2, 16 * GROUP)
                    dst = meta_a[:, :, :].bitcast(I32)[:, :, R_DST - FEAT]
                    reach = meta_a[:, :, 0]
                    v, w = vf[:, 0:TILES], qf[:, 0:TILES]
                    link(dve.tensor_scalar(v.bitcast(I32), dst, P.bit_length() - 1, None, ALU.logical_shift_right))
                    dve.tensor_copy(w, v.bitcast(I32)).then_inc(s_near1, 1)
                    dve.wait_ge(s_near1, 1)
                    for i in range(4):
                        ts = slice(i * TCH, (i + 1) * TCH)
                        dve.wait_ge(s_near2, i + 1)
                        dve.tensor_scalar(v[:, ts], bank(5, TCH), float(SLOTS - NEAR), None, ALU.min).then_inc(s_near1, 1)
                    dve.wait_ge(s_near1, 5)
                    link(dve.scalar_tensor_tensor(reach, v, -float(P), dst, ALU.mult, ALU.add))
                    link(dve.scalar_tensor_tensor(w, meta_a[:, :, R_LO - FEAT], 0.0, reach, ALU.is_ge, ALU.mult))
                    link(dve.tensor_reduce(small[:, 6, 0:1], w, AX_X, ALU.max))
                    link(dve.tensor_reduce(small[:, 6, 1:2], w, AX_X, ALU.min))
                    link(dve.tensor_scalar(small[:, 6, 0:1], small[:, 6, 0:1], float(NEAR * P), None, ALU.is_ge))
                    link(dve.tensor_scalar(small[:, 6, 1:2], small[:, 6, 1:2], 0.0, None, ALU.is_lt))
                    dve.tensor_tensor(small[:, 6, 0:1], small[:, 6, 0:1], small[:, 6, 1:2], ALU.add).then_inc(s_nearf, 1)
                    dve.wait_ge(s_nearp, 1)
                    link(dve.tensor_scalar(far[:, 0:1], bank(5, 1), 0.5, None, ALU.is_gt))
                    dve.tensor_scalar(far[:, 1:2], bank(5, 1), 0.5, None, ALU.is_le).then_inc(s_flag2, 1)
                    link(dve.tensor_scalar(w.bitcast(I32), v, float(FEAT), None, ALU.mult))
            dve.wait_ge(s_used, 4 * GROUPS)
            r = slice(AT_NEAR, AT_NEAR + 1)
            link(dve.tensor_copy(at_table[r, :], qf[r, 0:TILES].bitcast(I32)))
            link(dve.tensor_scalar(small[:, 5, :].rearrange("p (k s) -> p k s", k=ACC_BANKS), acc[:, :, :, FEAT],
                                   1e-30, None, ALU.max))
            link(dve.reciprocal(small[:, 5, :], small[:, 5, :]))
            for k in range(ACC_BANKS):
                inv = small[:, 5, k * PER_BANK:(k + 1) * PER_BANK]
                last = dve.tensor_tensor(banks(V)[:, k], acc[:, k, :, 0:FEAT],
                                         inv[:, :, None].to_broadcast([P, PER_BANK, FEAT]), ALU.mult)
            last.then_inc(s_epi, 1)
            dve.wait_ge(s_epi, 3)
            dve.tensor_scalar(Q[:, :, :], V[:, :, :], 0.0, None, ALU.min).then_inc(s_sq, 1)
            asked()
            link(dve.tensor_scalar(V[:, :, :], V[:, :, :], 0.0, -1.0, ALU.max, ALU.add))
            link(dve.tensor_tensor(V[:, :, :], V[:, :, :], Q[:, :, :], ALU.add))
            link(dve.tensor_tensor(V[:, :, :], V[:, :, :], X[:, :, :], ALU.add))
            layernorm(X[:, :, :])
            def near_pass(k):
                first = (k - 2) * TILES
                AHEAD = 4

                def one_hots(t):
                    tt = first + t
                    if tt >= 8:
                        dve.wait_ge(s_fm, tt - 7)
                    dve.tensor_scalar(near_d[:, tt % 8, :], iota_s[:, :], meta_a[:, t, 0:1], None, ALU.is_equal)
                    dve.tensor_scalar(near_s[:, tt % 8, :], iota_b[:, 0:P], meta_a[:, t, R_LO - FEAT:R_LO - FEAT + 1], None,
                                      ALU.is_equal).then_inc(s_foh, 1)

                for t in range(AHEAD):
                    one_hots(t)
                for t in range(TILES):
                    if t + AHEAD < TILES:
                        one_hots(t + AHEAD)
                    tt = first + t
                    if by_dve(tt):
                        dve.wait_ge(s_fm, tt + 1)
                        if tt >= 4:
                            dve.wait_ge(s_fu, tt - 3)
                        dve.tensor_copy(near_m[:, tt % 4, :], bank(5 + tt % 3, NEAR * P)).then_inc(s_fd, 1)

            dve.tensor_tensor(V[:, :, :], X[:, :, :], bc(dinv[:, :]), ALU.mult).then_inc(s_tab, 1)
            dve.wait_ge(s_m2, 16 * GROUP)
            for k in (2, 3):
                with dve.If(dve.value_load(far[0:1, 0:1], min_val=0, max_val=1)):
                    weights(k)
                    dve.wait_ge(s_used_b, 2 * (k - 1) * GROUPS)
                with dve.If(dve.value_load(far[0:1, 1:2], min_val=0, max_val=1)):
                    near_pass(k)
                    dve.wait_ge(s_fu, (k - 1) * TILES)
                dve.wait_ge(s_tabw, 16 * k)
                dve.wait_ge(s_tab, k)
                for i in range(ACC_BANKS):
                    last = dve.tensor_tensor(banks(V)[:, i], acc[:, i, :, 0:FEAT], banks(V)[:, i], ALU.add)
                last.then_inc(s_epi, 1)
                dve.wait_ge(s_epi, k + 2)
                link(dve.tensor_tensor(V[:, :, :], V[:, :, :], bc(dinv[:, :]), ALU.mult))
                if k == 2:
                    dve.tensor_tensor(V[:, :, :], V[:, :, :], bc(dinv[:, :]), ALU.mult).then_inc(s_tab, 1)
            link(dve.tensor_tensor(V[:, :, :], V[:, :, :], X[:, :, :], ALU.add))
            layernorm(X[:, :, :])
            dve.wait_ge(s_embg, 16 * SLOTS)
            for k in range(ACC_BANKS):
                last = dve.tensor_copy(emb_of_v[:, k, :, 0:EMB], embs[:, k * PER_BANK:(k + 1) * PER_BANK, 0:EMB])
            link(last)
            dve.tensor_copy(embs[:, :, EMB - 1], node_mj[:, :]).then_inc(s_tab, 1)
            def one_hots(g):
                gg = 2 * GROUPS + g
                dve.wait_ge(s_recl[g % 3], 16 * (g // 3 + 1))
                dve.wait_ge(s_used, 2 * (gg - 3))
                for j in range(GROUP):
                    last = dve.tensor_scalar(W3[:, gg % 4, j, :], iota[:, 0:P], rec_in[:, g % 3, j, R_LO:R_LO + 1], None,
                                             ALU.is_equal)
                last.then_inc(s_oh, 1)

            one_hots(0)
            one_hots(1)
            for g in range(GROUPS):
                gg = 2 * GROUPS + g
                if g + 2 < GROUPS:
                    one_hots(g + 2)
                else:
                    dve.wait_ge(s_used, 2 * (gg - 1))
                dve.wait_ge(s_gat[gg % RING], 16 * GROUP * (gg // RING + 1))
                rows = ring[:, gg % RING, :, :]
                rin = rec_in[:, g % 3, :, :]
                wgt = wgt_2[:, g % 2, :]
                dve.wait_ge(s_ei, g + 1)
                dve.tensor_tensor(wgt, rin[:, :, R_CW], rows[:, :, X3_MJ], ALU.mult)
                dve.tensor_copy(msg[:, gg % 2, :, FEAT], rows[:, :, X3_MJ])
                dve.tensor_tensor(prod, bank(7, GROUP * EMB).rearrange("p (j w) -> p j w", j=GROUP),
                                  rows[:, :, X3_EMB:X3_W], ALU.mult).then_inc(s_prod, 1)
                dve.wait_ge(s_prod, g + 1)
                link(dve.tensor_reduce(adapt, prod, AX_X, ALU.add))
                m = msg[:, gg % 2, :, 0:FEAT]
                full = [P, GROUP, FEAT]
                dve.tensor_tensor(m, rin[:, :, 0:FEAT], adapt[:, :, None].to_broadcast(full), ALU.add) \
                    .then_inc(s_eir, 1)
                dve.wait_ge(s_eir, g + 1)
                link(dve.tensor_tensor(m, m, rows[:, :, 0:FEAT], ALU.mult))
                dve.tensor_tensor(m, m, wgt[:, :, None].to_broadcast(full), ALU.mult).then_inc(s_w, 2)
            dve.wait_ge(s_used, 6 * GROUPS)
            link(dve.tensor_scalar(small[:, 5, :].rearrange("p (k s) -> p k s", k=ACC_BANKS), acc[:, :, :, FEAT],
                                   1e-8, None, ALU.max))
            link(dve.reciprocal(small[:, 5, :], small[:, 5, :]))
            for k in range(ACC_BANKS):
                inv = small[:, 5, k * PER_BANK:(k + 1) * PER_BANK]
                last = dve.tensor_tensor(banks(V)[:, k], acc[:, k, :, 0:FEAT],
                                         inv[:, :, None].to_broadcast([P, PER_BANK, FEAT]), ALU.mult)
            link(last)
            link(dve.tensor_tensor(V[:, :, :], V[:, :, :], X[:, :, :], ALU.add))
            layernorm(V[:, :, :])
            row = [P, SLOTS, FEAT]
            link(dve.tensor_tensor(V[:, :, :], V[:, :, :], gamma[:, None, :].to_broadcast(row), ALU.mult))
            link(dve.tensor_tensor(V[:, :, :], V[:, :, :], beta[:, None, :].to_broadcast(row), ALU.add))
            link(dve.tensor_tensor(V[:, :, :], V[:, :, :], X[:, :, :], ALU.add))
            layernorm(X[:, :, :])
            dve.tensor_copy(red[:, 0, 0:1, 0], zeros_c[:, 0:1]).then_inc(s_tab, 1)


def kernel(**inputs):
    import concourse.bacc as bacc
    from concourse.bass_utils import run_bass_kernel_spmd

    a = {k: np.asarray(v) for k, v in inputs.items()}

    def edges(v, fill):
        v = np.concatenate([v.reshape(-1), np.full(TILES_IN * P - N_EDGES, fill, v.dtype)])
        return np.ascontiguousarray(v.reshape(TILES_IN, P).T)

    def nodes(v):
        v = v.reshape(N_NODES, -1)
        v = np.concatenate([v, np.zeros((NODES - N_NODES, v.shape[1]), v.dtype)])
        return v

    def by_place(v):
        v = nodes(v)
        return np.ascontiguousarray(v.reshape(SLOTS, P, v.shape[1]).transpose(1, 0, 2))

    f = np.float32
    default = np.zeros((P, GROUP * REC), f)
    default_rec = default.copy().reshape(P, GROUP, REC)
    default_rec[:, :, R_LO] = -1.0
    i = np.arange(P)
    attrT = np.zeros((ATTR, TILES_IN * P), f)
    attrT[:, :N_EDGES] = a["edge_attr_40"].T
    embT = np.zeros((EMB, P), f)
    embT[:, :a["L3_gnn_emb"].shape[0]] = a["L3_gnn_emb"].T
    arrays = {
        "src": edges(a["src"], PAD_NODE), "dst": edges(a["dst"], PAD_NODE),
        "etype": edges(a["edge_type_8"], 0), "norm": edges(a["edge_weight1"], 0), "dist": edges(a["edge_weight"], 0),
        "attrT": attrT,
        "x": by_place(a["x"]), "xT": np.ascontiguousarray(nodes(a["x"]).T),
        "node_z": by_place(a["node_type_119"])[:, :, 0], "node_mj": by_place(a["node_vec"])[:, :, 0],
        "weight1": a["L0_gnn_weight1"], "weight2": a["L0_gnn_weight2"],
        "bias1": a["L0_gnn_bias1"], "bias2": a["L0_gnn_bias2"],
        "W1T": np.ascontiguousarray(a["L3_gnn_W1"].T), "W2T": np.ascontiguousarray(a["L3_gnn_W2"].T),
        "b1": a["L3_gnn_b1"], "b2": a["L3_gnn_b2"], "embT": embT,
        "adaptT": np.ascontiguousarray(a["L3_gnn_adaptW"].T),
        "gamma": a["L3_gnn_gamma"], "beta": a["L3_gnn_beta"],
        "const": np.stack([np.eye(P, dtype=f), (i[:, None] < i[None, :]).astype(f),
                           (i[:, None] <= i[None, :]).astype(f)]
                          + [np.tile((h * P + i).astype(f), (P, 1)) for h in range(SPAN)]
                          + [np.tile((i == 0).astype(f)[:, None], (1, P))]),
        "tile_no": np.tile(np.arange(TILES, dtype=f), (N_BUCKETS, 1)),
        "default": default_rec.reshape(P, GROUP * REC),
        "default_meta": np.tile(np.array([-1, 0, 0, 0], f), (P, GROUP)),
    }
    arrays = {k: np.ascontiguousarray(v) for k, v in arrays.items()}
    nc = bacc.Bacc("TRN2", target_bir_lowering=False, num_devices=1)
    A = {k: nc.dram_tensor(f"in_{k}", v.shape, mybir.dt.from_np(v.dtype), kind="ExternalInput").ap()
         for k, v in arrays.items()}
    A["out"] = nc.dram_tensor("out_x", (N_NODES, FEAT), F32, kind="ExternalOutput").ap()
    build(nc, A)
    r = run_bass_kernel_spmd(nc, [{f"in_{k}": v for k, v in arrays.items()}], core_ids=[0])
    return r.results[0]["out_x"]
```
